# Optimizing a Trainium2 kernel written in Bass

```python
import numpy as np
import jax
import jax.numpy as jnp

def _softmax(x, axis=-1):
    return jax.nn.softmax(x, axis=axis)

def _gelu(x):
    return jax.nn.gelu(x, approximate=True)

def _silu(x):
    return jax.nn.silu(x)

def _sigmoid(x):
    return jax.nn.sigmoid(x)

def _layernorm(x, axis=-1, eps=1e-05):
    m = jnp.mean(x, axis=axis, keepdims=True)
    v = jnp.var(x, axis=axis, keepdims=True)
    return (x - m) / jnp.sqrt(v + eps)

def _scatter_add(tgt, idx, src, axis=0):
    return tgt.at[idx].add(src)

def _segment_sum(src, seg, n):
    return jax.ops.segment_sum(src, seg, n)
kernel_name = 'mk_gnn_ffn_d2_gnn_r16_08acc8'

def setup_inputs(seed: int=0):
    np.random.seed(seed)
    _w = jnp.asarray

    def _rec_inputs():
        import jax
        import jax.numpy as jnp
        _gk = jax.random.key(seed)
        x = -0.0003713 + 1 * jax.random.normal(jax.random.fold_in(_gk, 1), (6250, 256), jnp.float32)
        src = jax.random.randint(jax.random.fold_in(_gk, 2), (100000,), 0, 6250, jnp.int32)
        dst = jnp.minimum((6250 * jax.random.uniform(jax.random.fold_in(_gk, 3), (100000,)) ** 2.0).astype(jnp.int32), 99999)
        _o = jnp.argsort(dst, stable=True)
        src = src[_o]
        dst = dst[_o]
        edge_weight = jax.random.uniform(jax.random.fold_in(_gk, 14), (100000,), jnp.float32, 0.0, 1)
        edge_weight1 = 0.000937891 + 0.999965 * jax.random.normal(jax.random.fold_in(_gk, 15), (100000, 1), jnp.float32)
        return (x, src, dst, edge_weight, edge_weight1)
    x, src, dst, edge_weight, edge_weight1 = _rec_inputs()

    def _L0_gnn_setup():
        import jax, jax.numpy as jnp
        import numpy as np
        N, E, IN_DIM, HEADS, OUT_DIM, N_GRAPHS = (3125, 50000, 256, 4, 64, 8)
        HC = HEADS * OUT_DIM
        NEG_SLOPE = 0.2
        LN_EPS = 1e-05
        key = jax.random.key(seed)
        ks = jax.random.split(key, 12)
        x = jax.random.normal(ks[0], (N, IN_DIM), jnp.float32)
        edge_attr = jax.random.normal(ks[1], (E, 1), jnp.float32)
        src = jax.random.randint(ks[2], (E,), 0, N, dtype=jnp.int32)
        dst = jax.random.randint(ks[3], (E,), 0, N, dtype=jnp.int32)
        edge_index = jnp.stack([src, dst]).astype(jnp.int64)
        batch = jnp.sort(jax.random.randint(ks[4], (N,), 0, N_GRAPHS, dtype=jnp.int32)).astype(jnp.int64)
        s = 1.0 / np.sqrt(IN_DIM)
        W_src = jax.random.uniform(ks[5], (IN_DIM, HC), jnp.float32, -s, s)
        W_dst = jax.random.uniform(ks[6], (IN_DIM, HC), jnp.float32, -s, s)
        att_src = jax.random.uniform(ks[7], (HEADS, OUT_DIM), jnp.float32, -s, s)
        att_dst = jax.random.uniform(ks[8], (HEADS, OUT_DIM), jnp.float32, -s, s)
        bias = jnp.zeros((HC,), jnp.float32)
        ln_gamma = jnp.ones((HC,), jnp.float32)
        ln_beta = jnp.zeros((HC,), jnp.float32)
        prelu_w = jnp.full((HC,), 0.25, jnp.float32)
        return {'x': x, 'edge_attr': edge_attr, 'W_src': W_src, 'W_dst': W_dst, 'att_src': att_src, 'att_dst': att_dst, 'bias': bias, 'ln_gamma': ln_gamma, 'ln_beta': ln_beta, 'prelu_w': prelu_w, 'edge_index': edge_index, 'batch': batch}
    _L0_gnn_all = _L0_gnn_setup()
    _L0_gnn_in = {k: v for k, v in _L0_gnn_all.items() if k in ('W_src', 'W_dst', 'att_src', 'att_dst', 'bias', 'ln_gamma', 'ln_beta', 'prelu_w')}
    del _L0_gnn_all

    def _L0_ffn_setup():
        import jax, jax.numpy as jnp
        import numpy as np
        TOP_K = 2
        LN_EPS = 1e-05
        key = jax.random.key(seed)
        ks = jax.random.split(key, 8)
        B, S, D, E, H = (16, 1024, 256, 8, 1024)
        x = jax.random.normal(ks[0], (B, S, D), dtype=jnp.float32)
        Wr = jax.random.normal(ks[1], (D, E), dtype=jnp.float32) * 0.1
        br = jnp.zeros((E,), dtype=jnp.float32)
        ln_g = jnp.ones((E, D), dtype=jnp.float32)
        ln_b = jnp.zeros((E, D), dtype=jnp.float32)
        W1 = jax.random.normal(ks[2], (E, D, H), dtype=jnp.float32) * (1.0 / np.sqrt(D))
        b1 = jnp.zeros((E, H), dtype=jnp.float32)
        W2 = jax.random.normal(ks[3], (E, H, D), dtype=jnp.float32) * (1.0 / np.sqrt(H))
        b2 = jnp.zeros((E, D), dtype=jnp.float32)
        return {'x': x, 'Wr': Wr, 'br': br, 'ln_g': ln_g, 'ln_b': ln_b, 'W1': W1, 'b1': b1, 'W2': W2, 'b2': b2}
    _L0_ffn_all = _L0_ffn_setup()
    _L0_ffn_in = {k: v for k, v in _L0_ffn_all.items() if k in ('Wr', 'br', 'ln_g', 'ln_b', 'W1', 'b1', 'W2', 'b2')}
    del _L0_ffn_all

    def _L1_gnn_setup():
        import jax, jax.numpy as jnp
        import numpy as np
        N_NODES = 6250
        NNZ = 200000
        DIM = 256
        HOPS = 3
        key = jax.random.key(seed)
        ks = jax.random.split(key, 8)
        m = jax.random.normal(ks[0], (N_NODES, DIM), dtype=jnp.float32)
        vals = jax.random.uniform(ks[1], (NNZ,), dtype=jnp.float32)
        scale = 1.0 / np.sqrt(DIM)
        Wn = jax.random.normal(ks[2], (HOPS, DIM, DIM), dtype=jnp.float32) * scale
        bn = jax.random.normal(ks[3], (HOPS, DIM), dtype=jnp.float32) * 0.01
        Ws = jax.random.normal(ks[4], (HOPS, DIM, DIM), dtype=jnp.float32) * scale
        bs = jax.random.normal(ks[5], (HOPS, DIM), dtype=jnp.float32) * 0.01
        rows = jax.random.randint(ks[6], (NNZ,), 0, N_NODES, dtype=jnp.int64)
        cols = jax.random.randint(ks[7], (NNZ,), 0, N_NODES, dtype=jnp.int64)
        return {'m': m, 'vals': vals, 'Wn': Wn, 'bn': bn, 'Ws': Ws, 'bs': bs, 'rows': rows, 'cols': cols}
    _L1_gnn_all = _L1_gnn_setup()
    _L1_gnn_in = {k: v for k, v in _L1_gnn_all.items() if k in ('Wn', 'bn', 'Ws', 'bs')}
    del _L1_gnn_all

    def _L1_ffn_setup():
        import jax, jax.numpy as jnp
        import numpy as np
        from jax import lax
        key = jax.random.key(seed)
        B, T, I, H = (64, 128, 256, 256)
        ks = jax.random.split(key, 13)
        s = 1.0 / np.sqrt(H)

        def w(k, shape):
            return jax.random.uniform(k, shape, jnp.float32, -s, s)
        return {'x': jax.random.normal(ks[0], (B, T, I), jnp.float32), 'U_i': w(ks[1], (I, H)), 'V_i': w(ks[2], (H, H)), 'b_i': w(ks[3], (H,)), 'U_f': w(ks[4], (I, H)), 'V_f': w(ks[5], (H, H)), 'b_f': w(ks[6], (H,)), 'U_c': w(ks[7], (I, H)), 'V_c': w(ks[8], (H, H)), 'b_c': w(ks[9], (H,)), 'U_o': w(ks[10], (I, H)), 'V_o': w(ks[11], (H, H)), 'b_o': w(ks[12], (H,))}
    _L1_ffn_all = _L1_ffn_setup()
    _L1_ffn_in = {k: v for k, v in _L1_ffn_all.items() if k in ('U_i', 'V_i', 'b_i', 'U_f', 'V_f', 'b_f', 'U_c', 'V_c', 'b_c', 'U_o', 'V_o', 'b_o')}
    del _L1_ffn_all
    return {'x': x, 'src': src, 'dst': dst, 'edge_weight': edge_weight, 'edge_weight1': edge_weight1, 'L0_gnn_W_src': _L0_gnn_in['W_src'], 'L0_gnn_W_dst': _L0_gnn_in['W_dst'], 'L0_gnn_att_src': _L0_gnn_in['att_src'], 'L0_gnn_att_dst': _L0_gnn_in['att_dst'], 'L0_gnn_bias': _L0_gnn_in['bias'], 'L0_gnn_ln_gamma': _L0_gnn_in['ln_gamma'], 'L0_gnn_ln_beta': _L0_gnn_in['ln_beta'], 'L0_gnn_prelu_w': _L0_gnn_in['prelu_w'], 'L0_ffn_Wr': _L0_ffn_in['Wr'], 'L0_ffn_br': _L0_ffn_in['br'], 'L0_ffn_ln_g': _L0_ffn_in['ln_g'], 'L0_ffn_ln_b': _L0_ffn_in['ln_b'], 'L0_ffn_W1': _L0_ffn_in['W1'], 'L0_ffn_b1': _L0_ffn_in['b1'], 'L0_ffn_W2': _L0_ffn_in['W2'], 'L0_ffn_b2': _L0_ffn_in['b2'], 'L1_gnn_Wn': _L1_gnn_in['Wn'], 'L1_gnn_bn': _L1_gnn_in['bn'], 'L1_gnn_Ws': _L1_gnn_in['Ws'], 'L1_gnn_bs': _L1_gnn_in['bs'], 'L1_ffn_U_i': _L1_ffn_in['U_i'], 'L1_ffn_V_i': _L1_ffn_in['V_i'], 'L1_ffn_b_i': _L1_ffn_in['b_i'], 'L1_ffn_U_f': _L1_ffn_in['U_f'], 'L1_ffn_V_f': _L1_ffn_in['V_f'], 'L1_ffn_b_f': _L1_ffn_in['b_f'], 'L1_ffn_U_c': _L1_ffn_in['U_c'], 'L1_ffn_V_c': _L1_ffn_in['V_c'], 'L1_ffn_b_c': _L1_ffn_in['b_c'], 'L1_ffn_U_o': _L1_ffn_in['U_o'], 'L1_ffn_V_o': _L1_ffn_in['V_o'], 'L1_ffn_b_o': _L1_ffn_in['b_o']}

def reference(x, src, dst, edge_weight, edge_weight1, L0_gnn_W_src, L0_gnn_W_dst, L0_gnn_att_src, L0_gnn_att_dst, L0_gnn_bias, L0_gnn_ln_gamma, L0_gnn_ln_beta, L0_gnn_prelu_w, L0_ffn_Wr, L0_ffn_br, L0_ffn_ln_g, L0_ffn_ln_b, L0_ffn_W1, L0_ffn_b1, L0_ffn_W2, L0_ffn_b2, L1_gnn_Wn, L1_gnn_bn, L1_gnn_Ws, L1_gnn_bs, L1_ffn_U_i, L1_ffn_V_i, L1_ffn_b_i, L1_ffn_U_f, L1_ffn_V_f, L1_ffn_b_f, L1_ffn_U_c, L1_ffn_V_c, L1_ffn_b_c, L1_ffn_U_o, L1_ffn_V_o, L1_ffn_b_o):
    import jax
    import jax.numpy as jnp

    def _L0_gnn_ref(x, edge_attr, W_src, W_dst, att_src, att_dst, bias, ln_gamma, ln_beta, prelu_w, edge_index, batch):
        import jax, jax.numpy as jnp
        import numpy as np
        N, E, IN_DIM, HEADS, OUT_DIM, N_GRAPHS = (3125, 50000, 256, 4, 64, 8)
        HC = HEADS * OUT_DIM
        NEG_SLOPE = 0.2
        LN_EPS = 1e-05
        src, dst = (edge_index[0], edge_index[1])
        n = x.shape[0]
        h_src = (x @ W_src).reshape(n, HEADS, OUT_DIM)
        h_dst = (x @ W_dst).reshape(n, HEADS, OUT_DIM)
        a_src = jnp.einsum('nhc,hc->nh', h_src, att_src)
        a_dst = jnp.einsum('nhc,hc->nh', h_dst, att_dst)
        e = a_src[src] + a_dst[dst]
        e = jnp.where(e > 0, e, NEG_SLOPE * e)
        m = jax.ops.segment_max(e, dst, num_segments=n)
        p = jnp.exp(e - m[dst])
        denom = jax.ops.segment_sum(p, dst, num_segments=n)
        alpha = p / jnp.maximum(denom[dst], 1e-16)
        msg = alpha[:, :, None] * h_src[src]
        out = jax.ops.segment_sum(msg, dst, num_segments=n).reshape(n, HC) + bias
        mu = out.mean(-1, keepdims=True)
        var = ((out - mu) ** 2).mean(-1, keepdims=True)
        out = (out - mu) * jax.lax.rsqrt(var + LN_EPS) * ln_gamma + ln_beta
        return jnp.where(out > 0, out, prelu_w * out)

    def _L0_ffn_ref(x, Wr, br, ln_g, ln_b, W1, b1, W2, b2):
        import jax, jax.numpy as jnp
        import numpy as np
        TOP_K = 2
        LN_EPS = 1e-05
        B, S, D = x.shape
        N = B * S
        xt = x.reshape(N, D)
        logits = xt @ Wr + br
        probs = jax.nn.softmax(logits, axis=-1)
        top_p, top_idx = jax.lax.top_k(probs, TOP_K)
        weights = top_p / top_p.sum(axis=-1, keepdims=True)
        mu = xt.mean(axis=-1, keepdims=True)
        var = ((xt - mu) ** 2).mean(axis=-1, keepdims=True)
        xn = (xt - mu) * jax.lax.rsqrt(var + LN_EPS)
        xe = xn[None, :, :] * ln_g[:, None, :] + ln_b[:, None, :]
        h = jax.nn.gelu(jnp.einsum('end,edh->enh', xe, W1) + b1[:, None, :], approximate=False)
        y = jnp.einsum('enh,ehd->end', h, W2) + b2[:, None, :]
        y_tok = jnp.transpose(y, (1, 0, 2))
        sel = jnp.take_along_axis(y_tok, top_idx[:, :, None], axis=1)
        out = (weights[:, :, None] * sel).sum(axis=1)
        return out.reshape(B, S, D)

    def _L1_gnn_ref(m, vals, Wn, bn, Ws, bs, rows, cols):
        import jax, jax.numpy as jnp
        import numpy as np
        N_NODES = 6250
        NNZ = 200000
        DIM = 256
        HOPS = 3
        N = m.shape[0]
        hop_num = Wn.shape[0]
        H = m
        for i in range(hop_num):
            msg = H[cols] * vals[:, None]
            Hn = jax.ops.segment_sum(msg, rows, num_segments=N)
            Hn = Hn @ Wn[i].T + bn[i]
            Hs = H @ Ws[i].T + bs[i]
            H = Hn + Hs
            if i != hop_num - 1:
                H = jax.nn.elu(H)
        return H

    def _L1_ffn_ref(x, U_i, V_i, b_i, U_f, V_f, b_f, U_c, V_c, b_c, U_o, V_o, b_o):
        import jax, jax.numpy as jnp
        import numpy as np
        from jax import lax
        B, T, _ = x.shape
        H = U_i.shape[1]
        xt = jnp.swapaxes(x, 0, 1)
        xi = xt @ U_i + b_i
        xf = xt @ U_f + b_f
        xg = xt @ U_c + b_c
        xo = xt @ U_o + b_o
        h0 = jnp.zeros((B, H), x.dtype)
        c0 = jnp.zeros((B, H), x.dtype)

        def step(carry, xs):
            h, c = carry
            xi_t, xf_t, xg_t, xo_t = xs
            i_t = jax.nn.sigmoid(xi_t + h @ V_i)
            f_t = jax.nn.sigmoid(xf_t + h @ V_f)
            g_t = jnp.tanh(xg_t + h @ V_c)
            o_t = jax.nn.sigmoid(xo_t + h @ V_o)
            c_new = h * c + i_t * g_t
            h_new = o_t * jnp.tanh(c_new)
            return ((h_new, c_new), h_new)
        (_, _), hs = lax.scan(step, (h0, c0), (xi, xf, xg, xo))
        return jnp.swapaxes(hs, 0, 1)
    edge_index = jnp.stack([src, dst])
    batch0 = jnp.zeros((6250,), jnp.int32)
    x = x + _L0_gnn_ref(_layernorm(x, axis=-1), edge_weight1, L0_gnn_W_src, L0_gnn_W_dst, L0_gnn_att_src, L0_gnn_att_dst, L0_gnn_bias, L0_gnn_ln_gamma, L0_gnn_ln_beta, L0_gnn_prelu_w, edge_index, batch0)
    x = x + _L0_ffn_ref(_layernorm(x, axis=-1)[None], L0_ffn_Wr, L0_ffn_br, L0_ffn_ln_g, L0_ffn_ln_b, L0_ffn_W1, L0_ffn_b1, L0_ffn_W2, L0_ffn_b2)[0]
    x = x + _L1_gnn_ref(_layernorm(x, axis=-1), edge_weight, L1_gnn_Wn, L1_gnn_bn, L1_gnn_Ws, L1_gnn_bs, src, dst)
    x = x + _L1_ffn_ref(_layernorm(x, axis=-1)[None], L1_ffn_U_i, L1_ffn_V_i, L1_ffn_b_i, L1_ffn_U_f, L1_ffn_V_f, L1_ffn_b_f, L1_ffn_U_c, L1_ffn_V_c, L1_ffn_b_c, L1_ffn_U_o, L1_ffn_V_o, L1_ffn_b_o)[0]
    return x

_drawn_inputs = setup_inputs


def setup_inputs(seed=0):
    import zlib

    import numpy as np

    out = dict(_drawn_inputs(seed))
    spreads = {'L0_gnn_bias': (0.0, 0.1),
     'L0_gnn_ln_gamma': (1.0, 0.2),
     'L0_gnn_ln_beta': (0.0, 0.1),
     'L0_gnn_prelu_w': (0.25, 0.2),
     'L0_ffn_br': (0.0, 0.1),
     'L0_ffn_ln_g': (1.0, 0.2),
     'L0_ffn_ln_b': (0.0, 0.1),
     'L0_ffn_b1': (0.0, 0.1),
     'L0_ffn_b2': (0.0, 0.1)}
    factors = {'L0_gnn_W_dst': 8.0,
     'L0_gnn_att_dst': 8.0,
     'L1_gnn_bn': 8.0,
     'L1_gnn_bs': 8.0,
     'L1_ffn_U_i': 8.0,
     'L1_ffn_V_i': 8.0,
     'L1_ffn_b_i': 8.0,
     'L1_ffn_U_c': 8.0,
     'L1_ffn_V_c': 8.0,
     'L1_ffn_b_c': 8.0,
     'L1_ffn_U_o': 8.0,
     'L1_ffn_V_o': 8.0,
     'L1_ffn_b_o': 8.0}
    for name, (base, spread) in spreads.items():
        noise = np.random.default_rng([zlib.crc32(name.encode()), seed]).standard_normal(out[name].shape)
        drawn = base * np.exp(spread * noise) if base else spread * noise
        out[name] = jnp.asarray(drawn.astype(out[name].dtype))
    for name, factor in factors.items():
        out[name] = (out[name] * factor).astype(out[name].dtype)
    return out
```

```python
import concourse.bass as bass
from concourse import mybir
from contextlib import ExitStack

F32 = mybir.dt.float32
F16 = mybir.dt.float16
BF16 = mybir.dt.bfloat16
I32 = mybir.dt.int32
ACT = mybir.ActivationFunctionType
ALU = mybir.AluOpType
AXX = mybir.AxisListType.X

P = 128
LOGP = 7
N = 6250
D = 256
E = 100000
KD = D // P
NB = 50
NP = NB * P
FULL = N // P
TAIL = N - FULL * P
LN_EPS = 1e-5

EC = 784
ELAST = E - (P - 1) * EC
U = 7
ET = 840
EROW = ET + U
HEADS = 4
HD = D // HEADS
NEG_SLOPE = 0.2


class Chain:

    def __init__(self, eng, sem):
        self.eng, self.sem, self.base, self.n = eng, sem, 0, 0

    def at(self, base):
        self.base, self.n = base, 0

    def mark(self, ins):
        ins.then_inc(self.sem, 1)
        self.n += 1

    def wait(self):
        self.eng.wait_ge(self.sem, self.base + self.n)

    def __call__(self, ins):
        self.mark(ins)
        self.wait()


class Phase:

    def __init__(self, nc, name):
        self.nc, self.name, self.ctx, self.sems = nc, name, ExitStack(), []

    def __enter__(self):
        self.ctx.__enter__()
        return self

    def __exit__(self, *a):
        if self.sems and a[0] is None:
            with self.nc.Block() as block:
                @block.sync
                def _(sp):
                    for s in self.sems:
                        sp.sem_clear(s)
        return self.ctx.__exit__(*a)

    def sb(self, name, shape, dt=F32):
        return self.ctx.enter_context(self.nc.sbuf_tensor(f"{self.name}_{name}", shape, dt))

    def ps(self, name, shape=(P, 512), dt=F32):
        return self.ctx.enter_context(self.nc.psum_tensor(f"{self.name}_{name}", list(shape), dt))

    def sem(self, name):
        self.sems.append(self.ctx.enter_context(self.nc.semaphore(f"{self.name}_{name}")))
        return self.sems[-1]

    def indirect(self, k, count):
        before = k.indirect_before
        k.indirect_before += 16 * count
        return k.indirect, before

    def block(self):
        return self.nc.Block()


def constants(nc, k):
    with Phase(nc, "const") as ph:
        made = ph.sem("made")
        with ph.block() as block:
            @block.gpsimd
            def _(pool):
                c = Chain(pool, made)
                c(nc.gpsimd.iota(k.cols[:], [[1, P]], base=0, channel_multiplier=0, allow_small_or_imprecise_dtypes=True))
                c(nc.gpsimd.iota(k.part[:], [[0, 1]], base=0, channel_multiplier=1, allow_small_or_imprecise_dtypes=True))
                c(nc.gpsimd.memset(k.ident[:], 0.0))
                c(nc.gpsimd.affine_select(out=k.ident[:], in_=k.ident[:], compare_op=ALU.not_equal, fill=1.0,
                                          base=0, pattern=[[-1, P]], channel_multiplier=1))
                c(nc.gpsimd.memset(k.ones[:], 1.0))
                c(nc.gpsimd.memset(k.onesf[:], 1.0))
                c(nc.gpsimd.memset(k.before[:], 1.0))
                c(nc.gpsimd.affine_select(out=k.before[:], in_=k.before[:], compare_op=ALU.is_gt, fill=0.0,
                                          base=0, pattern=[[1, P]], channel_multiplier=-1))


def load_rows(nc, x, X):
    with Phase(nc, "load") as ph:
        zeroed, loaded = ph.sem("zeroed"), ph.sem("loaded")
        with ph.block() as block:
            @block.vector
            def _(dve):
                nc.vector.memset(X[:, FULL:NB, :], 0.0).then_inc(zeroed, 1)

            @block.sync
            def _(sp):
                sp.dma_start(X[:, 0:FULL, :], x[0:FULL * P, :].rearrange("(b p) d -> p b d", p=P)).then_inc(loaded, 16)
                sp.wait_ge(zeroed, 1)
                sp.dma_start(X[0:TAIL, FULL, :], x[FULL * P:N, :]).then_inc(loaded, 16)
                sp.wait_ge(loaded, 32)


def store_rows(nc, X, out):
    with Phase(nc, "store") as ph:
        stored = ph.sem("stored")
        with ph.block() as block:
            @block.sync
            def _(sp):
                sp.dma_start(out[0:FULL * P, :].rearrange("(b p) d -> p b d", p=P), X[:, 0:FULL, :]).then_inc(stored, 16)
                sp.dma_start(out[FULL * P:N, :], X[0:TAIL, FULL, :]).then_inc(stored, 16)
                sp.wait_ge(stored, 32)


class RowNorm:

    def __init__(self, nc, ph, src, tag=""):
        self.nc, self.src = nc, src
        self.parts = ph.sb(f"parts{tag}", [P, NB, nc.vector.BN_STATS_DIM])
        self.mv = ph.sb(f"mv{tag}", [P, NB, nc.vector.BN_AGGR_DIM])
        self.rstd = ph.sb(f"rstd{tag}", [P, NB])
        self.std = ph.sb(f"std{tag}", [P, NB])
        self.var_made, self.std_made = ph.sem(f"var_made{tag}"), ph.sem(f"std_made{tag}")

    def root(self, act):
        act.wait_ge(self.var_made, 1)
        self.nc.scalar.activation(self.std[:], self.rstd[:], ACT.Sqrt).then_inc(self.std_made, 1)

    def stats(self, dve, chain):
        nc = self.nc
        with dve.Fori(0, NB) as b:
            nc.vector.bn_stats(self.parts[:, bass.ds(b, 1), :], self.src[:, bass.ds(b, 1), :]).then_inc(chain.sem, 1)
        chain.n += NB
        chain.wait()
        for b in range(NB):
            chain.mark(nc.vector.bn_aggr(self.mv[:, b, :], self.parts[:, b, :]))
        chain.wait()
        nc.vector.tensor_scalar_add(self.rstd[:], self.mv[:, :, 1], LN_EPS).then_inc(self.var_made, 1)
        dve.wait_ge(self.std_made, 1)
        chain(nc.vector.reciprocal(self.rstd[:], self.std[:]))

    def apply(self, dst, b):
        return self.nc.vector.tensor_scalar(dst, self.src[:, bass.ds(b, 1), :], self.mv[:, bass.ds(b, 1), 0],
                                            self.rstd[:, bass.ds(b, 1)], ALU.subtract, ALU.mult)

    def all(self, dve, chain, dst):
        self.stats(dve, chain)
        with dve.Fori(0, NB) as b:
            self.apply(dst[:, bass.ds(b, 1), :], b).then_inc(chain.sem, 1)
        chain.n += NB
        chain.wait()


def sort_items(nc, k, name, bins, prep, C, G, NBIN, TM, TROW, HU, RW, records, pos_out=None, tile_bin=None, prefill=None):
    NG = C // G
    with Phase(nc, name) as ph:
        rec = ph.sb("rec", [P, C, RW])
        binrow = ph.sb("binrow", [P, NBIN])
        oh = ph.sb("oh", [P, 2, G, NBIN], BF16)
        zero = ph.sb("zero", [P, G * NBIN], BF16)
        count = ph.sb("count", [P, NBIN])
        counti = ph.sb("counti", [P, NBIN], I32)
        tiles = ph.sb("tiles", [P, NBIN])
        incl = ph.sb("incl", [P, 2, NBIN])
        run = ph.sb("run", [P, 2, NBIN])
        ranks = ph.sb("ranks", [P, G, NBIN])
        picked = ph.sb("picked", [P, G, NBIN])
        pos = ph.sb("pos", [P, C])
        low, high = ph.sb("low", [P, C]), ph.sb("high", [P, C])
        lowi, highi = ph.sb("lowi", [P, C], I32), ph.sb("highi", [P, C], I32)
        place = ph.sb("place", [P, C], I32)
        TQ = -(-TM // P)
        tno = ph.sb("tno", [P, TQ])
        tcmp = ph.sb("tcmp", [P, TQ, NBIN])
        tb = ph.sb("tb", [P, TQ])
        tbi = ph.sb("tbi", [P, TQ], I32)
        ring_place = ph.sb("ring_place", [P, 2, HU], I32)
        ring_rec = ph.sb("ring_rec", [P, 2, HU, RW])
        fill = ph.sb("fill", [P, TROW, RW])
        tb_dram = nc.dram_tensor(f"{name}_tbd", [TQ * P], I32, kind="Internal").ap()
        cnt_ps = ph.ps("cnt")
        rank_ps = [ph.ps(f"rank{j}") for j in range(2)]
        tot_ps = [ph.ps(f"tot{j}") for j in range(2)]

        loaded, step = ph.sem("loaded"), ph.sem("step")
        with ph.block() as block:
            @block.sync
            def _(sp):
                prep.loads(ph, sp, loaded)

            @block.gpsimd
            def _(pool):
                nc.gpsimd.iota(tno[:], [[1, TQ]], base=0, channel_multiplier=TQ, allow_small_or_imprecise_dtypes=True)

            @block.vector
            def _(dve):
                ch = Chain(dve, step)
                ch.mark(nc.vector.tensor_copy(binrow[:], k.cols[:, 0:NBIN]))
                ch.mark(nc.vector.memset(zero[:], 0.0))
                prep.compute(ph, dve, ch, loaded, bins, rec)
                ch.mark(nc.vector.memset(fill[:], 0.0))
                if prefill is not None:
                    ch.wait()
                    prefill(ch, fill)
                ch.wait()

        oh_made, counted, filled, step = ph.sem("oh_made"), ph.sem("counted"), ph.sem("filled"), ph.sem("step2")
        step3, tb_out = ph.sem("step3"), ph.sem("tb_out")
        flat = lambda a: a.rearrange("p g b -> p (g b)")

        def one_hot(g, j):
            return nc.vector.tensor_tensor(
                oh[:, j], bins[:, bass.ds(g * G, G)].unsqueeze(2).broadcast_to([P, G, NBIN]),
                binrow[:].unsqueeze(1).broadcast_to([P, G, NBIN]), ALU.is_equal)

        with ph.block() as block:
            @block.sync
            def _(sp):
                sp.dma_start(records.rearrange("(p t) r -> p t r", p=P), fill[:]).then_inc(filled, 16)
                sp.wait_ge(filled, 16)
                sp.wait_ge(step3, 1)
                sp.dma_start(tb_dram.rearrange("(p q) -> p q", p=P), tbi[:]).then_inc(tb_out, 16)
                sp.wait_ge(tb_out, 16)
                sp.dma_start(tile_bin[0:1, 0:TM], tb_dram[0:TM].unsqueeze(0)).then_inc(tb_out, 16)
                sp.wait_ge(tb_out, 32)

            @block.vector
            def _(dve):
                with dve.Fori(0, NG // 2) as i:
                    for j in range(2):
                        dve.wait_ge(counted, i * 2 + j + 1)
                        one_hot(i * 2 + j, j).then_inc(oh_made, 1)
                dve.wait_ge(counted, NG + 2)
                ch = Chain(dve, step)
                ch(nc.vector.reduce_sum(count[:], cnt_ps[:, 0:G * NBIN].rearrange("p (g b) -> p b g", g=G), AXX))
                ch(nc.vector.tensor_scalar_add(count[:], count[:], float(P - 1)))
                ch(nc.vector.tensor_copy(counti[:], count[:]))
                ch(nc.vector.tensor_scalar(counti[:], counti[:], LOGP, None, ALU.logical_shift_right))
                ch(nc.vector.tensor_copy(tiles[:], counti[:]))
                ch(nc.vector.tensor_copy(incl[:, 0], tiles[:]))
                cur, s = 0, 1
                while s < NBIN:
                    ch.mark(nc.vector.tensor_copy(incl[:, 1 - cur, 0:s], incl[:, cur, 0:s]))
                    ch(nc.vector.tensor_tensor(incl[:, 1 - cur, s:NBIN], incl[:, cur, s:NBIN], incl[:, cur, 0:NBIN - s], ALU.add))
                    cur, s = 1 - cur, s * 2
                ch(nc.vector.tensor_tensor(run[:, 0], incl[:, cur], tiles[:], ALU.subtract))
                ch(nc.vector.tensor_scalar_mul(run[:, 0], run[:, 0], float(P)))
                ch(nc.vector.tensor_tensor(tcmp[:], incl[:, cur].unsqueeze(1).broadcast_to([P, TQ, NBIN]),
                                           tno[:].unsqueeze(2).broadcast_to([P, TQ, NBIN]), ALU.is_le))
                ch(nc.vector.reduce_sum(tb[:], tcmp[:], AXX))
                ch(nc.vector.tensor_scalar_min(tb[:], tb[:], float(NBIN - 1)))
                nc.vector.tensor_copy(tbi[:], tb[:]).then_inc(step3, 1)

            @block.tensor
            def _(pe):
                pe.sem_inc(counted, 2)
                nc.tensor.matmul(cnt_ps[:, 0:G * NBIN], k.ones[:], zero[:], start=True, stop=False, skip_group_check=True)
                with pe.Fori(0, NG // 2) as i:
                    for j in range(2):
                        pe.wait_ge(oh_made, i * 2 + j + 1)
                        nc.tensor.matmul(cnt_ps[:, 0:G * NBIN], k.ones[:], flat(oh[:, j]), start=False, stop=False,
                                         skip_group_check=True).then_inc(counted, 1)

        oh2, ranked, used, step, run_s = ph.sem("oh2"), ph.sem("ranked"), ph.sem("used"), ph.sem("step4"), ph.sem("run")
        with ph.block() as block:
            @block.vector
            def _(dve):
                dve.sem_inc(used, 2)
                ch = Chain(dve, step)
                STEPS = 4
                one_hot(0, 0).then_inc(oh2, 1)
                with dve.Fori(0, NG // 2) as i:
                    for j in range(2):
                        g = i * 2 + j
                        if j == 0:
                            one_hot(g + 1, 1).then_inc(oh2, 1)
                        else:
                            one_hot(g + 1, 0).then_inc(oh2, 1)
                        dve.wait_ge(ranked, g + 1)
                        ch.at(g * STEPS)
                        ch.mark(nc.vector.tensor_tensor(run[:, 1 - j], run[:, j], tot_ps[j][:, 0:NBIN], ALU.add))
                        ch(nc.vector.tensor_tensor(ranks[:], rank_ps[j][:, 0:G * NBIN].rearrange("p (g b) -> p g b", g=G),
                                                   run[:, j].unsqueeze(1).broadcast_to([P, G, NBIN]), ALU.add))
                        ch(nc.vector.tensor_tensor(picked[:], ranks[:], oh[:, j], ALU.mult))
                        dve.sem_inc(used, 1)
                        ch(nc.vector.reduce_sum(pos[:, bass.ds(g * G, G)], picked[:], AXX))
                ch2 = Chain(dve, run_s)
                ch2(nc.vector.tensor_copy(place[:], pos[:]))
                ch2.mark(nc.vector.tensor_scalar(lowi[:], place[:], P - 1, None, ALU.bitwise_and))
                ch2(nc.vector.tensor_scalar(highi[:], place[:], LOGP, None, ALU.logical_shift_right))
                if pos_out is not None:
                    ch2.mark(nc.vector.tensor_copy(pos_out, pos[:]))
                ch2.mark(nc.vector.tensor_copy(low[:], lowi[:]))
                ch2(nc.vector.tensor_copy(high[:], highi[:]))
                ch2(nc.vector.scalar_tensor_tensor(low[:], low[:], float(TROW), high[:], ALU.mult, ALU.add))
                ch2(nc.vector.tensor_copy(place[:], low[:]))

            @block.tensor
            def _(pe):
                with pe.Fori(0, NG // 2) as i:
                    for j in range(2):
                        g = i * 2 + j
                        pe.wait_ge(oh2, g + 1)
                        pe.wait_ge(used, g + 1)
                        nc.tensor.matmul(rank_ps[j][:, 0:G * NBIN], k.before[:], flat(oh[:, j]), start=True, stop=False,
                                         skip_group_check=True)
                        for s in range(1, G):
                            nc.tensor.matmul(rank_ps[j][:, s * NBIN:G * NBIN], k.ones[:], flat(oh[:, j])[:, 0:(G - s) * NBIN],
                                             start=False, stop=(s == G - 1), skip_group_check=True)
                        for s in range(G):
                            last = nc.tensor.matmul(tot_ps[j][:, 0:NBIN], k.ones[:], oh[:, j, s], start=(s == 0), stop=(s == G - 1))
                        last.then_inc(ranked, 1)

        turns = ph.sem("turns")
        ringed = ph.sem("ringed")
        sent, before = ph.indirect(k, C // 2)
        with ph.block() as block:
            @block.vector
            def _(dve):
                def fill_ring(c0, j):
                    nc.vector.tensor_copy(ring_place[:, j], place[:, bass.ds(c0, HU)]).then_inc(ringed, 1)
                    nc.vector.tensor_copy(ring_rec[:, j], rec[:, bass.ds(c0, HU), :]).then_inc(ringed, 1)

                fill_ring(0, 0)
                fill_ring(HU, 1)
                with dve.Fori(1, C // (2 * HU)) as i:
                    for j in range(2):
                        dve.wait_ge(sent[j], before + i * (16 * HU))
                        fill_ring((i * 2 + j) * HU, j)

            @block.gpsimd
            def _(pool):
                with pool.Fori(0, C // (2 * HU)) as i:
                    for j in range(2):
                        pool.wait_ge(ringed, (i * 2 + j) * 2 + 2)
                        pool.sem_inc(turns)
                        for u in range(HU):
                            nc.gpsimd.indirect_dma_start(
                                out=records[:, :], out_offset=bass.IndirectOffsetOnAxis(ap=ring_place[:, j, u:u + 1], axis=0),
                                in_=ring_rec[:, j, u, :], in_offset=None).then_inc(sent[j], 16)
                for j in range(2):
                    pool.wait_ge(sent[j], before + C // 2 * 16)
    return tb_dram


class EdgePrep:

    def __init__(self, nc, key, other, weight):
        self.nc, self.key, self.other, self.weight = nc, key, other, weight

    def loads(self, ph, sp, loaded):
        self.ki, self.oi = ph.sb("ki", [P, EC], I32), ph.sb("oi", [P, EC], I32)
        self.w = ph.sb("w", [P, EC])
        zeroed = self.zeroed = ph.sem("zeroed")
        sp.wait_ge(zeroed, 3)
        for t, a in ((self.ki, self.key), (self.oi, self.other), (self.w, self.weight)):
            if a is None:
                continue
            sp.dma_start(t[0:P - 1, :], a[0:(P - 1) * EC].rearrange("(p c) -> p c", c=EC)).then_inc(loaded, 16)
            sp.dma_start(t[P - 1:P, 0:ELAST], a[(P - 1) * EC:E].unsqueeze(0)).then_inc(loaded, 16)

    def compute(self, ph, dve, ch, loaded, bins, rec):
        nc = self.nc
        nc.vector.memset(self.ki[:], (NB - 1) * P).then_inc(self.zeroed, 1)
        nc.vector.memset(self.oi[:], 0).then_inc(self.zeroed, 1)
        nc.vector.memset(self.w[:], 0.0).then_inc(self.zeroed, 1)
        kl, kb = ph.sb("kl", [P, EC], I32), ph.sb("kb", [P, EC], I32)
        dve.wait_ge(loaded, 64 if self.weight is None else 96)
        ch.mark(nc.vector.memset(bins[:, EC:], 0.0))
        ch.mark(nc.vector.memset(rec[:], 0.0))
        ch.mark(nc.vector.tensor_scalar(kl[:], self.ki[:], P - 1, None, ALU.bitwise_and))
        ch(nc.vector.tensor_scalar(kb[:], self.ki[:], LOGP, None, ALU.logical_shift_right))
        ch.mark(nc.vector.tensor_copy(rec[:, :, 0], self.oi[:]))
        ch.mark(nc.vector.tensor_copy(rec[:, :, 2], self.w[:]))
        ch.mark(nc.vector.tensor_copy(rec[:, :, 1], kl[:]))
        ch(nc.vector.tensor_copy(bins[:, 0:EC], kb[:]))


def sort_edges(nc, k, name, key, other, weight, SRT, tile_block, zero_tail=None):
    records = nc.dram_tensor(f"{name}_records", [P * EROW, 4], F32, kind="Internal").ap()
    G = 8
    with Phase(nc, f"{name}b") as ph:
        bins = ph.sb("bins", [P, EC + G])

        def prefill(ch, fill):
            ch(nc.vector.memset(fill[:, :, 1], -1.0))

        sort_items(nc, k, name, bins, EdgePrep(nc, key, other, weight), EC, G, NB, ET, EROW, 8, 4, records,
                   tile_bin=tile_block, prefill=prefill)
    with Phase(nc, f"{name}l") as ph:
        loaded, zeroed = ph.sem("loaded"), ph.sem("zeroed")
        with ph.block() as block:
            @block.vector
            def _(dve):
                nc.vector.memset(tile_block[0:1, ET:EROW], 0).then_inc(zeroed, 1)
                if zero_tail is not None:
                    nc.vector.memset(zero_tail[:, ET:EROW, :], 0.0).then_inc(zeroed, 1)

            @block.sync
            def _(sp):
                sp.dma_start(SRT[:], records.rearrange("(p t) r -> p t r", p=P)).then_inc(loaded, 16)
                sp.wait_ge(loaded, 16)


def propagate(nc, k, hop, table, SRT, tile_block, agg):
    with Phase(nc, f"prop{hop}") as ph:
        G = ph.sb("G", [P, 2, U, D])
        idx = ph.sb("idx", [P, 2, U], I32)
        lw = ph.sb("lw", [P, 2, U, 2])
        S = ph.sb("S", [P, 2, U, P])
        ps = [ph.ps(f"sum{u}") for u in range(U)]
        prepped, built, mm, added = ph.sem("prepped"), ph.sem("built"), ph.sem("mm"), ph.sem("added")
        zeroed, turns = ph.sem("zeroed"), ph.sem("turns")
        got, before = ph.indirect(k, ET // 2)
        PAIRS = ET // (2 * U)
        with ph.block() as block:
            @block.scalar
            def _(act):
                def prep(n, hf, first=False):
                    if not first:
                        act.wait_ge(mm, U * n + U)
                    nc.scalar.copy(idx[:, hf], SRT[:, bass.ds(n * U, U), 0]).then_inc(prepped, 1)
                    nc.scalar.copy(lw[:, hf], SRT[:, bass.ds(n * U, U), 1:3]).then_inc(prepped, 1)
                prep(0, 0, True)
                with act.Fori(0, PAIRS) as i:
                    prep(2 * i + 1, 1)
                    prep(2 * i + 2, 0)

            @block.gpsimd
            def _(pool):
                with pool.Fori(0, PAIRS) as i:
                    for hf in range(2):
                        n = 2 * i + hf
                        pool.wait_ge(prepped, 2 * n + 2)
                        pool.sem_inc(turns)
                        pool.wait_ge(mm, U * n + U)
                        pool.sem_inc(turns)
                        for u in range(U):
                            nc.gpsimd.indirect_dma_start(
                                out=G[:, hf, u, :], out_offset=None, in_=table[:, :],
                                in_offset=bass.IndirectOffsetOnAxis(ap=idx[:, hf, u:u + 1], axis=0)).then_inc(got[hf], 16)

            @block.tensor
            def _(pe):
                pe.sem_inc(mm, 2 * U)
                with pe.Fori(0, PAIRS) as i:
                    for hf in range(2):
                        n = 2 * i + hf
                        pe.wait_ge(got[hf], before + i * (16 * U) + 16 * U)
                        for u in range(U):
                            pe.wait_ge(built, n * U + u + 1)
                            pe.wait_ge(added, n * U + u + 1)
                            nc.tensor.matmul(ps[u][:, 0:D], S[:, hf, u, :], G[:, hf, u, :], start=True, stop=True).then_inc(mm, 1)

            @block.vector
            def _(dve):
                dve.sem_inc(added, U)
                nc.vector.memset(agg[:], 0.0).then_inc(zeroed, 1)
                dve.wait_ge(zeroed, 1)

                def build(n, hf, u):
                    if u == 0:
                        dve.wait_ge(prepped, 2 * n + 2)
                    nc.vector.tensor_scalar(S[:, hf, u, :], k.cols[:], lw[:, hf, u, 0:1], lw[:, hf, u, 1:2],
                                            ALU.is_equal, ALU.mult).then_inc(built, 1)

                for u in range(U):
                    build(0, 0, u)
                with dve.Fori(0, PAIRS) as i:
                    for hf in range(2):
                        n = 2 * i + hf
                        for u in range(U):
                            build(n + 1, 1 - hf, u)
                            b = dve.value_load(tile_block[0:1, bass.ds(n * U + u, 1)], min_val=0, max_val=NB - 1)
                            dve.wait_ge(mm, 2 * U + n * U + u + 1)
                            dve.wait_ge(added, U + n * U + u)
                            nc.vector.tensor_tensor(agg[:, bass.ds(b, 1), :], agg[:, bass.ds(b, 1), :],
                                                    ps[u][:, 0:D].unsqueeze(1), ALU.add).then_inc(added, 1)


def load_broadcast(nc, sp, dst, src, sem):
    sp.dma_start(dst, src.unsqueeze(0).broadcast_to([P, src.shape[0]])).then_inc(sem, 16)


def gat_tables(nc, k, X, W_src, W_dst, att_src, att_dst, table, atable, QT):
    W8 = D + 2 * HEADS
    with Phase(nc, "gt") as ph:
        W = ph.sb("W", [P, KD, W8])
        Wd = ph.sb("Wd", [P, KD, D])
        att = ph.sb("att", [P, 2, D])
        prod = ph.sb("prod", [P, KD, D])
        norm = RowNorm(nc, ph, X)
        xn = ph.sb("xn", [P, 2, 1, D])
        xT = ph.sb("xT", [P, 2, KD, P])
        hs = ph.sb("hs", [P, 2, D])
        A = ph.sb("A", [P, NB, 2 * HEADS])
        mins = ph.sb("mins", [P, HEADS])
        shift = ph.sb("shift", [P, HEADS])
        As = ph.sb("As", [P, NB, HEADS])
        psT = [ph.ps(f"T{j}") for j in range(2)]
        psH = [ph.ps(f"H{j}") for j in range(2)]
        loaded, step = ph.sem("loaded"), ph.sem("step")
        normed = ph.sem("normed")
        trans, copied, prod_s, taken = ph.sem("trans"), ph.sem("copied"), ph.sem("prod"), ph.sem("taken")
        stored, folded = [ph.sem("stored0"), ph.sem("stored1")], ph.sem("folded")
        reduced, shifted, end = ph.sem("reduced"), ph.sem("shifted"), ph.sem("end")
        with ph.block() as block:
            @block.sync
            def _(sp):
                sp.dma_start(W[:, :, 0:D], W_src.rearrange("(k p) n -> p k n", p=P)).then_inc(loaded, 16)
                sp.dma_start(Wd[:], W_dst.rearrange("(k p) n -> p k n", p=P)).then_inc(loaded, 16)
                load_broadcast(nc, sp, att[:, 0, :], att_src.rearrange("h c -> (h c)"), loaded)
                load_broadcast(nc, sp, att[:, 1, :], att_dst.rearrange("h c -> (h c)"), loaded)
                with sp.Fori(0, NB // 2) as i:
                    for j in range(2):
                        sp.wait_ge(taken, 4 * i + 2 * j + 2)
                        sp.dma_start(table[bass.ds((2 * i + j) * P, P), :], hs[:, j]).then_inc(stored[j], 16)
                sp.wait_ge(shifted, 1)
                sp.dma_start(atable.rearrange("(b p) h -> p b h", p=P), As[:]).then_inc(end, 16)
                sp.wait_ge(end, 16)
                for j in range(2):
                    sp.wait_ge(stored[j], 16 * NB // 2)

            @block.vector
            def _(dve):
                ch = Chain(dve, step)
                norm.stats(dve, ch)
                dve.wait_ge(loaded, 64)
                for j, w in ((0, W[:, :, 0:D]), (1, Wd[:])):
                    ch(nc.vector.tensor_tensor(prod[:], w, att[:, j].unsqueeze(1).broadcast_to([P, KD, D]), ALU.mult))
                    ch(nc.vector.reduce_sum(W[:, :, D + HEADS * j:D + HEADS * (j + 1)],
                                            prod[:].rearrange("p k (h c) -> p k h c", h=HEADS), AXX))
                nc.vector.memset(mins[:], 0.0).then_inc(folded, 1)

                def normalise(n, j):
                    norm.apply(xn[:, j], n).then_inc(normed, 1)

                def take(i, j, first=False):
                    dve.wait_ge(prod_s, 2 * i + j + 1)
                    if not first:
                        dve.wait_ge(stored[j], 16 * i)
                    nc.vector.tensor_copy(hs[:, j], psH[j][:, 0:D]).then_inc(taken, 1)
                    nc.vector.tensor_copy(A[:, bass.ds(2 * i + j, 1), :], psH[j][:, D:W8].unsqueeze(1)).then_inc(taken, 1)

                normalise(0, 0)
                normalise(1, 1)
                take(0, 0, True)
                take(0, 1, True)
                with dve.Fori(1, NB // 2) as i:
                    normalise(2 * i, 0)
                    normalise(2 * i + 1, 1)
                    take(i, 0)
                    take(i, 1)
                dve.wait_ge(taken, 2 * NB)
                ch(nc.vector.tensor_scalar_mul(As[:], A[:, :, 0:HEADS], -1.0))
                nc.vector.tensor_reduce(mins[:], As[:].rearrange("p b h -> p h b"), AXX, ALU.max).then_inc(reduced, 1)
                dve.wait_ge(reduced, 2)
                sh = shift[:].unsqueeze(1).broadcast_to([P, NB, HEADS])
                nc.vector.tensor_tensor(As[:], A[:, :, 0:HEADS], sh, ALU.add).then_inc(shifted, 1)
                ch(nc.vector.tensor_tensor(QT[:, :, 0:HEADS], A[:, :, HEADS:2 * HEADS], sh, ALU.subtract))

            @block.gpsimd
            def _(pool):
                pool.wait_ge(reduced, 1)
                nc.gpsimd.partition_all_reduce(shift[:], mins[:], P, bass.bass_isa.ReduceOp.max).then_inc(reduced, 1)

            @block.tensor
            def _(pe):
                pe.wait_ge(folded, 1)

                def block_of(i, j, first=False):
                    n = 2 * i + j
                    pe.wait_ge(normed, n + 1)
                    if not first:
                        pe.wait_ge(copied, n - 1)
                    for c in range(KD):
                        last = nc.tensor.transpose(psT[j][:, c * P:(c + 1) * P], xn[:, j, 0, c * P:(c + 1) * P], k.ident[:])
                    last.then_inc(trans, 1)
                    pe.wait_ge(copied, n + 1)
                    if not first:
                        pe.wait_ge(taken, 2 * n - 2)
                    for c in range(KD):
                        last = nc.tensor.matmul(psH[j][:, 0:W8], xT[:, j, c], W[:, c], start=(c == 0), stop=(c == KD - 1))
                    last.then_inc(prod_s, 1)

                block_of(0, 0, True)
                block_of(0, 1, True)
                with pe.Fori(1, NB // 2) as i:
                    block_of(i, 0)
                    block_of(i, 1)

            @block.scalar
            def _(act):
                norm.root(act)

                def copy(i, j, first=False):
                    n = 2 * i + j
                    act.wait_ge(trans, n + 1)
                    if not first:
                        act.wait_ge(prod_s, n - 1)
                    nc.scalar.copy(xT[:, j], psT[j][:, 0:D].rearrange("p (c n) -> p c n", c=KD)).then_inc(copied, 1)
                copy(0, 0, True)
                copy(0, 1, True)
                with act.Fori(1, NB // 2) as i:
                    copy(i, 0)
                    copy(i, 1)


def gat_max(nc, k, atable, SRT, tile_block, AE, QT):
    with Phase(nc, "gm") as ph:
        AG = ph.sb("AG", [P, 2, U, HEADS])
        idx = ph.sb("idx", [P, 2, U], I32)
        loc = ph.sb("loc", [P, 2, U])
        S = ph.sb("S", [P, 2, U, P])
        diag = ph.sb("diag", [P, 2, HEADS, P])
        top = ph.sb("top", [P, U, HEADS])
        MX = ph.sb("MX", [P, NB, HEADS])
        lk = ph.sb("lk", [P, NB, HEADS])
        NPS = 4
        ps = [ph.ps(f"m{u}") for u in range(U)]
        prepped, built, mm, topped, maxed = ph.sem("prepped"), ph.sem("built"), ph.sem("mm"), ph.sem("topped"), ph.sem("maxed")
        zeroed, turns, diags, kept, step = ph.sem("zeroed"), ph.sem("turns"), ph.sem("diags"), ph.sem("kept"), ph.sem("step")
        got, before = ph.indirect(k, ET // 2)
        PAIRS = ET // (2 * U)
        with ph.block() as block:
            @block.scalar
            def _(act):
                def prep(n, hf, first=False):
                    if not first:
                        act.wait_ge(mm, U * n + U)
                    nc.scalar.copy(idx[:, hf], SRT[:, bass.ds(n * U, U), 0]).then_inc(prepped, 1)
                    nc.scalar.copy(loc[:, hf], SRT[:, bass.ds(n * U, U), 1]).then_inc(prepped, 1)

                def diagonals(n, hf, i):
                    act.wait_ge(got[hf], before + i * (16 * U) + 16 * U)
                    nc.scalar.copy(AE[:, bass.ds(n * U, U), :], AG[:, hf]).then_inc(kept, 1)
                    for u in range(U):
                        act.wait_ge(mm, n * U + u + 2 * U - 1)
                        for h in range(HEADS):
                            nc.scalar.activation(diag[:, (hf * U + u) % 2, h], k.ident[:], ACT.Copy,
                                                 scale=AG[:, hf, u, h:h + 1]).then_inc(diags, 1)
                prep(0, 0, True)
                with act.Fori(0, PAIRS) as i:
                    prep(2 * i + 1, 1)
                    diagonals(2 * i, 0, i)
                    prep(2 * i + 2, 0)
                    diagonals(2 * i + 1, 1, i)

            @block.gpsimd
            def _(pool):
                with pool.Fori(0, PAIRS) as i:
                    for hf in range(2):
                        n = 2 * i + hf
                        pool.wait_ge(prepped, 2 * n + 2)
                        pool.sem_inc(turns)
                        pool.wait_ge(mm, U * n + U)
                        pool.sem_inc(turns)
                        for u in range(U):
                            nc.gpsimd.indirect_dma_start(
                                out=AG[:, hf, u, :], out_offset=None, in_=atable[:, :],
                                in_offset=bass.IndirectOffsetOnAxis(ap=idx[:, hf, u:u + 1], axis=0)).then_inc(got[hf], 16)

            @block.tensor
            def _(pe):
                pe.sem_inc(mm, 2 * U)
                with pe.Fori(0, PAIRS) as i:
                    for hf in range(2):
                        n = 2 * i + hf
                        for u in range(U):
                            pe.wait_ge(built, n * U + u + 1)
                            pe.wait_ge(diags, (n * U + u + 1) * HEADS)
                            pe.wait_ge(topped, n * U + u + 1)
                            nc.tensor.matmul(ps[u][:, 0:HEADS * P], S[:, hf, u, :],
                                             diag[:, (hf * U + u) % 2].rearrange("p h e -> p (h e)"), start=True, stop=True).then_inc(mm, 1)

            @block.vector
            def _(dve):
                dve.sem_inc(topped, U)
                nc.vector.memset(MX[:], 0.0).then_inc(zeroed, 1)
                dve.wait_ge(zeroed, 1)

                def build(n, hf, u):
                    if u == 0:
                        dve.wait_ge(prepped, 2 * n + 2)
                    nc.vector.tensor_scalar(S[:, hf, u, :], k.cols[:], loc[:, hf, u:u + 1], None,
                                            ALU.is_equal).then_inc(built, 1)

                for u in range(U):
                    build(0, 0, u)
                with dve.Fori(0, PAIRS) as i:
                    for hf in range(2):
                        n = 2 * i + hf
                        for u in range(U):
                            dve.wait_ge(mm, 2 * U + n * U + u + 1)
                            nc.vector.tensor_reduce(top[:, u], ps[u][:, 0:HEADS * P].rearrange("p (h e) -> p h e", h=HEADS),
                                                    AXX, ALU.max).then_inc(topped, 1)
                            build(n + 1, 1 - hf, u)
                            b = dve.value_load(tile_block[0:1, bass.ds(n * U + u, 1)], min_val=0, max_val=NB - 1)
                            dve.wait_ge(topped, U + n * U + u + 1)
                            if not (hf == 0 and u == 0):
                                dve.wait_ge(maxed, n * U + u)
                            else:
                                dve.wait_ge(maxed, n * U)
                            nc.vector.tensor_tensor(MX[:, bass.ds(b, 1), :], MX[:, bass.ds(b, 1), :],
                                                    top[:, u].unsqueeze(1), ALU.max).then_inc(maxed, 1)
                dve.wait_ge(maxed, ET)
                ch = Chain(dve, step)
                ch(nc.vector.tensor_tensor(lk[:], MX[:], QT[:, :, 0:HEADS], ALU.add))
                ch(nc.vector.scalar_tensor_tensor(QT[:, :, HEADS:2 * HEADS], lk[:], NEG_SLOPE, lk[:], ALU.mult, ALU.max))


HW = HD + 1


def gat_sum(nc, k, table, SRT, tile_block, AE, QT, acc):
    with Phase(nc, "gs") as ph:
        G = ph.sb("G", [P, 2, U, D])
        idx = ph.sb("idx", [P, 2, U], I32)
        loc = ph.sb("loc", [P, 2, U])
        S = ph.sb("S", [P, 2, U, P])
        ST = ph.sb("ST", [P, 2, P])
        e1 = ph.sb("e1", [P, U, HEADS])
        e2 = ph.sb("e2", [P, U, HEADS])
        e3 = ph.sb("e3", [P, U, HEADS])
        M = ph.sb("M", [P, 2, U, HEADS, HW])
        NO = 4
        psT = [ph.ps(f"T{j}") for j in range(2)]
        psQ = [ph.ps(f"Q{j}") for j in range(2)]
        psO = [ph.ps(f"O{j}") for j in range(NO)]
        prepped, built, mm, added = ph.sem("prepped"), ph.sem("built"), ph.sem("mm"), ph.sem("added")
        zeroed, turns, trans, tcopied = ph.sem("zeroed"), ph.sem("turns"), ph.sem("trans"), ph.sem("tcopied")
        asked, es, logits, weighed, msgs = ph.sem("asked"), ph.sem("es"), ph.sem("logits"), ph.sem("weighed"), ph.sem("msgs")
        got, before = ph.indirect(k, ET // 2)
        PAIRS = ET // (2 * U)
        with ph.block() as block:
            @block.scalar
            def _(act):
                def prep(n, hf, first=False):
                    if not first:
                        act.wait_ge(mm, U * n + U)
                    nc.scalar.copy(idx[:, hf], SRT[:, bass.ds(n * U, U), 0]).then_inc(prepped, 1)
                    nc.scalar.copy(loc[:, hf], SRT[:, bass.ds(n * U, U), 1]).then_inc(prepped, 1)

                def weigh(n, hf):
                    for u in range(U):
                        act.wait_ge(trans, n * U + u + 1)
                        act.wait_ge(asked, n * U + u + 1)
                        nc.scalar.copy(ST[:, (hf * U + u) % 2], psT[(hf * U + u) % 2][:, 0:P]).then_inc(tcopied, 1)
                    act.wait_ge(logits, n + 1)
                    nc.scalar.activation(M[:, hf, :, :, HD], e3[:], ACT.Exp).then_inc(weighed, 1)

                prep(0, 0, True)
                weigh(0, 0)
                with act.Fori(0, PAIRS) as i:
                    prep(2 * i + 1, 1)
                    weigh(2 * i + 1, 1)
                    prep(2 * i + 2, 0)
                    weigh(2 * i + 2, 0)

            @block.gpsimd
            def _(pool):
                with pool.Fori(0, PAIRS) as i:
                    for hf in range(2):
                        n = 2 * i + hf
                        pool.wait_ge(prepped, 2 * n + 2)
                        pool.sem_inc(turns)
                        pool.wait_ge(mm, U * n + U)
                        pool.sem_inc(turns)
                        for u in range(U):
                            nc.gpsimd.indirect_dma_start(
                                out=G[:, hf, u, :], out_offset=None, in_=table[:, :],
                                in_offset=bass.IndirectOffsetOnAxis(ap=idx[:, hf, u:u + 1], axis=0)).then_inc(got[hf], 16)

            @block.tensor
            def _(pe):
                pe.sem_inc(mm, 2 * U)
                pe.sem_inc(asked, 2)

                def ask(n, hf, u):
                    r = (hf * U + u) % 2
                    pe.wait_ge(built, n * U + u + 1)
                    nc.tensor.transpose(psT[r][:, 0:P], S[:, hf, u, :], k.ident[:]).then_inc(trans, 1)
                    b = pe.value_load(tile_block[0:1, bass.ds(n * U + u, 1)], min_val=0, max_val=NB - 1)
                    pe.wait_ge(tcopied, n * U + u + 1)
                    if u == 0:
                        pe.wait_ge(es, n + 1)
                    nc.tensor.matmul(psQ[hf][:, u * 2 * HEADS:(u + 1) * 2 * HEADS], ST[:, r],
                                     QT[:, bass.ds(b, 1), :].rearrange("p a q -> p (a q)"), start=True, stop=True).then_inc(asked, 1)

                for u in range(U):
                    ask(0, 0, u)
                with pe.Fori(0, PAIRS) as i:
                    for hf in range(2):
                        n = 2 * i + hf
                        for u in range(U):
                            ask(n + 1, 1 - hf, u)
                            o = (hf * U + u) % NO
                            pe.wait_ge(msgs, n * U + u + 1)
                            pe.wait_ge(added, n * U + u + 1)
                            nc.tensor.matmul(psO[u % NO][:, 0:HEADS * HW], S[:, hf, u, :],
                                             M[:, hf, u].rearrange("p h c -> p (h c)"), start=True, stop=True).then_inc(mm, 1)

            @block.vector
            def _(dve):
                dve.sem_inc(added, NO)
                dve.sem_inc(es, 2)
                nc.vector.memset(acc[:], 0.0).then_inc(zeroed, 1)
                dve.wait_ge(zeroed, 1)
                ch = Chain(dve, zeroed)

                def build(n, hf, u):
                    if u == 0:
                        dve.wait_ge(prepped, 2 * n + 2)
                    nc.vector.tensor_scalar(S[:, hf, u, :], k.cols[:], loc[:, hf, u:u + 1], None,
                                            ALU.is_equal).then_inc(built, 1)

                def edge_logits(n, hf):
                    ch.at(3 * n + 1)
                    dve.wait_ge(asked, 2 + n * U + U)
                    q = psQ[hf][:, 0:U * 2 * HEADS].rearrange("p (u q) -> p u q", u=U)
                    dve.wait_ge(weighed, n) if n is not 0 else None
                    ch(nc.vector.tensor_tensor(e1[:], AE[:, bass.ds(n * U, U), :], q[:, :, 0:HEADS], ALU.add))
                    ch(nc.vector.scalar_tensor_tensor(e2[:], e1[:], NEG_SLOPE, e1[:], ALU.mult, ALU.max))
                    ch(nc.vector.tensor_tensor(e1[:], e2[:], q[:, :, HEADS:2 * HEADS], ALU.subtract))
                    dve.sem_inc(es, 1)
                    nc.vector.tensor_scalar_min(e3[:], e1[:], 0.0).then_inc(logits, 1)

                for u in range(U):
                    build(0, 0, u)
                edge_logits(0, 0)
                with dve.Fori(0, PAIRS) as i:
                    for hf in range(2):
                        n = 2 * i + hf
                        dve.wait_ge(weighed, n + 1)
                        dve.wait_ge(got[hf], before + i * (16 * U) + 16 * U)

                        def message(u):
                            nc.vector.tensor_tensor(M[:, hf, u, :, 0:HD], G[:, hf, u].rearrange("p (h c) -> p h c", h=HEADS),
                                                    M[:, hf, u, :, HD:HW].broadcast_to([P, HEADS, HD]), ALU.mult).then_inc(msgs, 1)
                        message(0)
                        for u in range(U):
                            build(n + 1, 1 - hf, u)
                            if u + 1 < U:
                                message(u + 1)
                            b = dve.value_load(tile_block[0:1, bass.ds(n * U + u, 1)], min_val=0, max_val=NB - 1)
                            dve.wait_ge(mm, 2 * U + n * U + u + 1)
                            dve.wait_ge(added, NO + n * U + u)
                            a = acc[:, bass.ds(b, 1), :, :].rearrange("p a h c -> p a (h c)")
                            nc.vector.tensor_tensor(a, a, psO[u % NO][:, 0:HEADS * HW].unsqueeze(1), ALU.add).then_inc(added, 1)
                        edge_logits(n + 1, 1 - hf)


def gat_finish(nc, k, X, acc, bias, gamma, beta, prelu):
    with Phase(nc, "gf") as ph:
        vec = ph.sb("vec", [P, 4, D])
        den = ph.sb("den", [P, NB, HEADS])
        XL = ph.sb("XL", [P, NB, D])
        loaded, step, made = ph.sem("loaded"), ph.sem("step"), ph.sem("made")
        norm = RowNorm(nc, ph, XL)
        row = lambda j: vec[:, j].unsqueeze(1).broadcast_to([P, NB, D])
        with ph.block() as block:
            @block.sync
            def _(sp):
                for j, v in enumerate((bias, gamma, beta, prelu)):
                    load_broadcast(nc, sp, vec[:, j, :], v, loaded)

            @block.scalar
            def _(act):
                norm.root(act)

            @block.vector
            def _(dve):
                ch = Chain(dve, step)
                ch(nc.vector.tensor_scalar_max(den[:], acc[:, :, :, HD], 1e-16))
                ch(nc.vector.reciprocal(den[:], den[:]))
                for h in range(HEADS):
                    ch.mark(nc.vector.tensor_tensor(XL[:, :, h * HD:(h + 1) * HD], acc[:, :, h, 0:HD],
                                                    den[:, :, h:h + 1].broadcast_to([P, NB, HD]), ALU.mult))
                ch.wait()
                dve.wait_ge(loaded, 64)
                ch(nc.vector.tensor_tensor(XL[:], XL[:], row(0), ALU.add))
                norm.all(dve, ch, XL)
                ch(nc.vector.tensor_tensor(XL[:], XL[:], row(1), ALU.mult))
                ch(nc.vector.tensor_tensor(XL[:], XL[:], row(2), ALU.add))
                neg = acc[:].rearrange("p b h c -> p (b h c)")[:, 0:NB * D].rearrange("p (b d) -> p b d", b=NB)
                ch(nc.vector.scalar_tensor_tensor(neg, XL[:], 0.0, row(3), ALU.min, ALU.mult))
                ch(nc.vector.scalar_tensor_tensor(XL[:], XL[:], 0.0, neg, ALU.max, ALU.add))
                ch(nc.vector.tensor_tensor(X[:], X[:], XL[:], ALU.add))


def gat_layer(nc, k, X, src, dst, W_src, W_dst, att_src, att_dst, bias, gamma, beta, prelu):
    table = nc.dram_tensor("gat_table", [NP, D], F32, kind="Internal").ap()
    atable = nc.dram_tensor("gat_atable", [NP, HEADS], F32, kind="Internal").ap()
    with Phase(nc, "gat") as ph:
        SRT, tbk = ph.sb("SRT", [P, EROW, 4]), ph.sb("tbk", [1, EROW], I32)
        QT, AE = ph.sb("QT", [P, NB, 2 * HEADS]), ph.sb("AE", [P, EROW, HEADS])
        sort_edges(nc, k, "sd", dst, src, None, SRT, tbk, zero_tail=AE)
        gat_tables(nc, k, X, W_src, W_dst, att_src, att_dst, table, atable, QT)
        gat_max(nc, k, atable, SRT, tbk, AE, QT)
        with Phase(nc, "gacc") as pa:
            acc = pa.sb("acc", [P, NB, HEADS, HW])
            gat_sum(nc, k, table, SRT, tbk, AE, QT, acc)
            gat_finish(nc, k, X, acc, bias, gamma, beta, prelu)


NE = 8
TOPK = 2
HID = 1024
KH = HID // P
MC = NB * TOPK
MU = 2
MT = (P * MC + NE * (P - 1)) // P // MU * MU + MU
BANK = 512


class ItemPrep:

    def __init__(self, nc, k, expert):
        self.nc, self.k, self.expert = nc, k, expert

    def loads(self, ph, sp, loaded):
        pass

    def compute(self, ph, dve, ch, loaded, bins, rec):
        nc = self.nc
        node = ph.sb("node", [P, NB])
        ch.mark(nc.vector.memset(bins[:, MC:], 0.0))
        ch.mark(nc.vector.tensor_copy(bins[:, 0:MC], self.expert[:].rearrange("p k b -> p (k b)")))
        ch(nc.vector.tensor_scalar(node[:], self.k.cols[:, 0:NB], float(P), self.k.part[:, 0:1], ALU.mult, ALU.add))
        for j in range(TOPK):
            ch.mark(nc.vector.tensor_copy(rec[:, j * NB:(j + 1) * NB, 0], node[:]))


def moe_route(nc, k, X, Wr, br, table, expert, weight):
    with Phase(nc, "mr") as ph:
        norm = RowNorm(nc, ph, X)
        XT1 = ph.sb("xt", [P, NB, D])
        norm2 = RowNorm(nc, ph, XT1, "2")
        xs = ph.sb("xs", [P, 2, D])
        xT = ph.sb("xT", [P, 2, KD, P])
        W = ph.sb("W", [P, KD, NE])
        b1 = ph.sb("b", [1, NE])
        L = ph.sb("L", [P, NB, NE])
        Pr = ph.sb("Pr", [P, NB, NE])
        eq = ph.sb("eq", [P, NB, NE])
        m = ph.sb("m", [P, TOPK, NB])
        s = ph.sb("s", [P, NB])
        psT = [ph.ps(f"T{j}") for j in range(2)]
        psL = [ph.ps(f"L{j}") for j in range(2)]
        loaded, step = ph.sem("loaded"), ph.sem("step")
        ready, trans, copied, prods, taken = ph.sem("ready"), ph.sem("trans"), ph.sem("copied"), ph.sem("prods"), ph.sem("taken")
        centred, exped, tabled, stored = ph.sem("centred"), ph.sem("exped"), ph.sem("tabled"), ph.sem("stored")
        with ph.block() as block:
            @block.sync
            def _(sp):
                sp.dma_start(W[:], Wr.rearrange("(k p) n -> p k n", p=P)).then_inc(loaded, 16)
                sp.dma_start(b1[:], br.unsqueeze(0)).then_inc(loaded, 16)
                sp.wait_ge(tabled, 1)
                sp.dma_start(table.rearrange("(b p) d -> p b d", p=P), XT1[:]).then_inc(stored, 16)
                sp.wait_ge(stored, 16)

            @block.vector
            def _(dve):
                ch = Chain(dve, step)
                norm.all(dve, ch, XT1)
                nc.vector.tensor_copy(xs[:, 0], XT1[:, 0]).then_inc(ready, 1)
                nc.vector.tensor_copy(xs[:, 1], XT1[:, 1]).then_inc(ready, 1)

                def take(n, j):
                    dve.wait_ge(prods, n + 1)
                    nc.vector.tensor_copy(L[:, bass.ds(n, 1), :], psL[j][:, 0:NE].unsqueeze(1)).then_inc(taken, 1)

                with dve.Fori(0, NB // 2 - 1) as i:
                    for j in range(2):
                        take(2 * i + j, j)
                        nc.vector.tensor_copy(xs[:, j].unsqueeze(1), XT1[:, bass.ds(2 * i + j + 2, 1)]).then_inc(ready, 1)
                take(NB - 2, 0)
                take(NB - 1, 1)
                dve.wait_ge(taken, NB)
                norm2.stats(dve, ch)
                with dve.Fori(0, NB) as b:
                    norm2.apply(XT1[:, bass.ds(b, 1), :], b).then_inc(ch.sem, 1)
                ch.n += NB
                ch.wait()
                ch(nc.vector.reduce_max(s[:], L[:], AXX))
                dve.sem_inc(tabled, 1)
                wide = lambda a: a.unsqueeze(2).broadcast_to([P, NB, NE])
                nc.vector.tensor_tensor(L[:], L[:], wide(s[:]), ALU.subtract).then_inc(centred, 1)
                dve.wait_ge(exped, 1)
                ch(nc.vector.reduce_sum(s[:], Pr[:], AXX))
                ch(nc.vector.reciprocal(s[:], s[:]))
                ch(nc.vector.tensor_tensor(Pr[:], Pr[:], wide(s[:]), ALU.mult))
                iota = k.cols[:, 0:NE].unsqueeze(1).broadcast_to([P, NB, NE])
                for j in range(TOPK):
                    ch(nc.vector.reduce_max(m[:, j], Pr[:], AXX))
                    ch(nc.vector.tensor_tensor(eq[:], Pr[:], wide(m[:, j]), ALU.is_equal))
                    ch(nc.vector.tensor_scalar(L[:], iota, -1.0, float(NE), ALU.mult, ALU.add))
                    ch(nc.vector.tensor_tensor(eq[:], eq[:], L[:], ALU.mult))
                    ch(nc.vector.reduce_max(s[:], eq[:], AXX))
                    ch(nc.vector.tensor_scalar(expert[:, j], s[:], -1.0, float(NE), ALU.mult, ALU.add))
                    if j + 1 < TOPK:
                        ch(nc.vector.tensor_tensor(eq[:], iota, wide(expert[:, j]), ALU.is_equal))
                        ch(nc.vector.scalar_tensor_tensor(Pr[:], eq[:], -2.0, Pr[:], ALU.mult, ALU.add))
                ch(nc.vector.tensor_tensor(s[:], m[:, 0], m[:, 1], ALU.add))
                ch(nc.vector.reciprocal(s[:], s[:]))
                for j in range(TOPK):
                    ch.mark(nc.vector.tensor_tensor(weight[:, j], m[:, j], s[:], ALU.mult))
                ch.wait()

            @block.scalar
            def _(act):
                norm.root(act)
                with act.Fori(0, NB // 2) as i:
                    for j in range(2):
                        act.wait_ge(trans, 2 * i + j + 1)
                        nc.scalar.copy(xT[:, j], psT[j][:, 0:D].rearrange("p (c n) -> p c n", c=KD)).then_inc(copied, 1)
                norm2.root(act)
                act.wait_ge(centred, 1)
                nc.scalar.activation(Pr[:], L[:], ACT.Exp).then_inc(exped, 1)

            @block.tensor
            def _(pe):
                pe.wait_ge(loaded, 32)
                with pe.Fori(0, NB // 2) as i:
                    for j in range(2):
                        n = 2 * i + j
                        pe.wait_ge(ready, n + 1)
                        for c in range(KD):
                            last = nc.tensor.transpose(psT[j][:, c * P:(c + 1) * P], xs[:, j, c * P:(c + 1) * P], k.ident[:])
                        last.then_inc(trans, 1)
                        pe.wait_ge(copied, n + 1)
                        for c in range(KD):
                            nc.tensor.matmul(psL[j][:, 0:NE], xT[:, j, c], W[:, c], start=(c == 0), stop=False)
                        nc.tensor.matmul(psL[j][:, 0:NE], k.onesf[0:1, :], b1[:], start=False, stop=True).then_inc(prods, 1)


def moe_experts(nc, k, table, slots, tile_bin, tb_dram, ln_g, ln_b, W1, b1, W2, b2, Y):
    with Phase(nc, "me") as ph:
        W1s = ph.sb("W1", [P, NE, KD, HID])
        W2s = ph.sb("W2", [P, NE, KH, D])
        g8 = ph.sb("g8", [P, KD, NE])
        b8 = ph.sb("b8", [P, KD, NE])
        bsel = ph.sb("bsel", [P, NE, KD, NE])
        b1s = ph.sb("b1s", [NE, HID])
        b2s = ph.sb("b2s", [NE, D])
        oht = ph.sb("oht", [NE, MT])
        oh = ph.sb("oh", [NE, 2, P])
        tbi = ph.sb("tbi", [NE, MT], I32)
        idx = ph.sb("idx", [P, 2], I32)
        XG = ph.sb("XG", [P, 2, D])
        xT = ph.sb("xT", [P, KD, P])
        Hs = ph.sb("H", [P, HID])
        HT = ph.sb("HT", [P, KH, P])
        Ys = ph.sb("Ys", [P, 2, D])
        NHB = HID // BANK
        HPB = BANK // P
        psX = ph.ps("X")
        psH = [ph.ps(f"H{j}") for j in range(2 * NHB)]
        psT = [ph.ps(f"T{j}") for j in range(2)]
        psY = ph.ps("Y")
        loaded, step, small = ph.sem("loaded"), ph.sem("step"), ph.sem("small")
        ready, biased, b1done = ph.sem("ready"), ph.sem("biased"), ph.sem("b1done")
        with ph.block() as block:
            @block.sync
            def _(sp):
                for a, t in ((ln_g, g8), (ln_b, b8)):
                    for c in range(KD):
                        with nc.allow_non_contiguous_dma(reason="8 x 256 values to columns"):
                            sp.dma_start(t[:, c, :], a[:, c * P:(c + 1) * P].rearrange("e p -> p e")).then_inc(small, 16)
                sp.dma_start(b1s[:], b1).then_inc(small, 16)
                sp.dma_start(b2s[:], b2).then_inc(small, 16)
                sp.dma_start(tbi[:], tb_dram[0:MT].unsqueeze(0).broadcast_to([NE, MT])).then_inc(small, 16)
                for e in range(NE):
                    sp.dma_start(W1s[:, e], W1[e].rearrange("(k p) h -> p k h", p=P)).then_inc(loaded, 16)
                for e in range(NE):
                    sp.dma_start(W2s[:, e], W2[e].rearrange("(k p) d -> p k d", p=P)).then_inc(loaded, 16)
                sp.wait_ge(loaded, 32 * NE)

            @block.vector
            def _(dve):
                ch = Chain(dve, step)
                ch.mark(nc.vector.memset(bsel[:], 0.0))
                dve.wait_ge(small, 16 * (2 * KD + 3))
                ch(nc.vector.tensor_copy(oht[:], tbi[:]))
                ch.mark(nc.vector.tensor_scalar(oht[:], oht[:], k.part[0:NE, 0:1], None, ALU.is_equal))
                for e in range(NE):
                    ch.mark(nc.vector.tensor_copy(bsel[:, e, :, e], b8[:, :, e]))
                ch.wait()
                dve.sem_inc(ready, 1)
                dve.wait_ge(biased, 1)
                for e in range(NE):
                    for c in range(KD):
                        ch.mark(nc.vector.tensor_scalar_mul(W1s[:, e, c], W1s[:, e, c], g8[:, c, e:e + 1]))
                for n in range(NHB):
                    ch.mark(nc.vector.tensor_tensor(b1s[:, n * BANK:(n + 1) * BANK], psH[n][0:NE, :],
                                                    b1s[:, n * BANK:(n + 1) * BANK], ALU.add))
                ch.wait()

            @block.tensor
            def _(pe):
                pe.wait_ge(ready, 1)
                pe.wait_ge(loaded, 32 * NE)
                for n in range(NHB):
                    for e in range(NE):
                        for c in range(KD):
                            last = nc.tensor.matmul(psH[n][0:NE, :], bsel[:, e, c], W1s[:, e, c, n * BANK:(n + 1) * BANK],
                                                    start=(e == 0 and c == 0), stop=(e == NE - 1 and c == KD - 1))
                last.then_inc(biased, 1)

        prepped, turns, chosen = ph.sem("prepped"), ph.sem("turns"), ph.sem("chosen")
        got, before = ph.indirect(k, MT // 2)
        transx, xcopied, hid, act_s, transh, hcopied = (ph.sem("transx"), ph.sem("xcopied"), ph.sem("hid"), ph.sem("gelu"),
                                                        ph.sem("transh"), ph.sem("hcopied"))
        outs, taken = ph.sem("outs"), ph.sem("taken")
        sent = [ph.sem("sent0"), ph.sem("sent1")]
        R = MT // 2
        with ph.block() as block:
            @block.scalar
            def _(act):
                def rows(t, j, first=False):
                    if not first:
                        act.wait_ge(transx, t - 1)
                    nc.scalar.copy(idx[:, j:j + 1], slots[:, bass.ds(t, 1)]).then_inc(prepped, 1)

                def one_hot(t, j, first=False):
                    if not first:
                        act.wait_ge(outs, t - 1)
                    nc.scalar.copy(oh[:, j], oht[:, bass.ds(t, 1)].broadcast_to([NE, P])).then_inc(chosen, 1)

                def gelus(t, j):
                    act.wait_ge(hid, t + 1)
                    act.wait_ge(transh, 2 * t + 2)
                    for n in range(NHB):
                        nc.scalar.activation(Hs[:, n * BANK:(n + 1) * BANK], psH[2 * j + n][:], ACT.Gelu).then_inc(act_s, 1)

                for j in range(2):
                    rows(j, j, True)
                    one_hot(j, j, True)
                gelus(0, 0)
                with act.Fori(1, R) as i:
                    for j in range(2):
                        rows(2 * i + j, j)
                        gelus(2 * i + j - 1, 1 - j)
                        one_hot(2 * i + j, j)
                gelus(MT - 1, 1)

            @block.gpsimd
            def _(pool):
                def gather(t, j, first=False):
                    pool.wait_ge(prepped, t + 1)
                    pool.sem_inc(turns)
                    nc.gpsimd.indirect_dma_start(out=XG[:, j], out_offset=None, in_=table[:, :],
                                                 in_offset=bass.IndirectOffsetOnAxis(ap=idx[:, j:j + 1], axis=0)).then_inc(got[j], 16)
                with pool.Fori(0, R) as i:
                    for j in range(2):
                        gather(2 * i + j, j)

            @block.tensor
            def _(pe):
                pe.sem_inc(transh, 2)

                def up(t, j, i):
                    pe.wait_ge(got[j], before + 16 * i + 16)
                    for c in range(KD):
                        last = nc.tensor.transpose(psX[:, c * P:(c + 1) * P], XG[:, j, c * P:(c + 1) * P], k.ident[:])
                    last.then_inc(transx, 1)
                    e = pe.value_load(tile_bin[0:1, bass.ds(t, 1)], min_val=0, max_val=NE - 1)
                    pe.wait_ge(xcopied, t + 1)
                    for n in range(NHB):
                        for c in range(KD):
                            nc.tensor.matmul(psH[2 * j + n][:], xT[:, c],
                                             W1s[:, bass.ds(e, 1), c, n * BANK:(n + 1) * BANK].rearrange("p a h -> p (a h)"),
                                             start=(c == 0), stop=False)
                        if n == 0:
                            pe.wait_ge(chosen, t + 1)
                        last = nc.tensor.matmul(psH[2 * j + n][:], oh[:, j], b1s[:, n * BANK:(n + 1) * BANK], start=False, stop=True)
                    last.then_inc(hid, 1)

                def down(t, j):
                    for n in range(NHB):
                        pe.wait_ge(act_s, 2 * t + n + 1)
                        pe.wait_ge(hcopied, 2 * t + n + 1)
                        for c in range(HPB):
                            last = nc.tensor.transpose(psT[n][:, c * P:(c + 1) * P],
                                                       Hs[:, n * BANK + c * P:n * BANK + (c + 1) * P], k.ident[:])
                        last.then_inc(transh, 1)
                    e = pe.value_load(tile_bin[0:1, bass.ds(t, 1)], min_val=0, max_val=NE - 1)
                    pe.wait_ge(taken, t + 1)
                    nc.tensor.matmul(psY[:, 0:D], oh[:, j], b2s[:], start=True, stop=False)
                    for n in range(NHB):
                        pe.wait_ge(hcopied, 2 * t + n + 3)
                        for c in range(HPB):
                            q = n * HPB + c
                            last = nc.tensor.matmul(psY[:, 0:D], HT[:, q], W2s[:, bass.ds(e, 1), q].rearrange("p a d -> p (a d)"),
                                                    start=False, stop=(q == KH - 1))
                    last.then_inc(outs, 1)

                up(0, 0, 0)
                with pe.Fori(0, R - 1) as i:
                    up(2 * i + 1, 1, i)
                    down(2 * i, 0)
                    up(2 * i + 2, 0, i + 1)
                    down(2 * i + 1, 1)
                up(MT - 1, 1, R - 1)
                down(MT - 2, 0)
                down(MT - 1, 1)

            @block.vector
            def _(dve):
                dve.sem_inc(hcopied, 2)
                dve.sem_inc(taken, 1)

                def xcopy(t):
                    dve.wait_ge(transx, t + 1)
                    nc.vector.tensor_copy(xT[:], psX[:, 0:D].rearrange("p (c n) -> p c n", c=KD)).then_inc(xcopied, 1)

                def finish(t, j, i, first=False):
                    for n in range(NHB):
                        dve.wait_ge(transh, 2 + 2 * t + n + 1)
                        nc.vector.tensor_copy(HT[:, n * HPB:(n + 1) * HPB], psT[n][:].rearrange("p (c n) -> p c n", c=HPB)).then_inc(hcopied, 1)
                    dve.wait_ge(outs, t + 1)
                    if not first:
                        dve.wait_ge(sent[j], 16 * i)
                    nc.vector.tensor_copy(Ys[:, j], psY[:, 0:D]).then_inc(taken, 1)

                xcopy(0)
                dve.wait_ge(hid, 1)
                xcopy(1)
                finish(0, 0, 0, True)
                dve.wait_ge(hid, 2)
                xcopy(2)
                finish(1, 1, 0, True)
                with dve.Fori(1, R - 1) as i:
                    dve.wait_ge(hid, 2 * i + 1)
                    xcopy(2 * i + 1)
                    finish(2 * i, 0, i)
                    dve.wait_ge(hid, 2 * i + 2)
                    xcopy(2 * i + 2)
                    finish(2 * i + 1, 1, i)
                dve.wait_ge(hid, MT - 1)
                xcopy(MT - 1)
                finish(MT - 2, 0, R - 1)
                finish(MT - 1, 1, R - 1)

            @block.sync
            def _(sp):
                with sp.Fori(0, R) as i:
                    for j in range(2):
                        sp.wait_ge(taken, 2 * i + j + 2)
                        sp.dma_start(Y[bass.ds((2 * i + j) * P, P), :], Ys[:, j]).then_inc(sent[j], 16)
                for j in range(2):
                    sp.wait_ge(sent[j], 16 * R)


def moe_combine(nc, k, X, Y, where, weight):
    with Phase(nc, "mc") as ph:
        G = ph.sb("G", [P, 2, TOPK, D])
        T = ph.sb("T", [P, 2, TOPK, D])
        idx = ph.sb("idx", [P, 2, TOPK], I32)
        prepped, turns, weighed, first, added = ph.sem("prepped"), ph.sem("turns"), ph.sem("weighed"), ph.sem("first"), ph.sem("added")
        got, before = ph.indirect(k, NB // 2 * TOPK)
        with ph.block() as block:
            @block.scalar
            def _(act):
                def prep(b, j, first=False):
                    if not first:
                        act.wait_ge(weighed, 2 * b - 2)
                    nc.scalar.copy(idx[:, j], where[:, :, bass.ds(b, 1)].rearrange("p k a -> p (k a)")).then_inc(prepped, 1)
                prep(0, 0, True)
                prep(1, 1, True)
                with act.Fori(1, NB // 2) as i:
                    prep(2 * i, 0)
                    prep(2 * i + 1, 1)

            @block.gpsimd
            def _(pool):
                with pool.Fori(0, NB // 2) as i:
                    for j in range(2):
                        pool.wait_ge(prepped, 2 * i + j + 1)
                        pool.sem_inc(turns)
                        for c in range(TOPK):
                            nc.gpsimd.indirect_dma_start(out=G[:, j, c], out_offset=None, in_=Y[:, :],
                                                         in_offset=bass.IndirectOffsetOnAxis(ap=idx[:, j, c:c + 1], axis=0)).then_inc(got[j], 16)

            @block.vector
            def _(dve):
                with dve.Fori(0, NB // 2) as i:
                    for j in range(2):
                        b = 2 * i + j
                        dve.wait_ge(got[j], before + (i + 1) * (16 * TOPK))
                        for c in range(TOPK):
                            nc.vector.tensor_scalar_mul(T[:, j, c], G[:, j, c], weight[:, c, bass.ds(b, 1)]).then_inc(weighed, 1)
                        dve.wait_ge(weighed, 2 * b + 2)
                        nc.vector.tensor_tensor(T[:, j, 0], T[:, j, 0], T[:, j, 1], ALU.add).then_inc(first, 1)
                        dve.wait_ge(first, b + 1)
                        nc.vector.tensor_tensor(X[:, bass.ds(b, 1)], X[:, bass.ds(b, 1)], T[:, j, 0].unsqueeze(1), ALU.add).then_inc(added, 1)


def moe_layer(nc, k, X, Wr, br, ln_g, ln_b, W1, b1, W2, b2):
    table = nc.dram_tensor("moe_table", [NP, D], F32, kind="Internal").ap()
    Y = nc.dram_tensor("moe_out", [MT * P, D], F32, kind="Internal").ap()
    records = nc.dram_tensor("moe_records", [P * MT, 1], F32, kind="Internal").ap()
    with Phase(nc, "moe") as ph:
        expert, weight = ph.sb("expert", [P, TOPK, NB]), ph.sb("weight", [P, TOPK, NB])
        where = ph.sb("where", [P, TOPK, NB], I32)
        tbk = ph.sb("tbk", [1, MT], I32)
        slots = ph.sb("slots", [P, MT])
        moe_route(nc, k, X, Wr, br, table, expert, weight)
        with Phase(nc, "mob") as pb:
            G = 10
            bins = pb.sb("bins", [P, MC + G])
            tb_dram = sort_items(nc, k, "ms", bins, ItemPrep(nc, k, expert), MC, G, NE, MT, MT, 5, 1, records,
                                 pos_out=where[:].rearrange("p k b -> p (k b)"), tile_bin=tbk)
            loaded = pb.sem("loaded")
            with pb.block() as block:
                @block.sync
                def _(sp):
                    sp.dma_start(slots[:], records.rearrange("(p t) r -> p (t r)", p=P)).then_inc(loaded, 16)
                    sp.wait_ge(loaded, 16)
        moe_experts(nc, k, table, slots, tbk, tb_dram, ln_g, ln_b, W1, b1, W2, b2, Y)
        moe_combine(nc, k, X, Y, where, weight)


HOPS = 3


def hop_transform(nc, k, hop, X, H, agg, table, WnT, WsT, bn, bs):
    last_hop = hop == HOPS - 1
    with Phase(nc, f"ht{hop}") as ph:
        W = ph.sb("W", [P, 2 * KD, D])
        b = ph.sb("b", [1, 2, D])
        xs = ph.sb("xs", [P, 2, 2, D])
        xT = ph.sb("xT", [P, 2, 2 * KD, P])
        neg = ph.sb("neg", [P, 2, D])
        pos = ph.sb("pos", [P, 2, D])
        ex = ph.sb("ex", [P, 2, D])
        psT = [ph.ps(f"T{j}") for j in range(2)]
        psO = [ph.ps(f"O{j}") for j in range(2)]
        loaded, biased, ringed, trans, copied, prods = (ph.sem("loaded"), ph.sem("biased"), ph.sem("ringed"), ph.sem("trans"),
                                                        ph.sem("copied"), ph.sem("prods"))
        split, exped, done, stored = ph.sem("split"), ph.sem("exped"), ph.sem("done"), ph.sem("stored")
        with ph.block() as block:
            @block.sync
            def _(sp):
                sp.dma_start(W[:, 0:KD], WnT[hop].rearrange("(k p) n -> p k n", p=P)).then_inc(loaded, 16)
                sp.dma_start(W[:, KD:2 * KD], WsT[hop].rearrange("(k p) n -> p k n", p=P)).then_inc(loaded, 16)
                sp.dma_start(b[:, 0], bn[hop:hop + 1, :]).then_inc(loaded, 16)
                sp.dma_start(b[:, 1], bs[hop:hop + 1, :]).then_inc(loaded, 16)
                if not last_hop:
                    sp.wait_ge(done, NB)
                    sp.dma_start(table.rearrange("(b p) d -> p b d", p=P), H[:]).then_inc(stored, 16)
                    sp.wait_ge(stored, 16)

            @block.scalar
            def _(act):
                def ring(n, j, first=False):
                    if not first:
                        act.wait_ge(trans, n - 1)
                    nc.scalar.copy(xs[:, j, 0].unsqueeze(1), agg[:, bass.ds(n, 1)]).then_inc(ringed, 1)
                    nc.scalar.copy(xs[:, j, 1].unsqueeze(1), H[:, bass.ds(n, 1)]).then_inc(ringed, 1)

                def turned(n, j, first=False):
                    act.wait_ge(trans, n + 1)
                    if not first:
                        act.wait_ge(prods, n - 1)
                    nc.scalar.copy(xT[:, j], psT[j][:].rearrange("p (c n) -> p c n", c=2 * KD)).then_inc(copied, 1)

                def exps(n, j):
                    if not last_hop:
                        act.wait_ge(split, 2 * n + 2)
                        nc.scalar.activation(ex[:, j], neg[:, j], ACT.Exp).then_inc(exped, 1)

                ring(0, 0, True)
                ring(1, 1, True)
                turned(0, 0, True)
                turned(1, 1, True)
                with act.Fori(1, NB // 2) as i:
                    ring(2 * i, 0)
                    ring(2 * i + 1, 1)
                    exps(2 * i - 2, 0)
                    turned(2 * i, 0)
                    exps(2 * i - 1, 1)
                    turned(2 * i + 1, 1)
                exps(NB - 2, 0)
                exps(NB - 1, 1)

            @block.tensor
            def _(pe):
                pe.wait_ge(biased, 1)

                def turn(n, j, first=False):
                    pe.wait_ge(ringed, 2 * n + 2)
                    if not first:
                        pe.wait_ge(copied, n - 1)
                    for c in range(2 * KD):
                        last = nc.tensor.transpose(psT[j][:, c * P:(c + 1) * P], xs[:, j, c // KD, c % KD * P:(c % KD + 1) * P], k.ident[:])
                    last.then_inc(trans, 1)

                def product(n, j, first=False):
                    pe.wait_ge(copied, n + 1)
                    if not first:
                        pe.wait_ge(done, n - 1)
                    for c in range(2 * KD):
                        nc.tensor.matmul(psO[j][:, 0:D], xT[:, j, c], W[:, c], start=(c == 0), stop=False)
                    nc.tensor.matmul(psO[j][:, 0:D], k.onesf[0:1, :], b[:, 0], start=False, stop=True).then_inc(prods, 1)

                turn(0, 0, True)
                turn(1, 1, True)
                product(0, 0, True)
                product(1, 1, True)
                with pe.Fori(1, NB // 2) as i:
                    turn(2 * i, 0)
                    turn(2 * i + 1, 1)
                    product(2 * i, 0)
                    product(2 * i + 1, 1)

            @block.vector
            def _(dve):
                dve.wait_ge(loaded, 64)
                nc.vector.tensor_tensor(b[:, 0], b[:, 0], b[:, 1], ALU.add).then_inc(biased, 1)
                with dve.Fori(0, NB // 2) as i:
                    for j in range(2):
                        n = 2 * i + j
                        dve.wait_ge(prods, n + 1)
                        z = psO[j][:, 0:D]
                        if last_hop:
                            nc.vector.tensor_tensor(X[:, bass.ds(n, 1)], X[:, bass.ds(n, 1)], z.unsqueeze(1), ALU.add).then_inc(done, 1)
                            continue
                        nc.vector.tensor_scalar_min(neg[:, j], z, 0.0).then_inc(split, 1)
                        nc.vector.tensor_scalar_max(pos[:, j], z, 0.0).then_inc(split, 1)
                        dve.wait_ge(exped, n + 1)
                        nc.vector.scalar_tensor_tensor(H[:, bass.ds(n, 1)], ex[:, j].unsqueeze(1), -1.0, pos[:, j].unsqueeze(1),
                                                       ALU.add, ALU.add).then_inc(done, 1)


def gnn_layer(nc, k, X, src, dst, weight, WnT, bn, WsT, bs):
    table = nc.dram_tensor("hop_table", [NP, D], F32, kind="Internal").ap()
    with Phase(nc, "gnn") as ph:
        SRT, tbk = ph.sb("SRT", [P, EROW, 4]), ph.sb("tbk", [1, EROW], I32)
        sort_edges(nc, k, "ss", src, dst, weight, SRT, tbk)
        H, agg = ph.sb("H", [P, NB, D]), ph.sb("agg", [P, NB, D])
        with Phase(nc, "gn") as pn:
            norm = RowNorm(nc, pn, X)
            step, stored = pn.sem("step"), pn.sem("stored")
            with pn.block() as block:
                @block.scalar
                def _(act):
                    norm.root(act)

                @block.vector
                def _(dve):
                    norm.all(dve, Chain(dve, step), H)

                @block.sync
                def _(sp):
                    sp.wait_ge(step, 3 * NB + 1)
                    sp.dma_start(table.rearrange("(b p) d -> p b d", p=P), H[:]).then_inc(stored, 16)
                    sp.wait_ge(stored, 16)
        for hop in range(HOPS):
            propagate(nc, k, hop, table, SRT, tbk, agg)
            hop_transform(nc, k, hop, X, H, agg, table, WnT, WsT, bn, bs)


HALF = 25
BODY = 2 * HALF
assert N % BODY == 0
FP16_TOP = 14
TAILS = [(FULL * P, min(P, TAIL + HALF))] + ([(FULL * P + P, TAIL + HALF - P)] if TAIL + HALF > P else [])
GATES = "igo"
M6 = len(GATES) * KD
ROWS = [g + str(m) for g in GATES for m in range(KD)]
PLACE = {"i0": (0, 0), "g0": (0, 1), "i1": (1, 0), "g1": (1, 1), "o0": (2, 0), "o1": (3, 0)}
BANKS = 4


def terms(rows, parts, q):
    return [(row, part, q) for row in rows.split() for part in parts.split()]


ORDER = (terms("i0 g0 i1 g1", "11 21", 0) + terms("i0 g0 i1", "11 21", 1)
         + [t for q in range(KD) for t in terms("i0 g0", "12", q)]
         + terms("g1", "11 21", 1) + [t for q in range(KD) for t in terms("i1 g1", "12", q)]
         + [t for row in ("o0", "o1") for q in range(KD) for t in terms(row, "11 21 12", q)])
assert len(ORDER) == len(set(ORDER)) == 3 * KD * M6


def lstm_layer(nc, k, X, U, V, b):
    with Phase(nc, "ls") as ph:
        XT1 = ph.sb("XT1", [P, KD, N + HALF], F16)
        XT2 = ph.sb("XT2", [P, KD, N + HALF], F16)
        HT = ph.sb("HT", [P, NP, KD])
        U1, U2 = (ph.sb(n, [P, KD, M6, P], F16) for n in ("U1", "U2"))
        V1, V2 = (ph.sb(n, [P, KD, M6, P], F16) for n in ("V1", "V2"))
        b1, b2 = (ph.sb(n, [1, M6, P], F16) for n in ("b1", "b2"))
        ones = ph.sb("ones", [1, HALF], F16)
        sc = ph.sb("sc", [P, 2], I32)
        h = ph.sb("h", [P, BODY, KD])
        h1 = ph.sb("h1", [P, BODY, KD], F16)
        h2 = ph.sb("h2", [P, BODY, KD], F16)
        c = ph.sb("c", [P, 2, KD])
        S = ph.sb("S", [P, 2, M6])
        hc = ph.sb("hc", [P, KD])
        th = ph.sb("th", [P, 2, KD])

        with Phase(nc, "lp") as pp:
            Us, Vs = (pp.sb(n, [P, KD, M6, P]) for n in ("U", "V"))
            brow = pp.sb("brow", [1, M6, P])
            mx = pp.sb("mx", [P, 2, 2])
            big = pp.sb("big", [P, 2])
            top = pp.sb("top", [P, 1])
            ex = pp.sb("ex", [P, 2], I32)
            norm = RowNorm(nc, pp, X)
            xs = pp.sb("xs", [P, 2, 1, D])
            xT = pp.sb("xT", [P, 2, KD, P])
            psT = [pp.ps(f"T{j}") for j in range(2)]
            step, normed, trans, loaded = pp.sem("step"), pp.sem("normed"), pp.sem("trans"), pp.sem("loaded")
            copied, high, low, reduced = pp.sem("copied"), pp.sem("high"), pp.sem("low"), pp.sem("reduced")
            scale = sc[:, 0:1].bitcast(F32)
            with pp.block() as block:
                @block.sync
                def _(sp):
                    sp.dma_start(Us[:], U.rearrange("(k p) (m c) -> p k m c", k=KD, c=P)).then_inc(loaded, 16)
                    sp.dma_start(Vs[:], V.rearrange("(k p) (m c) -> p k m c", k=KD, c=P)).then_inc(loaded, 16)
                    sp.dma_start(brow[:], b.rearrange("(a m c) -> a m c", a=1, c=P)).then_inc(loaded, 16)

                @block.vector
                def _(dve):
                    ch = Chain(dve, step)
                    norm.stats(dve, ch)
                    norm.apply(xs[:, 0], 0).then_inc(normed, 1)
                    norm.apply(xs[:, 1], 1).then_inc(normed, 1)

                    def split_block(n, j, cols, count):
                        dve.wait_ge(high, n + 1)
                        nc.vector.tensor_tensor(XT2[:, :, cols], xT[:, j, :, 0:count], XT1[:, :, cols], ALU.subtract).then_inc(low, 1)

                    with dve.Fori(1, FULL // 2) as i:
                        for j in range(2):
                            n = 2 * i + j
                            dve.wait_ge(trans, n - 1)
                            norm.apply(xs[:, j], n).then_inc(normed, 1)
                            split_block(n - 2, j, bass.ds((n - 2) * P, P), P)
                    for j in range(2):
                        dve.wait_ge(trans, FULL + j - 1)
                        norm.apply(xs[:, j], FULL + j).then_inc(normed, 1)
                        split_block(FULL - 2 + j, j, slice((FULL - 2 + j) * P, (FULL - 1 + j) * P), P)
                    for j, (c0, count) in enumerate(TAILS):
                        split_block(FULL + j, j, slice(c0, c0 + count), count)
                    dve.wait_ge(loaded, 48)
                    ch(nc.vector.memset(mx[:], 0.0))
                    for j, w in enumerate((Us, Vs)):
                        v = w[:].rearrange("p k m c -> p (k m c)")
                        ch.mark(nc.vector.tensor_reduce(mx[:, 0, j:j + 1], v, AXX, ALU.max))
                        ch(nc.vector.tensor_reduce(mx[:, 1, j:j + 1], v, AXX, ALU.min))
                    ch(nc.vector.scalar_tensor_tensor(mx[:, 0], mx[:, 1], -1.0, mx[:, 0], ALU.mult, ALU.max))
                    ch(nc.vector.reduce_max(big[:, 0:1], mx[:, 0], AXX))
                    v = brow[:].rearrange("p m c -> p (m c)")
                    ch.mark(nc.vector.tensor_reduce(mx[0:1, 0, 0:1], v, AXX, ALU.max))
                    ch(nc.vector.tensor_reduce(mx[0:1, 1, 0:1], v, AXX, ALU.min))
                    ch(nc.vector.scalar_tensor_tensor(mx[0:1, 0, 0:1], mx[0:1, 1, 0:1], -1.0, mx[0:1, 0, 0:1], ALU.mult, ALU.max))
                    ch(nc.vector.tensor_tensor(big[0:1, 0:1], big[0:1, 0:1], mx[0:1, 0, 0:1], ALU.max))
                    nc.vector.tensor_scalar_max(big[:, 1:2], big[:, 0:1], 2.0 ** -60).then_inc(reduced, 1)
                    dve.wait_ge(reduced, 2)
                    ch(nc.vector.tensor_scalar(ex[:, 0:1], top[:].bitcast(I32), 23, None, ALU.logical_shift_right))
                    ch(nc.vector.tensor_scalar(ex[:, 1:2], ex[:, 0:1], -1.0, 254.0 + FP16_TOP, ALU.mult, ALU.add))
                    ch(nc.vector.tensor_scalar(ex[:, 0:1], ex[:, 1:2], -1.0, 254.0, ALU.mult, ALU.add))
                    ch.mark(nc.vector.tensor_scalar(sc[:, 0:1], ex[:, 1:2], 23, None, ALU.logical_shift_left))
                    ch(nc.vector.tensor_scalar(sc[:, 1:2], ex[:, 0:1], 23, None, ALU.logical_shift_left))
                    parts = ((Us, U1, U2, scale), (Vs, V1, V2, scale), (brow, b1, b2, sc[0:1, 0:1].bitcast(F32)))
                    for w, w1, w2, by in parts:
                        ch.mark(nc.vector.tensor_scalar_mul(w[:], w[:], by))
                    ch.wait()
                    for w, w1, w2, by in parts:
                        ch.mark(nc.vector.tensor_copy(w1[:], w[:]))
                    ch.wait()
                    for w, w1, w2, by in parts:
                        ch.mark(nc.vector.tensor_tensor(w2[:], w[:], w1[:], ALU.subtract))
                    ch.wait()

                @block.gpsimd
                def _(pool):
                    nc.gpsimd.memset(HT[:, N:NP, :], 0.0)
                    nc.gpsimd.memset(ones[:], 1.0)
                    pool.wait_ge(reduced, 1)
                    nc.gpsimd.partition_all_reduce(top[:], big[:, 1:2], P, bass.bass_isa.ReduceOp.max).then_inc(reduced, 1)

                @block.tensor
                def _(pe):
                    def turn(n, j, first=False):
                        pe.wait_ge(normed, n + 1)
                        if not first:
                            pe.wait_ge(high, n - 1)
                        for q in range(KD):
                            last = nc.tensor.transpose(psT[j][:, q * P:(q + 1) * P], xs[:, j, 0, q * P:(q + 1) * P], k.ident[:])
                        last.then_inc(trans, 1)
                    turn(0, 0, True)
                    turn(1, 1, True)
                    with pe.Fori(1, NB // 2) as i:
                        turn(2 * i, 0)
                        turn(2 * i + 1, 1)

                @block.scalar
                def _(act):
                    norm.root(act)

                    def take(n, j, cols, count, first=False):
                        act.wait_ge(trans, n + 1)
                        if not first:
                            act.wait_ge(low, n - 1)
                        src = psT[j][:, 0:D].rearrange("p (c n) -> p c n", c=KD)[:, :, 0:count]
                        nc.scalar.copy(xT[:, j, :, 0:count], src)
                        nc.scalar.copy(XT1[:, :, cols], src).then_inc(high, 1)

                    take(0, 0, slice(0, P), P, True)
                    take(1, 1, slice(P, 2 * P), P, True)
                    with act.Fori(1, FULL // 2) as i:
                        for j in range(2):
                            take(2 * i + j, j, bass.ds((2 * i + j) * P, P), P)
                    for j, (c0, count) in enumerate(TAILS):
                        take(FULL + j, j, slice(c0, c0 + count), count)

        with Phase(nc, "lr") as pr:
            Z = [[pr.ps(f"Z{i}{g}") for g in range(BANKS)] for i in range(2)]
            z = [pr.sem(f"z{g}") for g in range(BANKS)]
            gates, cell, tanh_made, h1_made = ([pr.sem(f"{n}{j}") for j in range(KD)] for n in ("gates", "cell", "tanh", "h1_"))
            h_made, h2_made, hc_made, kept = (pr.sem(n) for n in ("h", "h2", "hc", "kept"))
            with pr.block() as block:
                @block.gpsimd
                def _(pool):
                    pool.sem_inc(kept, 2)
                    with pool.Fori(0, N // BODY) as i:
                        for hf in range(2):
                            pool.wait_ge(h_made, i * BODY + HALF * (hf + 1))
                            nc.gpsimd.tensor_copy(HT[:, bass.ds(i * BODY + hf * HALF, HALF), :],
                                                  h[:, hf * HALF:(hf + 1) * HALF, :]).then_inc(kept, 1)

                @block.tensor
                def _(pe):
                    AHEAD = [(row, kk, part) for row in sorted(ROWS, key=lambda r: PLACE[r][1]) for kk in range(KD + 1)
                             for part in (("1", "2") if kk == 0 else ("11", "21", "12"))]
                    PER = -(-len(AHEAD) // HALF)

                    def ahead(a, t0, hf):
                        row, kk, part = AHEAD[a]
                        bank, col = PLACE[row]
                        m = ROWS.index(row)
                        o = Z[hf][bank][:, 0:KD * HALF].rearrange("p (t m) -> p t m", m=KD)[:, :, col]
                        opens = kk == 0 and part == "1" and col == 0
                        if kk == 0:
                            w, x = (b1 if part == "1" else b2)[:, m, :], ones[:]
                        else:
                            w = (U2 if part == "21" else U1)[:, kk - 1, m, :]
                            x = (XT2 if part == "12" else XT1)[:, kk - 1, bass.ds(t0, HALF)]
                        nc.tensor.matmul(o, w, x, start=opens, stop=False, skip_group_check=True)

                    for a in range(len(AHEAD)):
                        ahead(a, 0, 0)
                    with pe.Fori(0, N // BODY) as i:
                        for s in range(BODY):
                            hf, prev = s // HALF, (s - 1) % BODY
                            waited = []
                            for n, (row, part, q) in enumerate(ORDER):
                                bank, col = PLACE[row]
                                col += s % HALF * KD
                                hx, made = (h2, h2_made) if part == "12" else (h1, h1_made[q])
                                if (part == "12", q) not in waited:
                                    pe.wait_ge(made, i * BODY + s + 1)
                                    waited.append(made)
                                ends = all(PLACE[r][0] != bank for r, _, _ in ORDER[n + 1:])
                                mm = nc.tensor.matmul(Z[hf][bank][:, col:col + 1], (V2 if part == "21" else V1)[:, q, ROWS.index(row), :],
                                                      hx[:, prev, q:q + 1], start=False, stop=ends, skip_group_check=True)
                                if ends:
                                    mm.then_inc(z[bank], 1)
                            for a in range(s % HALF * PER, min(len(AHEAD), (s % HALF + 1) * PER)):
                                ahead(a, i * BODY + HALF * (hf + 1), 1 - hf)

                @block.scalar
                def _(act):
                    back = act.alloc_register("unscale")
                    act.reg_load(back, sc[0:1, 1:2])
                    with act.Fori(0, N // BODY) as i:
                        for s in range(BODY):
                            hf, col, t = s // HALF, s % HALF * KD, i * BODY + s
                            for m in range(KD):
                                act.wait_ge(z[m], t + 1)
                                nc.scalar.activation(S[:, s % 2, m:m + 1], Z[hf][m][:, col:col + 1], ACT.Sigmoid, scale=back)
                                nc.scalar.activation(S[:, s % 2, KD + m:KD + m + 1], Z[hf][m][:, col + 1:col + 2], ACT.Tanh,
                                                     scale=back).then_inc(gates[m], 1)
                            for m in range(KD):
                                act.wait_ge(z[2 + m], t + 1)
                                nc.scalar.activation(S[:, s % 2, 2 * KD + m:2 * KD + m + 1], Z[hf][2 + m][:, col:col + 1], ACT.Sigmoid, scale=back)
                            for m in range(KD):
                                act.wait_ge(cell[m], t + 1)
                                nc.scalar.activation(th[:, s % 2, m:m + 1], c[:, s % 2, m:m + 1], ACT.Tanh).then_inc(tanh_made[m], 1)

                @block.vector
                def _(dve):
                    for m in range(KD):
                        nc.vector.memset(h1[:, BODY - 1, m:m + 1], 0.0).then_inc(h1_made[m], 1)
                    nc.vector.memset(h2[:, BODY - 1, :], 0.0).then_inc(h2_made, 1)
                    nc.vector.memset(hc[:], 0.0).then_inc(hc_made, 1)
                    with dve.Fori(0, N // BODY) as i:
                        for s in range(BODY):
                            t, e = i * BODY + s, s % 2
                            for m in range(KD):
                                dve.wait_ge(gates[m], t + 1)
                                if m == 0:
                                    dve.wait_ge(hc_made, t + 1)
                                nc.vector.scalar_tensor_tensor(c[:, e, m:m + 1], S[:, e, KD + m:KD + m + 1], S[:, e, m:m + 1], hc[:, m:m + 1],
                                                               ALU.mult, ALU.add).then_inc(cell[m], 1)
                            if s % HALF == 0:
                                dve.wait_ge(kept, 2 * i + s // HALF + 1)
                            for m in range(KD):
                                dve.wait_ge(tanh_made[m], t + 1)
                                nc.vector.tensor_tensor(h1[:, s, m:m + 1], S[:, e, 2 * KD + m:2 * KD + m + 1], th[:, e, m:m + 1],
                                                        ALU.mult).then_inc(h1_made[m], 1)
                            nc.vector.tensor_tensor(h[:, s, :], S[:, e, 2 * KD:M6], th[:, e, :], ALU.mult).then_inc(h_made, 1)
                            dve.wait_ge(h_made, t + 1)
                            nc.vector.tensor_tensor(h2[:, s, :], h[:, s, :], h1[:, s, :], ALU.subtract).then_inc(h2_made, 1)
                            nc.vector.tensor_tensor(hc[:], h[:, s, :], c[:, e, :], ALU.mult).then_inc(hc_made, 1)

        with Phase(nc, "lf") as pf:
            hs = pf.sb("hs", [P, 2, KD, P])
            psT = [pf.ps(f"T{j}") for j in range(2)]
            ringed, trans, added = pf.sem("ringed"), pf.sem("trans"), pf.sem("added")
            with pf.block() as block:
                @block.scalar
                def _(act):
                    def ring(n, j, first=False):
                        if not first:
                            act.wait_ge(trans, n - 1)
                        nc.scalar.copy(hs[:, j], HT[:, bass.ds(n * P, P), :].rearrange("p t k -> p k t")).then_inc(ringed, 1)
                    ring(0, 0, True)
                    ring(1, 1, True)
                    with act.Fori(1, NB // 2) as i:
                        ring(2 * i, 0)
                        ring(2 * i + 1, 1)

                @block.tensor
                def _(pe):
                    def turn(n, j, first=False):
                        pe.wait_ge(ringed, n + 1)
                        if not first:
                            pe.wait_ge(added, n - 1)
                        for q in range(KD):
                            last = nc.tensor.transpose(psT[j][:, q * P:(q + 1) * P], hs[:, j, q], k.ident[:])
                        last.then_inc(trans, 1)
                    turn(0, 0, True)
                    turn(1, 1, True)
                    with pe.Fori(1, NB // 2) as i:
                        turn(2 * i, 0)
                        turn(2 * i + 1, 1)

                @block.vector
                def _(dve):
                    with dve.Fori(0, NB // 2) as i:
                        for j in range(2):
                            dve.wait_ge(trans, 2 * i + j + 1)
                            nc.vector.tensor_tensor(X[:, bass.ds(2 * i + j, 1)], X[:, bass.ds(2 * i + j, 1)],
                                                    psT[j][:, 0:D].unsqueeze(1), ALU.add).then_inc(added, 1)


class Constants:

    def __init__(self, nc, ph):
        self.cols = ph.sb("cols", [P, P])
        self.part = ph.sb("part", [P, 1])
        self.ident = ph.sb("ident", [P, P])
        self.ones = ph.sb("ones", [P, P], BF16)
        self.onesf = ph.sb("onesf", [P, P])
        self.before = ph.sb("before", [P, P], BF16)
        self.indirect = [ph.ctx.enter_context(nc.semaphore(f"indirect{j}")) for j in range(2)]
        self.indirect_before = 0
        constants(nc, self)


def build(nc, x, src, dst, edge_weight, gat_W_src, gat_W_dst, gat_att_src, gat_att_dst, gat_bias, gat_gamma, gat_beta,
          gat_prelu, moe_Wr, moe_br, moe_g, moe_b, moe_W1, moe_b1, moe_W2, moe_b2, gnn_WnT, gnn_bn, gnn_WsT, gnn_bs,
          lstm_U, lstm_V, lstm_b, out):
    with Phase(nc, "all") as ph:
        k = Constants(nc, ph)
        X = ph.sb("X", [P, NB, D])
        load_rows(nc, x, X)
        gat_layer(nc, k, X, src, dst, gat_W_src, gat_W_dst, gat_att_src, gat_att_dst, gat_bias, gat_gamma, gat_beta, gat_prelu)
        moe_layer(nc, k, X, moe_Wr, moe_br, moe_g, moe_b, moe_W1, moe_b1, moe_W2, moe_b2)
        gnn_layer(nc, k, X, src, dst, edge_weight, gnn_WnT, gnn_bn, gnn_WsT, gnn_bs)
        lstm_layer(nc, k, X, lstm_U, lstm_V, lstm_b)
        store_rows(nc, X, out)


def kernel(**inputs):
    import numpy as np
    import concourse.bacc as bacc
    from concourse.bass_utils import run_bass_kernel_spmd

    given = {name: np.ascontiguousarray(inputs[name]) for name in (
        "x", "src", "dst", "edge_weight", "L0_gnn_W_src", "L0_gnn_W_dst", "L0_gnn_att_src", "L0_gnn_att_dst", "L0_gnn_bias",
        "L0_gnn_ln_gamma", "L0_gnn_ln_beta", "L0_gnn_prelu_w", "L0_ffn_Wr", "L0_ffn_br", "L0_ffn_ln_g", "L0_ffn_ln_b",
        "L0_ffn_W1", "L0_ffn_b1", "L0_ffn_W2", "L0_ffn_b2")}
    given["gnn_WnT"] = np.ascontiguousarray(np.transpose(inputs["L1_gnn_Wn"], (0, 2, 1)))
    given["gnn_bn"] = np.ascontiguousarray(inputs["L1_gnn_bn"])
    given["gnn_WsT"] = np.ascontiguousarray(np.transpose(inputs["L1_gnn_Ws"], (0, 2, 1)))
    given["gnn_bs"] = np.ascontiguousarray(inputs["L1_gnn_bs"])
    for part in ("U", "V", "b"):
        given[f"lstm_{part}"] = np.concatenate([np.asarray(inputs[f"L1_ffn_{part}_{gate}"]) for gate in ("i", "c", "o")], axis=-1)

    nc = bacc.Bacc("TRN2", target_bir_lowering=False, num_devices=1)
    arrays = {f"in_{name}": a for name, a in given.items()}
    args = [nc.dram_tensor(name, a.shape, mybir.dt.from_np(a.dtype), kind="ExternalInput").ap() for name, a in arrays.items()]
    args.append(nc.dram_tensor("out_0", (N, D), F32, kind="ExternalOutput").ap())
    build(nc, *args)
    r = run_bass_kernel_spmd(nc, [arrays], core_ids=[0])
    return r.results[0]["out_0"]
```

```python
import concourse.bass as bass
from concourse import mybir
from contextlib import ExitStack

F32 = mybir.dt.float32
F16 = mybir.dt.float16
BF16 = mybir.dt.bfloat16
I32 = mybir.dt.int32
ACT = mybir.ActivationFunctionType
ALU = mybir.AluOpType
AXX = mybir.AxisListType.X

P = 128
LOGP = 7
N = 6250
D = 256
E = 100000
KD = D // P
NB = 50
NP = NB * P
FULL = N // P
TAIL = N - FULL * P
LN_EPS = 1e-5

EC = 784
ELAST = E - (P - 1) * EC
U = 7
ET = 840
EROW = ET + 3 * U
HEADS = 4
HD = D // HEADS
NEG_SLOPE = 0.2


class Chain:

    def __init__(self, eng, sem):
        self.eng, self.sem, self.base, self.n = eng, sem, 0, 0

    def at(self, base):
        self.base, self.n = base, 0

    def mark(self, ins):
        ins.then_inc(self.sem, 1)
        self.n += 1

    def wait(self):
        self.eng.wait_ge(self.sem, self.base + self.n)

    def __call__(self, ins):
        self.mark(ins)
        self.wait()


class Phase:

    def __init__(self, nc, name):
        self.nc, self.name, self.ctx, self.sems = nc, name, ExitStack(), []

    def __enter__(self):
        self.ctx.__enter__()
        return self

    def __exit__(self, *a):
        if self.sems and a[0] is None:
            with self.nc.Block() as block:
                @block.sync
                def _(sp):
                    for s in self.sems:
                        sp.sem_clear(s)
        return self.ctx.__exit__(*a)

    def sb(self, name, shape, dt=F32):
        return self.ctx.enter_context(self.nc.sbuf_tensor(f"{self.name}_{name}", shape, dt))

    def ps(self, name, shape=(P, 512), dt=F32):
        return self.ctx.enter_context(self.nc.psum_tensor(f"{self.name}_{name}", list(shape), dt))

    def sem(self, name):
        self.sems.append(self.ctx.enter_context(self.nc.semaphore(f"{self.name}_{name}")))
        return self.sems[-1]

    def indirect(self, k, count):
        before = k.indirect_before
        k.indirect_before += 16 * count
        return k.indirect, before

    def block(self):
        return self.nc.Block()


def constants(nc, k):
    with Phase(nc, "const") as ph:
        made = ph.sem("made")
        with ph.block() as block:
            @block.gpsimd
            def _(pool):
                c = Chain(pool, made)
                c(nc.gpsimd.iota(k.cols[:], [[1, P]], base=0, channel_multiplier=0, allow_small_or_imprecise_dtypes=True))
                c(nc.gpsimd.iota(k.part[:], [[0, 1]], base=0, channel_multiplier=1, allow_small_or_imprecise_dtypes=True))
                c(nc.gpsimd.memset(k.ident[:], 0.0))
                c(nc.gpsimd.affine_select(out=k.ident[:], in_=k.ident[:], compare_op=ALU.not_equal, fill=1.0,
                                          base=0, pattern=[[-1, P]], channel_multiplier=1))
                c(nc.gpsimd.memset(k.ones[:], 1.0))
                c(nc.gpsimd.memset(k.onesf[:], 1.0))
                c(nc.gpsimd.memset(k.before[:], 1.0))
                c(nc.gpsimd.affine_select(out=k.before[:], in_=k.before[:], compare_op=ALU.is_gt, fill=0.0,
                                          base=0, pattern=[[1, P]], channel_multiplier=-1))


def load_rows(nc, x, X):
    with Phase(nc, "load") as ph:
        zeroed, loaded = ph.sem("zeroed"), ph.sem("loaded")
        with ph.block() as block:
            @block.vector
            def _(dve):
                nc.vector.memset(X[:, FULL:NB, :], 0.0).then_inc(zeroed, 1)

            @block.sync
            def _(sp):
                sp.dma_start(X[:, 0:FULL, :], x[0:FULL * P, :].rearrange("(b p) d -> p b d", p=P)).then_inc(loaded, 16)
                sp.wait_ge(zeroed, 1)
                sp.dma_start(X[0:TAIL, FULL, :], x[FULL * P:N, :]).then_inc(loaded, 16)
                sp.wait_ge(loaded, 32)


def store_rows(nc, X, out):
    with Phase(nc, "store") as ph:
        stored = ph.sem("stored")
        with ph.block() as block:
            @block.sync
            def _(sp):
                sp.dma_start(out[0:FULL * P, :].rearrange("(b p) d -> p b d", p=P), X[:, 0:FULL, :]).then_inc(stored, 16)
                sp.dma_start(out[FULL * P:N, :], X[0:TAIL, FULL, :]).then_inc(stored, 16)
                sp.wait_ge(stored, 32)


ROUND = 10
assert NB % ROUND == 0


class RowNorm:

    def __init__(self, nc, ph, src, tag=""):
        self.nc, self.src = nc, src
        self.parts = ph.sb(f"parts{tag}", [P, NB, nc.vector.BN_STATS_DIM])
        self.mv = ph.sb(f"mv{tag}", [P, NB, nc.vector.BN_AGGR_DIM])
        self.rstd = ph.sb(f"rstd{tag}", [P, NB])
        self.std = ph.sb(f"std{tag}", [P, NB])
        self.var_made, self.std_made = ph.sem(f"var_made{tag}"), ph.sem(f"std_made{tag}")

    def root(self, act):
        act.wait_ge(self.var_made, 1)
        self.nc.scalar.activation(self.std[:], self.rstd[:], ACT.Sqrt).then_inc(self.std_made, 1)

    def stats(self, dve, chain):
        nc = self.nc
        with dve.Fori(0, NB // ROUND) as i:
            for j in range(ROUND):
                b = i * ROUND + j
                nc.vector.bn_stats(self.parts[:, bass.ds(b, 1), :], self.src[:, bass.ds(b, 1), :]).then_inc(chain.sem, 1)
        chain.n += NB
        chain.wait()
        for b in range(NB):
            chain.mark(nc.vector.bn_aggr(self.mv[:, b, :], self.parts[:, b, :]))
        chain.wait()
        nc.vector.tensor_scalar_add(self.rstd[:], self.mv[:, :, 1], LN_EPS).then_inc(self.var_made, 1)
        dve.wait_ge(self.std_made, 1)
        chain(nc.vector.reciprocal(self.rstd[:], self.std[:]))

    def apply(self, dst, b):
        return self.nc.vector.tensor_scalar(dst, self.src[:, bass.ds(b, 1), :], self.mv[:, bass.ds(b, 1), 0],
                                            self.rstd[:, bass.ds(b, 1)], ALU.subtract, ALU.mult)

    def all(self, dve, chain, dst):
        self.stats(dve, chain)
        with dve.Fori(0, NB // ROUND) as i:
            for j in range(ROUND):
                b = i * ROUND + j
                self.apply(dst[:, bass.ds(b, 1), :], b).then_inc(chain.sem, 1)
        chain.n += NB
        chain.wait()


def sort_items(nc, k, name, bins, prep, C, G, NBIN, TM, TROW, HU, RW, records, pos_out=None, tile_bin=None, prefill=None,
               staged=None, beside=(None, None, None)):
    NG = C // G
    with Phase(nc, name) as ph:
        rec = ph.sb("rec", [P, C, RW])
        binrow = ph.sb("binrow", [P, NBIN])
        oh = ph.sb("oh", [P, 2, G, NBIN], BF16)
        zero = ph.sb("zero", [P, G * NBIN], BF16)
        count = ph.sb("count", [P, NBIN])
        counti = ph.sb("counti", [P, NBIN], I32)
        tiles = ph.sb("tiles", [P, NBIN])
        incl = ph.sb("incl", [P, 2, NBIN])
        run = ph.sb("run", [P, 2, NBIN])
        ranks = ph.sb("ranks", [P, G, NBIN])
        picked = ph.sb("picked", [P, G, NBIN])
        pos = ph.sb("pos", [P, C])
        low, high = ph.sb("low", [P, C]), ph.sb("high", [P, C])
        lowi, highi = ph.sb("lowi", [P, C], I32), ph.sb("highi", [P, C], I32)
        place = ph.sb("place", [P, C], I32)
        TQ = -(-TM // P)
        tno = ph.sb("tno", [P, TQ])
        tcmp = ph.sb("tcmp", [P, TQ, NBIN])
        tb = ph.sb("tb", [P, TQ])
        tbi = ph.sb("tbi", [P, TQ], I32)
        ring_place = ph.sb("ring_place", [P, 2, HU], I32)
        ring_rec = ph.sb("ring_rec", [P, 2, HU, RW])
        fill = ph.sb("fill", [P, TROW, RW])
        tb_dram = nc.dram_tensor(f"{name}_tbd", [TQ * P], I32, kind="Internal").ap()
        cnt_ps = ph.ps("cnt")
        rank_ps = [ph.ps(f"rank{j}") for j in range(2)]
        tot_ps = [ph.ps(f"tot{j}") for j in range(2)]

        loaded, step = ph.sem("loaded"), ph.sem("step")
        with ph.block() as block:
            @block.sync
            def _(sp):
                prep.loads(ph, sp, loaded)

            @block.gpsimd
            def _(pool):
                nc.gpsimd.iota(tno[:], [[1, TQ]], base=0, channel_multiplier=TQ, allow_small_or_imprecise_dtypes=True)
                if beside[0] is not None:
                    beside[0](pool)

            @block.vector
            def _(dve):
                ch = Chain(dve, step)
                ch.mark(nc.vector.tensor_copy(binrow[:], k.cols[:, 0:NBIN]))
                ch.mark(nc.vector.memset(zero[:], 0.0))
                prep.compute(ph, dve, ch, loaded, bins, rec)
                ch.mark(nc.vector.memset(fill[:], 0.0))
                if prefill is not None:
                    ch.wait()
                    prefill(ch, fill)
                ch.wait()

        oh_made, counted, filled, step = ph.sem("oh_made"), ph.sem("counted"), ph.sem("filled"), ph.sem("step2")
        step3, tb_out = ph.sem("step3"), ph.sem("tb_out")
        flat = lambda a: a.rearrange("p g b -> p (g b)")

        def one_hot(g, j):
            return nc.vector.tensor_tensor(
                oh[:, j], bins[:, bass.ds(g * G, G)].unsqueeze(2).broadcast_to([P, G, NBIN]),
                binrow[:].unsqueeze(1).broadcast_to([P, G, NBIN]), ALU.is_equal)

        with ph.block() as block:
            @block.sync
            def _(sp):
                sp.dma_start(records.rearrange("(p t) r -> p t r", p=P), fill[:]).then_inc(filled, 16)
                sp.wait_ge(filled, 16)
                sp.wait_ge(step3, 1)
                sp.dma_start(tb_dram.rearrange("(p q) -> p q", p=P), tbi[:]).then_inc(tb_out, 16)
                sp.wait_ge(tb_out, 16)
                if tile_bin is not None:
                    sp.dma_start(tile_bin[0:1, 0:TM], tb_dram[0:TM].unsqueeze(0)).then_inc(tb_out, 16)
                    sp.wait_ge(tb_out, 32)

            @block.gpsimd
            def _(pool):
                if beside[1] is not None:
                    beside[1](pool)

            @block.vector
            def _(dve):
                with dve.Fori(0, NG // 2) as i:
                    for j in range(2):
                        dve.wait_ge(counted, i * 2 + j + 1)
                        one_hot(i * 2 + j, j).then_inc(oh_made, 1)
                dve.wait_ge(counted, NG + 2)
                ch = Chain(dve, step)
                ch(nc.vector.reduce_sum(count[:], cnt_ps[:, 0:G * NBIN].rearrange("p (g b) -> p b g", g=G), AXX))
                ch(nc.vector.tensor_scalar_add(count[:], count[:], float(P - 1)))
                ch(nc.vector.tensor_copy(counti[:], count[:]))
                ch(nc.vector.tensor_scalar(counti[:], counti[:], LOGP, None, ALU.logical_shift_right))
                ch(nc.vector.tensor_copy(tiles[:], counti[:]))
                ch(nc.vector.tensor_copy(incl[:, 0], tiles[:]))
                cur, s = 0, 1
                while s < NBIN:
                    ch.mark(nc.vector.tensor_copy(incl[:, 1 - cur, 0:s], incl[:, cur, 0:s]))
                    ch(nc.vector.tensor_tensor(incl[:, 1 - cur, s:NBIN], incl[:, cur, s:NBIN], incl[:, cur, 0:NBIN - s], ALU.add))
                    cur, s = 1 - cur, s * 2
                ch(nc.vector.tensor_tensor(run[:, 0], incl[:, cur], tiles[:], ALU.subtract))
                ch(nc.vector.tensor_scalar_mul(run[:, 0], run[:, 0], float(P)))
                ch(nc.vector.tensor_tensor(tcmp[:], incl[:, cur].unsqueeze(1).broadcast_to([P, TQ, NBIN]),
                                           tno[:].unsqueeze(2).broadcast_to([P, TQ, NBIN]), ALU.is_le))
                ch(nc.vector.reduce_sum(tb[:], tcmp[:], AXX))
                ch(nc.vector.tensor_scalar_min(tb[:], tb[:], float(NBIN - 1)))
                nc.vector.tensor_copy(tbi[:], tb[:]).then_inc(step3, 1)

            @block.tensor
            def _(pe):
                pe.sem_inc(counted, 2)
                nc.tensor.matmul(cnt_ps[:, 0:G * NBIN], k.ones[:], zero[:], start=True, stop=False, skip_group_check=True)
                with pe.Fori(0, NG // 2) as i:
                    for j in range(2):
                        pe.wait_ge(oh_made, i * 2 + j + 1)
                        nc.tensor.matmul(cnt_ps[:, 0:G * NBIN], k.ones[:], flat(oh[:, j]), start=False, stop=False,
                                         skip_group_check=True).then_inc(counted, 1)

        oh2, ranked, used, step, run_s = ph.sem("oh2"), ph.sem("ranked"), ph.sem("used"), ph.sem("step4"), ph.sem("run")
        with ph.block() as block:
            @block.gpsimd
            def _(pool):
                if beside[2] is not None:
                    beside[2](pool)

            @block.vector
            def _(dve):
                dve.sem_inc(used, 2)
                ch = Chain(dve, step)
                STEPS = 4
                one_hot(0, 0).then_inc(oh2, 1)
                with dve.Fori(0, NG // 2) as i:
                    for j in range(2):
                        g = i * 2 + j
                        if j == 0:
                            one_hot(g + 1, 1).then_inc(oh2, 1)
                        else:
                            one_hot(g + 1, 0).then_inc(oh2, 1)
                        dve.wait_ge(ranked, g + 1)
                        ch.at(g * STEPS)
                        ch.mark(nc.vector.tensor_tensor(run[:, 1 - j], run[:, j], tot_ps[j][:, 0:NBIN], ALU.add))
                        ch(nc.vector.tensor_tensor(ranks[:], rank_ps[j][:, 0:G * NBIN].rearrange("p (g b) -> p g b", g=G),
                                                   run[:, j].unsqueeze(1).broadcast_to([P, G, NBIN]), ALU.add))
                        ch(nc.vector.tensor_tensor(picked[:], ranks[:], oh[:, j], ALU.mult))
                        dve.sem_inc(used, 1)
                        ch(nc.vector.reduce_sum(pos[:, bass.ds(g * G, G)], picked[:], AXX))
                ch2 = Chain(dve, run_s)
                ch2(nc.vector.tensor_copy(place[:], pos[:]))
                ch2.mark(nc.vector.tensor_scalar(lowi[:], place[:], P - 1, None, ALU.bitwise_and))
                ch2(nc.vector.tensor_scalar(highi[:], place[:], LOGP, None, ALU.logical_shift_right))
                if pos_out is not None:
                    ch2.mark(nc.vector.tensor_copy(pos_out, pos[:]))
                ch2.mark(nc.vector.tensor_copy(low[:], lowi[:]))
                ch2(nc.vector.tensor_copy(high[:], highi[:]))
                ch2(nc.vector.scalar_tensor_tensor(low[:], low[:], float(TROW), high[:], ALU.mult, ALU.add))
                ch2(nc.vector.tensor_copy(place[:], low[:]))

            @block.tensor
            def _(pe):
                with pe.Fori(0, NG // 2) as i:
                    for j in range(2):
                        g = i * 2 + j
                        pe.wait_ge(oh2, g + 1)
                        pe.wait_ge(used, g + 1)
                        nc.tensor.matmul(rank_ps[j][:, 0:G * NBIN], k.before[:], flat(oh[:, j]), start=True, stop=False,
                                         skip_group_check=True)
                        for s in range(1, G):
                            nc.tensor.matmul(rank_ps[j][:, s * NBIN:G * NBIN], k.ones[:], flat(oh[:, j])[:, 0:(G - s) * NBIN],
                                             start=False, stop=(s == G - 1), skip_group_check=True)
                        for s in range(G):
                            last = nc.tensor.matmul(tot_ps[j][:, 0:NBIN], k.ones[:], oh[:, j, s], start=(s == 0), stop=(s == G - 1))
                        last.then_inc(ranked, 1)

        if staged is not None:
            kept = ph.sem("kept")
            with ph.block() as block:
                @block.sync
                def _(sp):
                    sp.dma_start(staged[0], place[:]).then_inc(kept, 16)
                    sp.dma_start(staged[1], rec[:]).then_inc(kept, 16)
                    sp.wait_ge(kept, 32)
            return tb_dram

        turns = ph.sem("turns")
        ringed = ph.sem("ringed")
        sent, before = ph.indirect(k, C // 2)
        with ph.block() as block:
            @block.vector
            def _(dve):
                def fill_ring(c0, j):
                    nc.vector.tensor_copy(ring_place[:, j], place[:, bass.ds(c0, HU)]).then_inc(ringed, 1)
                    nc.vector.tensor_copy(ring_rec[:, j], rec[:, bass.ds(c0, HU), :]).then_inc(ringed, 1)

                fill_ring(0, 0)
                fill_ring(HU, 1)
                with dve.Fori(1, C // (2 * HU)) as i:
                    for j in range(2):
                        dve.wait_ge(sent[j], before + i * (16 * HU))
                        fill_ring((i * 2 + j) * HU, j)

            @block.gpsimd
            def _(pool):
                with pool.Fori(0, C // (2 * HU)) as i:
                    for j in range(2):
                        pool.wait_ge(ringed, (i * 2 + j) * 2 + 2)
                        pool.sem_inc(turns)
                        for u in range(HU):
                            nc.gpsimd.indirect_dma_start(
                                out=records[:, :], out_offset=bass.IndirectOffsetOnAxis(ap=ring_place[:, j, u:u + 1], axis=0),
                                in_=ring_rec[:, j, u, :], in_offset=None).then_inc(sent[j], 16)
                for j in range(2):
                    pool.wait_ge(sent[j], before + C // 2 * 16)
    return tb_dram


class EdgePrep:

    def __init__(self, nc, key, other, weight):
        self.nc, self.key, self.other, self.weight = nc, key, other, weight

    def loads(self, ph, sp, loaded):
        self.ki, self.oi = ph.sb("ki", [P, EC], I32), ph.sb("oi", [P, EC], I32)
        self.w = ph.sb("w", [P, EC])
        zeroed = self.zeroed = ph.sem("zeroed")
        sp.wait_ge(zeroed, 3)
        for t, a in ((self.ki, self.key), (self.oi, self.other), (self.w, self.weight)):
            if a is None:
                continue
            sp.dma_start(t[0:P - 1, :], a[0:(P - 1) * EC].rearrange("(p c) -> p c", c=EC)).then_inc(loaded, 16)
            sp.dma_start(t[P - 1:P, 0:ELAST], a[(P - 1) * EC:E].unsqueeze(0)).then_inc(loaded, 16)

    def compute(self, ph, dve, ch, loaded, bins, rec):
        nc = self.nc
        nc.vector.memset(self.ki[:], (NB - 1) * P).then_inc(self.zeroed, 1)
        nc.vector.memset(self.oi[:], 0).then_inc(self.zeroed, 1)
        nc.vector.memset(self.w[:], 0.0).then_inc(self.zeroed, 1)
        kl, kb = ph.sb("kl", [P, EC], I32), ph.sb("kb", [P, EC], I32)
        dve.wait_ge(loaded, 64 if self.weight is None else 96)
        ch.mark(nc.vector.memset(bins[:, EC:], 0.0))
        ch.mark(nc.vector.memset(rec[:], 0.0))
        ch.mark(nc.vector.tensor_scalar(kl[:], self.ki[:], P - 1, None, ALU.bitwise_and))
        ch(nc.vector.tensor_scalar(kb[:], self.ki[:], LOGP, None, ALU.logical_shift_right))
        ch.mark(nc.vector.tensor_copy(rec[:, :, 0], self.oi[:]))
        ch.mark(nc.vector.tensor_copy(rec[:, :, 2], self.w[:]))
        ch.mark(nc.vector.tensor_copy(rec[:, :, 1], kl[:]))
        ch(nc.vector.tensor_copy(bins[:, 0:EC], kb[:]))


class EdgeOrder:

    def __init__(self, nc, name, key, other, weight):
        self.nc, self.name, self.key, self.other, self.weight = nc, name, key, other, weight
        self.records = nc.dram_tensor(f"{name}_records", [P * EROW, 4], F32, kind="Internal").ap()
        self.places = nc.dram_tensor(f"{name}_places", [P, EC], I32, kind="Internal").ap()
        self.recs = nc.dram_tensor(f"{name}_recs", [P, EC, 4], F32, kind="Internal").ap()

    def plan(self, k, beside=(None, None, None)):
        G = 8
        with Phase(self.nc, f"{self.name}b") as ph:
            bins = ph.sb("bins", [P, EC + G])

            def prefill(ch, fill):
                ch(self.nc.vector.memset(fill[:, :, 1], -1.0))

            self.tb_dram = sort_items(self.nc, k, self.name, bins, EdgePrep(self.nc, self.key, self.other, self.weight),
                                      EC, G, NB, ET, EROW, 8, 4, self.records, prefill=prefill,
                                      staged=(self.places, self.recs), beside=beside)

    def load(self, SRT, tile_block, zero_tail=None):
        nc = self.nc
        with Phase(nc, f"{self.name}l") as ph:
            loaded, zeroed = ph.sem("loaded"), ph.sem("zeroed")
            with ph.block() as block:
                @block.vector
                def _(dve):
                    nc.vector.memset(tile_block[0:1, ET:EROW], 0).then_inc(zeroed, 1)
                    if zero_tail is not None:
                        nc.vector.memset(zero_tail[:, ET:EROW, :], 0.0).then_inc(zeroed, 1)

                @block.sync
                def _(sp):
                    sp.dma_start(SRT[:], self.records.rearrange("(p t) r -> p t r", p=P)).then_inc(loaded, 16)
                    sp.dma_start(tile_block[0:1, 0:ET], self.tb_dram[0:ET].unsqueeze(0)).then_inc(loaded, 16)
                    sp.wait_ge(loaded, 32)


class Scatter:
    HU = 8
    ROUNDS = EC // (2 * HU)

    def __init__(self, nc, k, ph, order, start=0, most=ROUNDS):
        self.nc, self.k, self.order, self.at = nc, k, order, start
        self.start, self.name = start, f"{order.name}{start}"
        self.last = min(start + most, self.ROUNDS)
        cols = slice(start * 2 * self.HU, self.last * 2 * self.HU)
        self.place = ph.sb(f"place{self.name}", [P, cols.stop - cols.start], I32)
        self.rec = ph.sb(f"rec{self.name}", [P, cols.stop - cols.start, 4])
        self.ring_place = ph.sb(f"ring_place{self.name}", [P, 2, self.HU], I32)
        self.ring_rec = ph.sb(f"ring_rec{self.name}", [P, 2, self.HU, 4])
        self.ringed, self.turns = ph.sem(f"ringed{self.name}"), ph.sem(f"scatter_turns{self.name}")
        loaded = ph.sem(f"scatter_loaded{self.name}")
        self.before = k.scattered_before - 16 * self.HU * start
        with ph.block() as block:
            @block.sync
            def _(sp):
                sp.dma_start(self.place[:], order.places[:, cols]).then_inc(loaded, 16)
                sp.dma_start(self.rec[:], order.recs[:, cols, :]).then_inc(loaded, 16)
                sp.wait_ge(loaded, 32)

    def piece(self, pool, rounds):
        first, end = self.at, min(self.at + rounds, self.last)

        def one(r, first=False):
            for j in range(2):
                self.half(pool, r, j, first)

        if first == self.start and end > first:
            one(first, True)
            first += 1
        if end > first:
            with pool.Fori(first, end) as r:
                one(r)
        self.at = end

    def half(self, pool, r, j, first=False):
        nc, HU, sent = self.nc, self.HU, self.k.scattered
        if not first:
            pool.wait_ge(sent[j], self.before + r * (16 * HU))
        c0 = (r - self.start) * (2 * HU) + j * HU
        nc.gpsimd.tensor_copy(self.ring_place[:, j], self.place[:, bass.ds(c0, HU)]).then_inc(self.ringed, 1)
        nc.gpsimd.tensor_copy(self.ring_rec[:, j], self.rec[:, bass.ds(c0, HU), :]).then_inc(self.ringed, 1)
        pool.wait_ge(self.ringed, (r - self.start) * 4 + 2 * j + 2)
        pool.sem_inc(self.turns)
        for u in range(HU):
            nc.gpsimd.indirect_dma_start(
                out=self.order.records[:, :], out_offset=bass.IndirectOffsetOnAxis(ap=self.ring_place[:, j, u:u + 1], axis=0),
                in_=self.ring_rec[:, j, u, :], in_offset=None).then_inc(sent[j], 16)

    def close(self, pool):
        self.k.scattered_before = self.before + 16 * self.HU * self.at
        for sent in self.k.scattered:
            pool.wait_ge(sent, self.k.scattered_before)


def blocks_of(nc, engine, tile_block, n):
    return nc.values_load_multi_w_load_instructions(tile_block[0:1, bass.ds(n * U, U)], engines=[engine],
                                                    min_val=0, max_val=NB - 1,
                                                    skip_runtime_bounds_check_because="the sort keeps them below NB")[1]


def propagate(nc, k, hop, table, SRT, tile_block, agg):
    with Phase(nc, f"prop{hop}") as ph:
        G = ph.sb("G", [P, 2, U, D])
        idx = ph.sb("idx", [P, 2, U], I32)
        lw = ph.sb("lw", [P, 2, U, 2])
        S = ph.sb("S", [P, 2, U, P])
        ps = [ph.ps(f"sum{u}") for u in range(U)]
        prepped, built, mm, added = ph.sem("prepped"), ph.sem("built"), ph.sem("mm"), ph.sem("added")
        zeroed, turns = ph.sem("zeroed"), ph.sem("turns")
        got, before = ph.indirect(k, ET // 2)
        PAIRS = ET // (2 * U)
        with ph.block() as block:
            @block.scalar
            def _(act):
                def prep(n, hf, first=False):
                    if not first:
                        act.wait_ge(mm, U * (n - 1))
                    nc.scalar.copy(idx[:, hf], SRT[:, bass.ds(n * U, U), 0]).then_inc(prepped, 1)
                    nc.scalar.copy(lw[:, hf], SRT[:, bass.ds(n * U, U), 1:3]).then_inc(prepped, 1)
                prep(0, 0, True)
                prep(1, 1, True)
                with act.Fori(1, PAIRS) as i:
                    prep(2 * i, 0)
                    prep(2 * i + 1, 1)
                prep(2 * PAIRS, 0)

            @block.gpsimd
            def _(pool):
                with pool.Fori(0, PAIRS) as i:
                    for hf in range(2):
                        n = 2 * i + hf
                        pool.wait_ge(prepped, 2 * n + 2)
                        pool.sem_inc(turns)
                        for u in range(U):
                            nc.gpsimd.indirect_dma_start(
                                out=G[:, hf, u, :], out_offset=None, in_=table[:, :],
                                in_offset=bass.IndirectOffsetOnAxis(ap=idx[:, hf, u:u + 1], axis=0)).then_inc(got[hf], 16)

            @block.tensor
            def _(pe):
                with pe.Fori(0, PAIRS) as i:
                    for hf in range(2):
                        n = 2 * i + hf
                        pe.wait_ge(got[hf], before + i * (16 * U) + 16 * U)
                        for u in range(U):
                            pe.wait_ge(built, n * U + u + 1)
                            pe.wait_ge(added, n * U + u + 1)
                            nc.tensor.matmul(ps[u][:, 0:D], S[:, hf, u, :], G[:, hf, u, :], start=True, stop=True).then_inc(mm, 1)

            @block.vector
            def _(dve):
                dve.sem_inc(added, U)
                nc.vector.memset(agg[:], 0.0).then_inc(zeroed, 1)
                dve.wait_ge(zeroed, 1)

                def build(n, hf, u):
                    if u == 0:
                        dve.wait_ge(prepped, 2 * n + 2)
                    nc.vector.tensor_scalar(S[:, hf, u, :], k.cols[:], lw[:, hf, u, 0:1], lw[:, hf, u, 1:2],
                                            ALU.is_equal, ALU.mult).then_inc(built, 1)

                for u in range(U):
                    build(0, 0, u)
                with dve.Fori(0, PAIRS) as i:
                    for hf in range(2):
                        n = 2 * i + hf
                        blocks = blocks_of(nc, mybir.EngineType.DVE, tile_block, n)
                        for u in range(U):
                            build(n + 1, 1 - hf, u)
                            b = blocks[u]
                            dve.wait_ge(mm, n * U + u + 1)
                            dve.wait_ge(added, U + n * U + u)
                            nc.vector.tensor_tensor(agg[:, bass.ds(b, 1), :], agg[:, bass.ds(b, 1), :],
                                                    ps[u][:, 0:D].unsqueeze(1), ALU.add).then_inc(added, 1)


def load_broadcast(nc, sp, dst, src, sem):
    sp.dma_start(dst, src.unsqueeze(0).broadcast_to([P, src.shape[0]])).then_inc(sem, 16)


def gat_tables(nc, k, X, W_src, W_dst, att_src, att_dst, table, atable, QT, beside):
    W8 = D + 2 * HEADS
    with Phase(nc, "gt") as ph:
        W = ph.sb("W", [P, KD, W8])
        Wd = ph.sb("Wd", [P, KD, D])
        att = ph.sb("att", [P, 2, D])
        prod = ph.sb("prod", [P, KD, D])
        norm = RowNorm(nc, ph, X)
        xn = ph.sb("xn", [P, 2, 1, D])
        xT = ph.sb("xT", [P, 2, KD, P])
        hs = ph.sb("hs", [P, 2, D])
        A = ph.sb("A", [P, NB, 2 * HEADS])
        mins = ph.sb("mins", [P, HEADS])
        shift = ph.sb("shift", [P, HEADS])
        As = ph.sb("As", [P, NB, HEADS])
        psT = [ph.ps(f"T{j}") for j in range(2)]
        psH = [ph.ps(f"H{j}") for j in range(2)]
        loaded, step = ph.sem("loaded"), ph.sem("step")
        normed = ph.sem("normed")
        trans, copied, prod_s, taken = ph.sem("trans"), ph.sem("copied"), ph.sem("prod"), ph.sem("taken")
        stored, folded = [ph.sem("stored0"), ph.sem("stored1")], ph.sem("folded")
        reduced, shifted, end = ph.sem("reduced"), ph.sem("shifted"), ph.sem("end")
        with ph.block() as block:
            @block.sync
            def _(sp):
                sp.dma_start(W[:, :, 0:D], W_src.rearrange("(k p) n -> p k n", p=P)).then_inc(loaded, 16)
                sp.dma_start(Wd[:], W_dst.rearrange("(k p) n -> p k n", p=P)).then_inc(loaded, 16)
                load_broadcast(nc, sp, att[:, 0, :], att_src.rearrange("h c -> (h c)"), loaded)
                load_broadcast(nc, sp, att[:, 1, :], att_dst.rearrange("h c -> (h c)"), loaded)
                with sp.Fori(0, NB // 2) as i:
                    for j in range(2):
                        sp.wait_ge(taken, 4 * i + 2 * j + 2)
                        sp.dma_start(table[bass.ds((2 * i + j) * P, P), :], hs[:, j]).then_inc(stored[j], 16)
                sp.wait_ge(shifted, 1)
                sp.dma_start(atable.rearrange("(b p) h -> p b h", p=P), As[:]).then_inc(end, 16)
                sp.wait_ge(end, 16)
                for j in range(2):
                    sp.wait_ge(stored[j], 16 * NB // 2)

            @block.vector
            def _(dve):
                ch = Chain(dve, step)
                norm.stats(dve, ch)
                dve.wait_ge(loaded, 64)
                for j, w in ((0, W[:, :, 0:D]), (1, Wd[:])):
                    ch(nc.vector.tensor_tensor(prod[:], w, att[:, j].unsqueeze(1).broadcast_to([P, KD, D]), ALU.mult))
                    ch(nc.vector.reduce_sum(W[:, :, D + HEADS * j:D + HEADS * (j + 1)],
                                            prod[:].rearrange("p k (h c) -> p k h c", h=HEADS), AXX))
                nc.vector.memset(mins[:], 0.0).then_inc(folded, 1)

                def normalise(n, j):
                    norm.apply(xn[:, j], n).then_inc(normed, 1)

                def take(i, j, first=False):
                    dve.wait_ge(prod_s, 2 * i + j + 1)
                    if not first:
                        dve.wait_ge(stored[j], 16 * i)
                    nc.vector.tensor_copy(hs[:, j], psH[j][:, 0:D]).then_inc(taken, 1)
                    nc.vector.tensor_copy(A[:, bass.ds(2 * i + j, 1), :], psH[j][:, D:W8].unsqueeze(1)).then_inc(taken, 1)

                normalise(0, 0)
                normalise(1, 1)
                take(0, 0, True)
                take(0, 1, True)
                with dve.Fori(1, NB // 2) as i:
                    normalise(2 * i, 0)
                    normalise(2 * i + 1, 1)
                    take(i, 0)
                    take(i, 1)
                dve.wait_ge(taken, 2 * NB)
                ch(nc.vector.tensor_scalar_mul(As[:], A[:, :, 0:HEADS], -1.0))
                nc.vector.tensor_reduce(mins[:], As[:].rearrange("p b h -> p h b"), AXX, ALU.max).then_inc(reduced, 1)
                dve.wait_ge(reduced, 2)
                sh = shift[:].unsqueeze(1).broadcast_to([P, NB, HEADS])
                nc.vector.tensor_tensor(As[:], A[:, :, 0:HEADS], sh, ALU.add).then_inc(shifted, 1)
                ch(nc.vector.tensor_tensor(QT[:, :, 0:HEADS], A[:, :, HEADS:2 * HEADS], sh, ALU.subtract))

            @block.gpsimd
            def _(pool):
                beside(pool)
                pool.wait_ge(reduced, 1)
                nc.gpsimd.partition_all_reduce(shift[:], mins[:], P, bass.bass_isa.ReduceOp.max).then_inc(reduced, 1)

            @block.tensor
            def _(pe):
                pe.wait_ge(folded, 1)

                def block_of(i, j, first=False):
                    n = 2 * i + j
                    pe.wait_ge(normed, n + 1)
                    if not first:
                        pe.wait_ge(copied, n - 1)
                    for c in range(KD):
                        last = nc.tensor.transpose(psT[j][:, c * P:(c + 1) * P], xn[:, j, 0, c * P:(c + 1) * P], k.ident[:])
                    last.then_inc(trans, 1)
                    pe.wait_ge(copied, n + 1)
                    if not first:
                        pe.wait_ge(taken, 2 * n - 2)
                    for c in range(KD):
                        last = nc.tensor.matmul(psH[j][:, 0:W8], xT[:, j, c], W[:, c], start=(c == 0), stop=(c == KD - 1))
                    last.then_inc(prod_s, 1)

                block_of(0, 0, True)
                block_of(0, 1, True)
                with pe.Fori(1, NB // 2) as i:
                    block_of(i, 0)
                    block_of(i, 1)

            @block.scalar
            def _(act):
                norm.root(act)

                def copy(i, j, first=False):
                    n = 2 * i + j
                    act.wait_ge(trans, n + 1)
                    if not first:
                        act.wait_ge(prod_s, n - 1)
                    nc.scalar.copy(xT[:, j], psT[j][:, 0:D].rearrange("p (c n) -> p c n", c=KD)).then_inc(copied, 1)
                copy(0, 0, True)
                copy(0, 1, True)
                with act.Fori(1, NB // 2) as i:
                    copy(i, 0)
                    copy(i, 1)


def gat_max(nc, k, atable, SRT, tile_block, AE, QT):
    with Phase(nc, "gm") as ph:
        AG = ph.sb("AG", [P, 2, U, HEADS])
        idx = ph.sb("idx", [P, 2, U], I32)
        loc = ph.sb("loc", [P, 2, U])
        S = ph.sb("S", [P, 2, U, P])
        diag = ph.sb("diag", [P, 2, HEADS, P])
        top = ph.sb("top", [P, U, HEADS])
        MX = ph.sb("MX", [P, NB, HEADS])
        lk = ph.sb("lk", [P, NB, HEADS])
        ps = [ph.ps(f"m{u}") for u in range(U)]
        prepped, built, mm, topped, maxed = ph.sem("prepped"), ph.sem("built"), ph.sem("mm"), ph.sem("topped"), ph.sem("maxed")
        zeroed, turns, diags, kept, step = ph.sem("zeroed"), ph.sem("turns"), ph.sem("diags"), ph.sem("kept"), ph.sem("step")
        got, before = ph.indirect(k, ET // 2)
        PAIRS = ET // (2 * U)
        with ph.block() as block:
            @block.scalar
            def _(act):
                def prep(n, hf, first=False):
                    if not first:
                        act.wait_ge(built, U * (n - 1))
                    nc.scalar.copy(idx[:, hf], SRT[:, bass.ds(n * U, U), 0]).then_inc(prepped, 1)
                    nc.scalar.copy(loc[:, hf], SRT[:, bass.ds(n * U, U), 1]).then_inc(prepped, 1)

                def diagonals(n, hf, i):
                    act.wait_ge(got[hf], before + i * (16 * U) + 16 * U)
                    nc.scalar.copy(AE[:, bass.ds(n * U, U), :], AG[:, hf]).then_inc(kept, 1)
                    for u in range(U):
                        act.wait_ge(mm, n * U + u + 2 * U - 1)
                        for h in range(HEADS):
                            nc.scalar.activation(diag[:, (hf * U + u) % 2, h], k.ident[:], ACT.Copy,
                                                 scale=AG[:, hf, u, h:h + 1]).then_inc(diags, 1)
                prep(0, 0, True)
                prep(1, 1, True)
                with act.Fori(0, PAIRS) as i:
                    for hf in range(2):
                        diagonals(2 * i + hf, hf, i)
                        prep(2 * i + hf + 2, hf)

            @block.gpsimd
            def _(pool):
                with pool.Fori(0, PAIRS) as i:
                    for hf in range(2):
                        n = 2 * i + hf
                        pool.wait_ge(prepped, 2 * n + 2)
                        pool.sem_inc(turns)
                        for u in range(U):
                            nc.gpsimd.indirect_dma_start(
                                out=AG[:, hf, u, :], out_offset=None, in_=atable[:, :],
                                in_offset=bass.IndirectOffsetOnAxis(ap=idx[:, hf, u:u + 1], axis=0)).then_inc(got[hf], 16)

            @block.tensor
            def _(pe):
                pe.sem_inc(mm, 2 * U)
                with pe.Fori(0, PAIRS) as i:
                    for hf in range(2):
                        n = 2 * i + hf
                        for u in range(U):
                            pe.wait_ge(built, n * U + u + 1)
                            pe.wait_ge(diags, (n * U + u + 1) * HEADS)
                            pe.wait_ge(topped, n * U + u + 1)
                            nc.tensor.matmul(ps[u][:, 0:HEADS * P], S[:, hf, u, :],
                                             diag[:, (hf * U + u) % 2].rearrange("p h e -> p (h e)"), start=True, stop=True).then_inc(mm, 1)

            @block.vector
            def _(dve):
                dve.sem_inc(topped, U)
                nc.vector.memset(MX[:], 0.0).then_inc(zeroed, 1)
                dve.wait_ge(zeroed, 1)

                def build(n, hf, u):
                    if u == 0:
                        dve.wait_ge(prepped, 2 * n + 2)
                    nc.vector.tensor_scalar(S[:, hf, u, :], k.cols[:], loc[:, hf, u:u + 1], None,
                                            ALU.is_equal).then_inc(built, 1)

                for u in range(U):
                    build(0, 0, u)
                with dve.Fori(0, PAIRS) as i:
                    for hf in range(2):
                        n = 2 * i + hf
                        blocks = blocks_of(nc, mybir.EngineType.DVE, tile_block, n)
                        for u in range(U):
                            dve.wait_ge(mm, 2 * U + n * U + u + 1)
                            nc.vector.tensor_reduce(top[:, u], ps[u][:, 0:HEADS * P].rearrange("p (h e) -> p h e", h=HEADS),
                                                    AXX, ALU.max).then_inc(topped, 1)
                            build(n + 1, 1 - hf, u)
                            b = blocks[u]
                            dve.wait_ge(topped, U + n * U + u + 1)
                            if not (hf == 0 and u == 0):
                                dve.wait_ge(maxed, n * U + u)
                            else:
                                dve.wait_ge(maxed, n * U)
                            nc.vector.tensor_tensor(MX[:, bass.ds(b, 1), :], MX[:, bass.ds(b, 1), :],
                                                    top[:, u].unsqueeze(1), ALU.max).then_inc(maxed, 1)
                dve.wait_ge(maxed, ET)
                ch = Chain(dve, step)
                ch(nc.vector.tensor_tensor(lk[:], MX[:], QT[:, :, 0:HEADS], ALU.add))
                ch(nc.vector.scalar_tensor_tensor(QT[:, :, HEADS:2 * HEADS], lk[:], NEG_SLOPE, lk[:], ALU.mult, ALU.max))


HW = HD + 1


def gat_sum(nc, k, table, SRT, tile_block, AE, QT, acc):
    with Phase(nc, "gs") as ph:
        G = ph.sb("G", [P, 2, U, D])
        idx = ph.sb("idx", [P, 2, U], I32)
        loc = ph.sb("loc", [P, 2, U])
        NS = 4
        S = ph.sb("S", [P, NS, U, P])
        ST = ph.sb("ST", [P, U, P], BF16)
        Q3 = ph.sb("Q3", [P, 3, NB, 2 * HEADS], BF16)
        rest = ph.sb("rest", [P, NB, 2 * HEADS])
        e1 = ph.sb("e1", [P, U, HEADS])
        e2 = ph.sb("e2", [P, U, HEADS])
        e3 = ph.sb("e3", [P, U, HEADS])
        M = ph.sb("M", [P, 2, U, HEADS, HW])
        NO = 4
        NT = 4
        psT = [ph.ps(f"T{j}") for j in range(2)]
        psQ = [ph.ps(f"Q{j}") for j in range(2)]
        psO = [ph.ps(f"O{j}") for j in range(NO)]
        indexed, located, built, mm, added = ph.sem("indexed"), ph.sem("located"), ph.sem("built"), ph.sem("mm"), ph.sem("added")
        zeroed, turns, trans, tcopied = ph.sem("zeroed"), ph.sem("turns"), ph.sem("trans"), ph.sem("tcopied")
        asked, logits, weighed, msgs = ph.sem("asked"), ph.sem("logits"), ph.sem("weighed"), ph.sem("msgs")
        got, before = ph.indirect(k, ET // 2)
        QUADS = ET // (NS * U)
        PARTS = ((0, 2), (2, 4), (4, 5), (5, 6), (6, 7))
        part_of = [next(j for j, (a, z) in enumerate(PARTS) if a <= u < z) for u in range(U)]
        NPART = len(PARTS)
        with ph.block() as block:
            @block.scalar
            def _(act):
                def index(n, hf):
                    nc.scalar.copy(idx[:, hf], SRT[:, bass.ds(n * U, U), 0]).then_inc(indexed, 1)

                def locate(n, hf):
                    nc.scalar.copy(loc[:, hf], SRT[:, bass.ds(n * U, U), 1]).then_inc(located, 1)

                def take_turned(n):
                    for j, (a, z) in enumerate(((0, NT), (NT, U))):
                        act.wait_ge(trans, 2 * n + j + 1)
                        nc.scalar.copy(ST[:, a:z], psT[j][:, 0:(z - a) * P].rearrange("p (u e) -> p u e", e=P)).then_inc(tcopied, 1)

                def weigh(n, hf):
                    act.wait_ge(logits, n + 1)
                    nc.scalar.activation(M[:, hf, :, :, HD], e3[:], ACT.Exp).then_inc(weighed, 1)

                for j in range(2):
                    index(j, j)
                    locate(j, j)
                take_turned(0)
                weigh(0, 0)
                locate(2, 0)
                take_turned(1)
                with act.Fori(0, QUADS) as i:
                    for r in range(NS):
                        n, hf = NS * i + r, r % 2
                        act.wait_ge(msgs, NPART * (n + 1))
                        index(n + 2, hf)
                        locate(n + 3, 1 - hf)
                        weigh(n + 1, 1 - hf)
                        take_turned(n + 2)

            @block.gpsimd
            def _(pool):
                with pool.Fori(0, QUADS) as i:
                    for r in range(NS):
                        n, hf = NS * i + r, r % 2
                        pool.wait_ge(indexed, n + 1)
                        pool.sem_inc(turns)
                        for u in range(U):
                            nc.gpsimd.indirect_dma_start(
                                out=G[:, hf, u, :], out_offset=None, in_=table[:, :],
                                in_offset=bass.IndirectOffsetOnAxis(ap=idx[:, hf, u:u + 1], axis=0)).then_inc(got[hf], 16)

            @block.tensor
            def _(pe):
                def turn(n, r, first, last):
                    for u in range(first, last):
                        pe.wait_ge(built, n * U + u + 1)
                        done = nc.tensor.transpose(psT[u // NT][:, (u % NT) * P:(u % NT + 1) * P], S[:, r, u, :], k.ident[:])
                    done.then_inc(trans, 1)

                def ask(n, hf):
                    blocks = blocks_of(nc, mybir.EngineType.PE, tile_block, n)
                    for u in range(U):
                        b = blocks[u]
                        if u in (0, NT):
                            pe.wait_ge(tcopied, 2 * n + 1 + u // NT)
                        for j in range(3):
                            last = nc.tensor.matmul(psQ[hf][:, u * 2 * HEADS:(u + 1) * 2 * HEADS], ST[:, u],
                                                    Q3[:, j, bass.ds(b, 1), :].rearrange("p a q -> p (a q)"),
                                                    start=(j == 0), stop=(j == 2))
                    last.then_inc(asked, 1)

                def product(n, r, hf, u):
                    pe.wait_ge(msgs, n * NPART + part_of[u] + 1)
                    if u >= NO:
                        pe.wait_ge(added, n * U + u - NO + 1)
                    nc.tensor.matmul(psO[u % NO][:, 0:HEADS * HW], S[:, r, u, :],
                                     M[:, hf, u].rearrange("p h c -> p (h c)"), start=True, stop=True).then_inc(mm, 1)

                turn(0, 0, 0, NT)
                turn(0, 0, NT, U)
                ask(0, 0)
                turn(1, 1, 0, NT)
                turn(1, 1, NT, U)
                with pe.Fori(0, QUADS) as i:
                    for r in range(NS):
                        n, hf = NS * i + r, r % 2
                        product(n, r, hf, 0)
                        product(n, r, hf, 1)
                        product(n, r, hf, 2)
                        product(n, r, hf, 3)
                        ask(n + 1, 1 - hf)
                        for u in range(NO, U):
                            product(n, r, hf, u)
                        turn(n + 2, (r + 2) % NS, 0, NT)
                        turn(n + 2, (r + 2) % NS, NT, U)

            @block.vector
            def _(dve):
                ch = Chain(dve, zeroed)
                ch.mark(nc.vector.memset(acc[:], 0.0))
                ch(nc.vector.tensor_copy(Q3[:, 0], QT[:]))
                ch(nc.vector.tensor_tensor(rest[:], QT[:], Q3[:, 0], ALU.subtract))
                ch(nc.vector.tensor_copy(Q3[:, 1], rest[:]))
                ch(nc.vector.tensor_tensor(rest[:], rest[:], Q3[:, 1], ALU.subtract))
                ch(nc.vector.tensor_copy(Q3[:, 2], rest[:]))
                SPLIT = ch.n

                def build(n, r, u):
                    if u == 0:
                        dve.wait_ge(located, n + 1)
                    nc.vector.tensor_scalar(S[:, r, u, :], k.cols[:], loc[:, r % 2, u:u + 1], None,
                                            ALU.is_equal).then_inc(built, 1)

                def edge_logits(n, hf):
                    q = psQ[hf][:, 0:U * 2 * HEADS].rearrange("p (u q) -> p u q", u=U)
                    def plus():
                        dve.wait_ge(asked, n + 1)
                        ch.at(3 * n + SPLIT)
                        ch.mark(nc.vector.tensor_tensor(e1[:], AE[:, bass.ds(n * U, U), :], q[:, :, 0:HEADS], ALU.add))
                    def leaky():
                        ch.wait()
                        ch.mark(nc.vector.scalar_tensor_tensor(e2[:], e1[:], NEG_SLOPE, e1[:], ALU.mult, ALU.max))
                    def minus():
                        ch.wait()
                        ch.mark(nc.vector.tensor_tensor(e1[:], e2[:], q[:, :, HEADS:2 * HEADS], ALU.subtract))
                    def guard():
                        ch.wait()
                        nc.vector.tensor_scalar_min(e3[:], e1[:], 0.0).then_inc(logits, 1)
                    return plus, leaky, minus, guard

                for n in range(2):
                    for u in range(U):
                        build(n, n, u)
                for step in edge_logits(0, 0):
                    step()
                with dve.Fori(0, QUADS) as i:
                    for r in range(NS):
                        n, hf = NS * i + r, r % 2

                        def message(j):
                            a, z = PARTS[j]
                            nc.vector.tensor_tensor(
                                M[:, hf, a:z, :, 0:HD].rearrange("p u h c -> p (u h) c"),
                                G[:, hf, a:z].rearrange("p u (h c) -> p (u h) c", h=HEADS),
                                M[:, hf, a:z, :, HD:HW].rearrange("p u h c -> p (u h) c").broadcast_to([P, (z - a) * HEADS, HD]),
                                ALU.mult).then_inc(msgs, 1)

                        def add(u):
                            b = blocks[u]
                            dve.wait_ge(mm, n * U + u + 1)
                            dve.wait_ge(added, n * U + u) if u or r else None
                            a = acc[:, bass.ds(b, 1), :, :].rearrange("p a h c -> p a (h c)")
                            nc.vector.tensor_tensor(a, a, psO[u % NO][:, 0:HEADS * HW].unsqueeze(1), ALU.add).then_inc(added, 1)

                        blocks = blocks_of(nc, mybir.EngineType.DVE, tile_block, n)
                        dve.wait_ge(weighed, n + 1)
                        dve.wait_ge(got[hf], before + i * (2 * 16 * U) + (r // 2 + 1) * 16 * U)
                        plus, leaky, minus, guard = edge_logits(n + 1, 1 - hf)
                        b = lambda u: build(n + 2, (r + 2) % NS, u)
                        message(0)
                        b(0), b(1), b(2)
                        message(1)
                        message(2)
                        add(0)
                        message(3)
                        add(1)
                        message(4)
                        add(2)
                        b(3)
                        add(3)
                        b(4)
                        plus()
                        b(5)
                        leaky()
                        add(4)
                        minus()
                        b(6)
                        guard()
                        add(5)
                        add(6)


def gat_finish(nc, k, X, acc, bias, gamma, beta, prelu, beside):
    with Phase(nc, "gf") as ph:
        vec = ph.sb("vec", [P, 4, D])
        den = ph.sb("den", [P, NB, HEADS])
        XL = ph.sb("XL", [P, NB, D])
        loaded, step, made = ph.sem("loaded"), ph.sem("step"), ph.sem("made")
        norm = RowNorm(nc, ph, XL)
        row = lambda j: vec[:, j].unsqueeze(1).broadcast_to([P, NB, D])
        with ph.block() as block:
            @block.sync
            def _(sp):
                for j, v in enumerate((bias, gamma, beta, prelu)):
                    load_broadcast(nc, sp, vec[:, j, :], v, loaded)

            @block.gpsimd
            def _(pool):
                beside(pool)

            @block.scalar
            def _(act):
                norm.root(act)

            @block.vector
            def _(dve):
                ch = Chain(dve, step)
                ch(nc.vector.tensor_scalar_max(den[:], acc[:, :, :, HD], 1e-16))
                ch(nc.vector.reciprocal(den[:], den[:]))
                for h in range(HEADS):
                    ch.mark(nc.vector.tensor_tensor(XL[:, :, h * HD:(h + 1) * HD], acc[:, :, h, 0:HD],
                                                    den[:, :, h:h + 1].broadcast_to([P, NB, HD]), ALU.mult))
                ch.wait()
                dve.wait_ge(loaded, 64)
                ch(nc.vector.tensor_tensor(XL[:], XL[:], row(0), ALU.add))
                norm.all(dve, ch, XL)
                ch(nc.vector.tensor_tensor(XL[:], XL[:], row(1), ALU.mult))
                ch(nc.vector.tensor_tensor(XL[:], XL[:], row(2), ALU.add))
                neg = acc[:].rearrange("p b h c -> p (b h c)")[:, 0:NB * D].rearrange("p (b d) -> p b d", b=NB)
                ch(nc.vector.scalar_tensor_tensor(neg, XL[:], 0.0, row(3), ALU.min, ALU.mult))
                ch(nc.vector.scalar_tensor_tensor(XL[:], XL[:], 0.0, neg, ALU.max, ALU.add))
                ch(nc.vector.tensor_tensor(X[:], X[:], XL[:], ALU.add))


def gat_layer(nc, k, X, src, dst, W_src, W_dst, att_src, att_dst, bias, gamma, beta, prelu, later, rounds=8):
    table = nc.dram_tensor("gat_table", [NP, D], F32, kind="Internal").ap()
    atable = nc.dram_tensor("gat_atable", [NP, HEADS], F32, kind="Internal").ap()
    order = EdgeOrder(nc, "sd", dst, src, None)
    with Phase(nc, "gat") as ph:
        QT = ph.sb("QT", [P, NB, 2 * HEADS])
        order.plan(k)
        with Phase(nc, "sc") as ps:
            scatter = Scatter(nc, k, ps, order)
            gat_tables(nc, k, X, W_src, W_dst, att_src, att_dst, table, atable, QT, lambda pool: scatter.piece(pool, 13))
            later.plan(k, (lambda pool: scatter.piece(pool, 1), lambda pool: scatter.piece(pool, 4),
                           lambda pool: scatter.piece(pool, 18)))
            with ps.block() as block:
                @block.gpsimd
                def _(pool):
                    scatter.piece(pool, scatter.ROUNDS)
                    scatter.close(pool)
        acc = ph.sb("acc", [P, NB, HEADS, HW])
        with Phase(nc, "edges") as pe:
            SRT, tbk, AE = pe.sb("SRT", [P, EROW, 4]), pe.sb("tbk", [1, EROW], I32), pe.sb("AE", [P, EROW, HEADS])
            order.load(SRT, tbk, zero_tail=AE)
            gat_max(nc, k, atable, SRT, tbk, AE, QT)
            gat_sum(nc, k, table, SRT, tbk, AE, QT, acc)
        with Phase(nc, "sc2") as ps:
            scatter = Scatter(nc, k, ps, later, 0, rounds)
            gat_finish(nc, k, X, acc, bias, gamma, beta, prelu, lambda pool: scatter.piece(pool, rounds))
            with ps.block() as block:
                @block.gpsimd
                def _(pool):
                    scatter.close(pool)
    return scatter.at


NE = 8
TOPK = 2
HID = 1024
KH = HID // P
MC = NB * TOPK
MU = 2
MT = (P * MC + NE * (P - 1)) // P // MU * MU + MU
BANK = 512
BPART = 32
BROWS = 2 * BPART + NE


class ItemPrep:

    def __init__(self, nc, k, expert):
        self.nc, self.k, self.expert = nc, k, expert

    def loads(self, ph, sp, loaded):
        pass

    def compute(self, ph, dve, ch, loaded, bins, rec):
        nc = self.nc
        node = ph.sb("node", [P, NB])
        ch.mark(nc.vector.memset(bins[:, MC:], 0.0))
        ch.mark(nc.vector.tensor_copy(bins[:, 0:MC], self.expert[:].rearrange("p k b -> p (k b)")))
        ch(nc.vector.tensor_scalar(node[:], self.k.cols[:, 0:NB], float(P), self.k.part[:, 0:1], ALU.mult, ALU.add))
        for j in range(TOPK):
            ch.mark(nc.vector.tensor_copy(rec[:, j * NB:(j + 1) * NB, 0], node[:]))


def moe_route(nc, k, X, Wr, br, table, expert, weight, beside):
    with Phase(nc, "mr") as ph:
        norm = RowNorm(nc, ph, X)
        XT1 = ph.sb("xt", [P, NB, D])
        norm2 = RowNorm(nc, ph, XT1, "2")
        xs = ph.sb("xs", [P, 2, D])
        xT = ph.sb("xT", [P, 2, KD, P])
        W = ph.sb("W", [P, KD, NE])
        b1 = ph.sb("b", [1, NE])
        L = ph.sb("L", [P, NB, NE])
        Pr = ph.sb("Pr", [P, NB, NE])
        eq = ph.sb("eq", [P, NB, NE])
        m = ph.sb("m", [P, TOPK, NB])
        s = ph.sb("s", [P, NB])
        psT = [ph.ps(f"T{j}") for j in range(2)]
        psL = [ph.ps(f"L{j}") for j in range(2)]
        loaded, step = ph.sem("loaded"), ph.sem("step")
        ready, trans, copied, prods, taken = ph.sem("ready"), ph.sem("trans"), ph.sem("copied"), ph.sem("prods"), ph.sem("taken")
        centred, exped, tabled, stored = ph.sem("centred"), ph.sem("exped"), ph.sem("tabled"), ph.sem("stored")
        with ph.block() as block:
            @block.sync
            def _(sp):
                sp.dma_start(W[:], Wr.rearrange("(k p) n -> p k n", p=P)).then_inc(loaded, 16)
                sp.dma_start(b1[:], br.unsqueeze(0)).then_inc(loaded, 16)
                sp.wait_ge(tabled, 1)
                sp.dma_start(table.rearrange("(b p) d -> p b d", p=P), XT1[:]).then_inc(stored, 16)
                sp.wait_ge(stored, 16)

            @block.gpsimd
            def _(pool):
                beside(pool)

            @block.vector
            def _(dve):
                ch = Chain(dve, step)
                norm.all(dve, ch, XT1)
                nc.vector.tensor_copy(xs[:, 0], XT1[:, 0]).then_inc(ready, 1)
                nc.vector.tensor_copy(xs[:, 1], XT1[:, 1]).then_inc(ready, 1)

                def take(n, j):
                    dve.wait_ge(prods, n + 1)
                    nc.vector.tensor_copy(L[:, bass.ds(n, 1), :], psL[j][:, 0:NE].unsqueeze(1)).then_inc(taken, 1)

                with dve.Fori(0, NB // 2 - 1) as i:
                    for j in range(2):
                        take(2 * i + j, j)
                        nc.vector.tensor_copy(xs[:, j].unsqueeze(1), XT1[:, bass.ds(2 * i + j + 2, 1)]).then_inc(ready, 1)
                take(NB - 2, 0)
                take(NB - 1, 1)
                dve.wait_ge(taken, NB)
                norm2.stats(dve, ch)
                with dve.Fori(0, NB // ROUND) as i:
                    for j in range(ROUND):
                        b = i * ROUND + j
                        norm2.apply(XT1[:, bass.ds(b, 1), :], b).then_inc(ch.sem, 1)
                ch.n += NB
                ch.wait()
                ch(nc.vector.reduce_max(s[:], L[:], AXX))
                dve.sem_inc(tabled, 1)
                wide = lambda a: a.unsqueeze(2).broadcast_to([P, NB, NE])
                nc.vector.tensor_tensor(L[:], L[:], wide(s[:]), ALU.subtract).then_inc(centred, 1)
                dve.wait_ge(exped, 1)
                ch(nc.vector.reduce_sum(s[:], Pr[:], AXX))
                ch(nc.vector.reciprocal(s[:], s[:]))
                ch(nc.vector.tensor_tensor(Pr[:], Pr[:], wide(s[:]), ALU.mult))
                iota = k.cols[:, 0:NE].unsqueeze(1).broadcast_to([P, NB, NE])
                for j in range(TOPK):
                    ch(nc.vector.reduce_max(m[:, j], Pr[:], AXX))
                    ch(nc.vector.tensor_tensor(eq[:], Pr[:], wide(m[:, j]), ALU.is_equal))
                    ch(nc.vector.tensor_scalar(L[:], iota, -1.0, float(NE), ALU.mult, ALU.add))
                    ch(nc.vector.tensor_tensor(eq[:], eq[:], L[:], ALU.mult))
                    ch(nc.vector.reduce_max(s[:], eq[:], AXX))
                    ch(nc.vector.tensor_scalar(expert[:, j], s[:], -1.0, float(NE), ALU.mult, ALU.add))
                    if j + 1 < TOPK:
                        ch(nc.vector.tensor_tensor(eq[:], iota, wide(expert[:, j]), ALU.is_equal))
                        ch(nc.vector.scalar_tensor_tensor(Pr[:], eq[:], -2.0, Pr[:], ALU.mult, ALU.add))
                ch(nc.vector.tensor_tensor(s[:], m[:, 0], m[:, 1], ALU.add))
                ch(nc.vector.reciprocal(s[:], s[:]))
                for j in range(TOPK):
                    ch.mark(nc.vector.tensor_tensor(weight[:, j], m[:, j], s[:], ALU.mult))
                ch.wait()

            @block.scalar
            def _(act):
                norm.root(act)
                with act.Fori(0, NB // 2) as i:
                    for j in range(2):
                        act.wait_ge(trans, 2 * i + j + 1)
                        nc.scalar.copy(xT[:, j], psT[j][:, 0:D].rearrange("p (c n) -> p c n", c=KD)).then_inc(copied, 1)
                norm2.root(act)
                act.wait_ge(centred, 1)
                nc.scalar.activation(Pr[:], L[:], ACT.Exp).then_inc(exped, 1)

            @block.tensor
            def _(pe):
                pe.wait_ge(loaded, 32)
                with pe.Fori(0, NB // 2) as i:
                    for j in range(2):
                        n = 2 * i + j
                        pe.wait_ge(ready, n + 1)
                        for c in range(KD):
                            last = nc.tensor.transpose(psT[j][:, c * P:(c + 1) * P], xs[:, j, c * P:(c + 1) * P], k.ident[:])
                        last.then_inc(trans, 1)
                        pe.wait_ge(copied, n + 1)
                        for c in range(KD):
                            nc.tensor.matmul(psL[j][:, 0:NE], xT[:, j, c], W[:, c], start=(c == 0), stop=False)
                        nc.tensor.matmul(psL[j][:, 0:NE], k.onesf[0:1, :], b1[:], start=False, stop=True).then_inc(prods, 1)


def moe_experts(nc, k, table, slots, tile_bin, tb_dram, ln_g, ln_b, W1, b1, W2, b2, Y, later, start):
    with Phase(nc, "me") as ph:
        W1s = ph.sb("W1", [P, NE, KD, HID])
        W2s = ph.sb("W2", [P, NE, KH, D])
        B3 = ph.sb("B3", [BROWS, HID + D], BF16)
        oht = ph.sb("oht", [BROWS, MT])
        oh = ph.sb("oh", [BROWS, 2, P], BF16)
        idx = ph.sb("idx", [P, 2], I32)
        XG = ph.sb("XG", [P, 2, D])
        xT = ph.sb("xT", [P, KD, P])
        Hs = ph.sb("H", [P, HID])
        HT = ph.sb("HT", [P, KH, P])
        Ys = ph.sb("Ys", [P, 2, D])
        NHB = HID // BANK
        HPB = BANK // P
        psX = ph.ps("X")
        psH = [ph.ps(f"H{j}") for j in range(2 * NHB)]
        psT = [ph.ps(f"T{j}") for j in range(2)]
        psY = ph.ps("Y")
        loaded, step, small = ph.sem("loaded"), ph.sem("step"), ph.sem("small")
        ready, biased, cleared, parted, spread = (ph.sem("ready"), ph.sem("biased"), ph.sem("cleared"), ph.sem("parted"),
                                                  ph.sem("spread"))
        with Phase(nc, "mef") as pf:
            g8 = pf.sb("g8", [P, KD, NE])
            b8 = pf.sb("b8", [P, KD, NE])
            bsel = pf.sb("bsel", [P, NE, KD, NE])
            bias = pf.sb("bias", [NE, HID + D])
            part = pf.sb("part", [NE, HID + D], BF16)
            own = pf.sb("own", [BROWS, 1], I32)
            ownf = pf.sb("ownf", [BROWS, 1])
            tbi = pf.sb("tbi", [BROWS, MT], I32)
            with ph.block() as block:
                @block.sync
                def _(sp):
                    for a, t in ((ln_g, g8), (ln_b, b8)):
                        for c in range(KD):
                            with nc.allow_non_contiguous_dma(reason="8 x 256 values to columns"):
                                sp.dma_start(t[:, c, :], a[:, c * P:(c + 1) * P].rearrange("e p -> p e")).then_inc(small, 16)
                    sp.dma_start(bias[:, 0:HID], b1).then_inc(small, 16)
                    sp.dma_start(bias[:, HID:], b2).then_inc(small, 16)
                    sp.wait_ge(cleared, 1)
                    for q in range(3):
                        sp.dma_start(tbi[q * BPART:q * BPART + NE, :], tb_dram[0:MT].unsqueeze(0).broadcast_to([NE, MT])).then_inc(small, 16)
                    for e in range(NE):
                        sp.dma_start(W1s[:, e], W1[e].rearrange("(k p) h -> p k h", p=P)).then_inc(loaded, 16)
                    for e in range(NE):
                        sp.dma_start(W2s[:, e], W2[e].rearrange("(k p) d -> p k d", p=P)).then_inc(loaded, 16)
                    for q in range(3):
                        sp.wait_ge(parted, q + 1)
                        sp.dma_start(B3[q * BPART:q * BPART + NE, :], part[:]).then_inc(spread, 16)
                    sp.wait_ge(loaded, 32 * NE)
                    sp.wait_ge(spread, 48)

                @block.vector
                def _(dve):
                    ch = Chain(dve, step)
                    nc.vector.memset(tbi[:], 0).then_inc(cleared, 1)
                    ch.mark(nc.vector.memset(bsel[:], 0.0))
                    ch.mark(nc.vector.memset(B3[:], 0.0))
                    ch(nc.vector.tensor_copy(own[:], k.part[0:BROWS, 0:1]))
                    ch(nc.vector.tensor_scalar(own[:], own[:], BPART - 1, None, ALU.bitwise_and))
                    ch(nc.vector.tensor_copy(ownf[:], own[:]))
                    dve.wait_ge(small, 16 * (2 * KD + 5))
                    ch(nc.vector.tensor_copy(oht[:], tbi[:]))
                    ch.mark(nc.vector.tensor_scalar(oht[:], oht[:], ownf[:, 0:1], None, ALU.is_equal))
                    for e in range(NE):
                        ch.mark(nc.vector.tensor_copy(bsel[:, e, :, e], b8[:, :, e]))
                    ch.wait()
                    dve.sem_inc(ready, 1)
                    dve.wait_ge(biased, 1)
                    for n in range(NHB):
                        ch.mark(nc.vector.tensor_tensor(bias[:, n * BANK:(n + 1) * BANK], psH[n][0:NE, :],
                                                        bias[:, n * BANK:(n + 1) * BANK], ALU.add))
                    ch.wait()
                    for q in range(3):
                        if q > 0:
                            dve.wait_ge(spread, 16 * q)
                        nc.vector.tensor_copy(part[:], bias[:]).then_inc(parted, 1)
                        dve.wait_ge(parted, q + 1)
                        if q < 2:
                            ch(nc.vector.tensor_tensor(bias[:], bias[:], part[:], ALU.subtract))
                    for e in range(NE):
                        for c in range(KD):
                            ch.mark(nc.vector.tensor_scalar_mul(W1s[:, e, c], W1s[:, e, c], g8[:, c, e:e + 1]))
                    ch.wait()

                @block.tensor
                def _(pe):
                    pe.wait_ge(ready, 1)
                    pe.wait_ge(loaded, 32 * NE)
                    for n in range(NHB):
                        for e in range(NE):
                            for c in range(KD):
                                last = nc.tensor.matmul(psH[n][0:NE, :], bsel[:, e, c], W1s[:, e, c, n * BANK:(n + 1) * BANK],
                                                        start=(e == 0 and c == 0), stop=(e == NE - 1 and c == KD - 1))
                    last.then_inc(biased, 1)

        scatter = Scatter(nc, k, ph, later, start)
        prepped, turns, chosen = ph.sem("prepped"), ph.sem("turns"), ph.sem("chosen")
        got, before = ph.indirect(k, MT // 2)
        transx, xcopied, hid, act_s, transh, hcopied = (ph.sem("transx"), ph.sem("xcopied"), ph.sem("hid"), ph.sem("gelu"),
                                                        ph.sem("transh"), ph.sem("hcopied"))
        outs, taken = ph.sem("outs"), ph.sem("taken")
        sent = [ph.sem("sent0"), ph.sem("sent1")]
        R = MT // 2
        with ph.block() as block:
            @block.scalar
            def _(act):
                def rows(t, j, first=False):
                    if not first:
                        act.wait_ge(transx, t - 1)
                    nc.scalar.copy(idx[:, j:j + 1], slots[:, bass.ds(t, 1)]).then_inc(prepped, 1)

                def one_hot(t, j, first=False):
                    if not first:
                        act.wait_ge(outs, t - 1)
                    nc.scalar.copy(oh[:, j], oht[:, bass.ds(t, 1)].broadcast_to([BROWS, P])).then_inc(chosen, 1)

                def gelus(t, j):
                    act.wait_ge(hid, t + 1)
                    act.wait_ge(transh, 2 * t + 2)
                    for n in range(NHB):
                        nc.scalar.activation(Hs[:, n * BANK:(n + 1) * BANK], psH[2 * j + n][:], ACT.Gelu).then_inc(act_s, 1)

                for j in range(2):
                    rows(j, j, True)
                    one_hot(j, j, True)
                gelus(0, 0)
                with act.Fori(1, R) as i:
                    for j in range(2):
                        rows(2 * i + j, j)
                        gelus(2 * i + j - 1, 1 - j)
                        one_hot(2 * i + j, j)
                gelus(MT - 1, 1)

            @block.gpsimd
            def _(pool):
                def gather(t, j, first=False):
                    pool.wait_ge(prepped, t + 1)
                    pool.sem_inc(turns)
                    nc.gpsimd.indirect_dma_start(out=XG[:, j], out_offset=None, in_=table[:, :],
                                                 in_offset=bass.IndirectOffsetOnAxis(ap=idx[:, j:j + 1], axis=0)).then_inc(got[j], 16)
                LEFT = scatter.ROUNDS - start
                for j in range(2):
                    gather(j, j)
                    scatter.half(pool, start, j, True)
                with pool.Fori(1, LEFT) as i:
                    for j in range(2):
                        gather(2 * i + j, j)
                        scatter.half(pool, i + start, j)
                with pool.Fori(LEFT, R) as i:
                    for j in range(2):
                        gather(2 * i + j, j)
                scatter.at = scatter.ROUNDS
                scatter.close(pool)

            @block.tensor
            def _(pe):
                pe.sem_inc(transh, 2)

                def up(t, j, i):
                    pe.wait_ge(got[j], before + 16 * i + 16)
                    for c in range(KD):
                        last = nc.tensor.transpose(psX[:, c * P:(c + 1) * P], XG[:, j, c * P:(c + 1) * P], k.ident[:])
                    last.then_inc(transx, 1)
                    e = pe.value_load(tile_bin[0:1, bass.ds(t, 1)], min_val=0, max_val=NE - 1)
                    pe.wait_ge(xcopied, t + 1)
                    for n in range(NHB):
                        for c in range(KD):
                            nc.tensor.matmul(psH[2 * j + n][:], xT[:, c],
                                             W1s[:, bass.ds(e, 1), c, n * BANK:(n + 1) * BANK].rearrange("p a h -> p (a h)"),
                                             start=(c == 0), stop=False)
                        if n == 0:
                            pe.wait_ge(chosen, t + 1)
                        last = nc.tensor.matmul(psH[2 * j + n][:], oh[:, j], B3[:, n * BANK:(n + 1) * BANK], start=False, stop=True)
                    last.then_inc(hid, 1)

                def down(t, j):
                    for n in range(NHB):
                        pe.wait_ge(act_s, 2 * t + n + 1)
                        pe.wait_ge(hcopied, 2 * t + n + 1)
                        for c in range(HPB):
                            last = nc.tensor.transpose(psT[n][:, c * P:(c + 1) * P],
                                                       Hs[:, n * BANK + c * P:n * BANK + (c + 1) * P], k.ident[:])
                        last.then_inc(transh, 1)
                    e = pe.value_load(tile_bin[0:1, bass.ds(t, 1)], min_val=0, max_val=NE - 1)
                    pe.wait_ge(taken, t + 1)
                    nc.tensor.matmul(psY[:, 0:D], oh[:, j], B3[:, HID:], start=True, stop=False)
                    for n in range(NHB):
                        pe.wait_ge(hcopied, 2 * t + n + 3)
                        for c in range(HPB):
                            q = n * HPB + c
                            last = nc.tensor.matmul(psY[:, 0:D], HT[:, q], W2s[:, bass.ds(e, 1), q].rearrange("p a d -> p (a d)"),
                                                    start=False, stop=(q == KH - 1))
                    last.then_inc(outs, 1)

                up(0, 0, 0)
                with pe.Fori(0, R - 1) as i:
                    up(2 * i + 1, 1, i)
                    down(2 * i, 0)
                    up(2 * i + 2, 0, i + 1)
                    down(2 * i + 1, 1)
                up(MT - 1, 1, R - 1)
                down(MT - 2, 0)
                down(MT - 1, 1)

            @block.vector
            def _(dve):
                dve.sem_inc(hcopied, 2)
                dve.sem_inc(taken, 1)

                def xcopy(t):
                    dve.wait_ge(transx, t + 1)
                    nc.vector.tensor_copy(xT[:], psX[:, 0:D].rearrange("p (c n) -> p c n", c=KD)).then_inc(xcopied, 1)

                def finish(t, j, i, first=False):
                    for n in range(NHB):
                        dve.wait_ge(transh, 2 + 2 * t + n + 1)
                        nc.vector.tensor_copy(HT[:, n * HPB:(n + 1) * HPB], psT[n][:].rearrange("p (c n) -> p c n", c=HPB)).then_inc(hcopied, 1)
                    dve.wait_ge(outs, t + 1)
                    if not first:
                        dve.wait_ge(sent[j], 16 * i)
                    nc.vector.tensor_copy(Ys[:, j], psY[:, 0:D]).then_inc(taken, 1)

                xcopy(0)
                dve.wait_ge(hid, 1)
                xcopy(1)
                finish(0, 0, 0, True)
                dve.wait_ge(hid, 2)
                xcopy(2)
                finish(1, 1, 0, True)
                with dve.Fori(1, R - 1) as i:
                    dve.wait_ge(hid, 2 * i + 1)
                    xcopy(2 * i + 1)
                    finish(2 * i, 0, i)
                    dve.wait_ge(hid, 2 * i + 2)
                    xcopy(2 * i + 2)
                    finish(2 * i + 1, 1, i)
                dve.wait_ge(hid, MT - 1)
                xcopy(MT - 1)
                finish(MT - 2, 0, R - 1)
                finish(MT - 1, 1, R - 1)

            @block.sync
            def _(sp):
                with sp.Fori(0, R) as i:
                    for j in range(2):
                        sp.wait_ge(taken, 2 * i + j + 2)
                        sp.dma_start(Y[bass.ds((2 * i + j) * P, P), :], Ys[:, j]).then_inc(sent[j], 16)
                for j in range(2):
                    sp.wait_ge(sent[j], 16 * R)


def moe_combine(nc, k, X, Y, where, weight):
    with Phase(nc, "mc") as ph:
        G = ph.sb("G", [P, 2, TOPK, D])
        T = ph.sb("T", [P, 2, TOPK, D])
        idx = ph.sb("idx", [P, 2, TOPK], I32)
        prepped, turns, weighed, first, added = ph.sem("prepped"), ph.sem("turns"), ph.sem("weighed"), ph.sem("first"), ph.sem("added")
        got, before = ph.indirect(k, NB // 2 * TOPK)
        with ph.block() as block:
            @block.scalar
            def _(act):
                def prep(b, j, first=False):
                    if not first:
                        act.wait_ge(weighed, 2 * b - 2)
                    nc.scalar.copy(idx[:, j], where[:, :, bass.ds(b, 1)].rearrange("p k a -> p (k a)")).then_inc(prepped, 1)
                prep(0, 0, True)
                prep(1, 1, True)
                with act.Fori(1, NB // 2) as i:
                    prep(2 * i, 0)
                    prep(2 * i + 1, 1)

            @block.gpsimd
            def _(pool):
                with pool.Fori(0, NB // 2) as i:
                    for j in range(2):
                        pool.wait_ge(prepped, 2 * i + j + 1)
                        pool.sem_inc(turns)
                        for c in range(TOPK):
                            nc.gpsimd.indirect_dma_start(out=G[:, j, c], out_offset=None, in_=Y[:, :],
                                                         in_offset=bass.IndirectOffsetOnAxis(ap=idx[:, j, c:c + 1], axis=0)).then_inc(got[j], 16)

            @block.vector
            def _(dve):
                with dve.Fori(0, NB // 2) as i:
                    for j in range(2):
                        b = 2 * i + j
                        dve.wait_ge(got[j], before + (i + 1) * (16 * TOPK))
                        for c in range(TOPK):
                            nc.vector.tensor_scalar_mul(T[:, j, c], G[:, j, c], weight[:, c, bass.ds(b, 1)]).then_inc(weighed, 1)
                        dve.wait_ge(weighed, 2 * b + 2)
                        nc.vector.tensor_tensor(T[:, j, 0], T[:, j, 0], T[:, j, 1], ALU.add).then_inc(first, 1)
                        dve.wait_ge(first, b + 1)
                        nc.vector.tensor_tensor(X[:, bass.ds(b, 1)], X[:, bass.ds(b, 1)], T[:, j, 0].unsqueeze(1), ALU.add).then_inc(added, 1)


def moe_layer(nc, k, X, Wr, br, ln_g, ln_b, W1, b1, W2, b2, later, start, rounds=14):
    table = nc.dram_tensor("moe_table", [NP, D], F32, kind="Internal").ap()
    Y = nc.dram_tensor("moe_out", [MT * P, D], F32, kind="Internal").ap()
    records = nc.dram_tensor("moe_records", [P * MT, 1], F32, kind="Internal").ap()
    with Phase(nc, "moe") as ph:
        expert, weight = ph.sb("expert", [P, TOPK, NB]), ph.sb("weight", [P, TOPK, NB])
        where = ph.sb("where", [P, TOPK, NB], I32)
        tbk = ph.sb("tbk", [1, MT], I32)
        slots = ph.sb("slots", [P, MT])
        with Phase(nc, "mob") as pb:
            scatter = Scatter(nc, k, pb, later, start, rounds)
            moe_route(nc, k, X, Wr, br, table, expert, weight, lambda pool: scatter.piece(pool, rounds))
            G = 10
            bins = pb.sb("bins", [P, MC + G])
            tb_dram = sort_items(nc, k, "ms", bins, ItemPrep(nc, k, expert), MC, G, NE, MT, MT, 5, 1, records,
                                 pos_out=where[:].rearrange("p k b -> p (k b)"), tile_bin=tbk)
            loaded = pb.sem("loaded")
            with pb.block() as block:
                @block.sync
                def _(sp):
                    sp.dma_start(slots[:], records.rearrange("(p t) r -> p (t r)", p=P)).then_inc(loaded, 16)
                    sp.wait_ge(loaded, 16)

                @block.gpsimd
                def _(pool):
                    scatter.close(pool)
        moe_experts(nc, k, table, slots, tbk, tb_dram, ln_g, ln_b, W1, b1, W2, b2, Y, later, scatter.at)
        moe_combine(nc, k, X, Y, where, weight)


HOPS = 3


def hop_transform(nc, k, hop, X, H, agg, table, WnT, WsT, bn, bs):
    last_hop = hop == HOPS - 1
    with Phase(nc, f"ht{hop}") as ph:
        W = ph.sb("W", [P, 2 * KD, D])
        b = ph.sb("b", [1, 2, D])
        xs = ph.sb("xs", [P, 2, 2, D])
        xT = ph.sb("xT", [P, 2, 2 * KD, P])
        neg = ph.sb("neg", [P, 2, D])
        pos = ph.sb("pos", [P, 2, D])
        ex = ph.sb("ex", [P, 2, D])
        psT = [ph.ps(f"T{j}") for j in range(2)]
        psO = [ph.ps(f"O{j}") for j in range(2)]
        loaded, biased, ringed, trans, copied, prods = (ph.sem("loaded"), ph.sem("biased"), ph.sem("ringed"), ph.sem("trans"),
                                                        ph.sem("copied"), ph.sem("prods"))
        split, exped, done, stored = ph.sem("split"), ph.sem("exped"), ph.sem("done"), ph.sem("stored")
        with ph.block() as block:
            @block.sync
            def _(sp):
                sp.dma_start(W[:, 0:KD], WnT[hop].rearrange("(k p) n -> p k n", p=P)).then_inc(loaded, 16)
                sp.dma_start(W[:, KD:2 * KD], WsT[hop].rearrange("(k p) n -> p k n", p=P)).then_inc(loaded, 16)
                sp.dma_start(b[:, 0], bn[hop:hop + 1, :]).then_inc(loaded, 16)
                sp.dma_start(b[:, 1], bs[hop:hop + 1, :]).then_inc(loaded, 16)
                if not last_hop:
                    sp.wait_ge(done, NB)
                    sp.dma_start(table.rearrange("(b p) d -> p b d", p=P), H[:]).then_inc(stored, 16)
                    sp.wait_ge(stored, 16)

            @block.scalar
            def _(act):
                def ring(n, j, first=False):
                    if not first:
                        act.wait_ge(trans, n - 1)
                    nc.scalar.copy(xs[:, j, 0].unsqueeze(1), agg[:, bass.ds(n, 1)]).then_inc(ringed, 1)
                    nc.scalar.copy(xs[:, j, 1].unsqueeze(1), H[:, bass.ds(n, 1)]).then_inc(ringed, 1)

                def turned(n, j, first=False):
                    act.wait_ge(trans, n + 1)
                    if not first:
                        act.wait_ge(prods, n - 1)
                    nc.scalar.copy(xT[:, j], psT[j][:].rearrange("p (c n) -> p c n", c=2 * KD)).then_inc(copied, 1)

                def exps(n, j):
                    if not last_hop:
                        act.wait_ge(split, 2 * n + 2)
                        nc.scalar.activation(ex[:, j], neg[:, j], ACT.Exp).then_inc(exped, 1)

                ring(0, 0, True)
                ring(1, 1, True)
                turned(0, 0, True)
                turned(1, 1, True)
                with act.Fori(1, NB // 2) as i:
                    ring(2 * i, 0)
                    ring(2 * i + 1, 1)
                    exps(2 * i - 2, 0)
                    turned(2 * i, 0)
                    exps(2 * i - 1, 1)
                    turned(2 * i + 1, 1)
                exps(NB - 2, 0)
                exps(NB - 1, 1)

            @block.tensor
            def _(pe):
                pe.wait_ge(biased, 1)

                def turn(n, j, first=False):
                    pe.wait_ge(ringed, 2 * n + 2)
                    if not first:
                        pe.wait_ge(copied, n - 1)
                    for c in range(2 * KD):
                        last = nc.tensor.transpose(psT[j][:, c * P:(c + 1) * P], xs[:, j, c // KD, c % KD * P:(c % KD + 1) * P], k.ident[:])
                    last.then_inc(trans, 1)

                def product(n, j, first=False):
                    pe.wait_ge(copied, n + 1)
                    if not first:
                        pe.wait_ge(done, n - 1)
                    for c in range(2 * KD):
                        nc.tensor.matmul(psO[j][:, 0:D], xT[:, j, c], W[:, c], start=(c == 0), stop=False)
                    nc.tensor.matmul(psO[j][:, 0:D], k.onesf[0:1, :], b[:, 0], start=False, stop=True).then_inc(prods, 1)

                turn(0, 0, True)
                turn(1, 1, True)
                product(0, 0, True)
                product(1, 1, True)
                with pe.Fori(1, NB // 2) as i:
                    turn(2 * i, 0)
                    turn(2 * i + 1, 1)
                    product(2 * i, 0)
                    product(2 * i + 1, 1)

            @block.vector
            def _(dve):
                dve.wait_ge(loaded, 64)
                nc.vector.tensor_tensor(b[:, 0], b[:, 0], b[:, 1], ALU.add).then_inc(biased, 1)
                with dve.Fori(0, NB // 2) as i:
                    for j in range(2):
                        n = 2 * i + j
                        dve.wait_ge(prods, n + 1)
                        z = psO[j][:, 0:D]
                        if last_hop:
                            nc.vector.tensor_tensor(X[:, bass.ds(n, 1)], X[:, bass.ds(n, 1)], z.unsqueeze(1), ALU.add).then_inc(done, 1)
                            continue
                        nc.vector.tensor_scalar_min(neg[:, j], z, 0.0).then_inc(split, 1)
                        nc.vector.tensor_scalar_max(pos[:, j], z, 0.0).then_inc(split, 1)
                        dve.wait_ge(exped, n + 1)
                        nc.vector.scalar_tensor_tensor(H[:, bass.ds(n, 1)], ex[:, j].unsqueeze(1), -1.0, pos[:, j].unsqueeze(1),
                                                       ALU.add, ALU.add).then_inc(done, 1)


def gnn_layer(nc, k, X, order, WnT, bn, WsT, bs):
    table = nc.dram_tensor("hop_table", [NP, D], F32, kind="Internal").ap()
    with Phase(nc, "gnn") as ph:
        H, agg = ph.sb("H", [P, NB, D]), ph.sb("agg", [P, NB, D])
        with Phase(nc, "gn") as pn:
            norm = RowNorm(nc, pn, X)
            step, stored = pn.sem("step"), pn.sem("stored")
            with pn.block() as block:
                @block.scalar
                def _(act):
                    norm.root(act)

                @block.vector
                def _(dve):
                    norm.all(dve, Chain(dve, step), H)

                @block.sync
                def _(sp):
                    sp.wait_ge(step, 3 * NB + 1)
                    sp.dma_start(table.rearrange("(b p) d -> p b d", p=P), H[:]).then_inc(stored, 16)
                    sp.wait_ge(stored, 16)
        SRT, tbk = ph.sb("SRT", [P, EROW, 4]), ph.sb("tbk", [1, EROW], I32)
        order.load(SRT, tbk)
        for hop in range(HOPS):
            propagate(nc, k, hop, table, SRT, tbk, agg)
            hop_transform(nc, k, hop, X, H, agg, table, WnT, WsT, bn, bs)


HALF = 25
BODY = 2 * HALF
assert N % BODY == 0
FP16_TOP = 14
TAILS = [(FULL * P, min(P, TAIL + HALF))] + ([(FULL * P + P, TAIL + HALF - P)] if TAIL + HALF > P else [])
GATES = "igo"
M6 = len(GATES) * KD
ROWS = [g + str(m) for g in GATES for m in range(KD)]
PLACE = {"i0": (0, 0), "g0": (0, 1), "i1": (1, 0), "g1": (1, 1), "o0": (2, 0), "o1": (3, 0)}
BANKS = 4


def terms(rows, parts, q):
    return [(row, part, q) for row in rows.split() for part in parts.split()]


ORDER = (terms("i0 g0 i1 g1", "11 21", 0) + terms("i0 g0 i1", "11 21", 1)
         + [t for q in range(KD) for t in terms("i0 g0", "12", q)]
         + terms("g1", "11 21", 1) + [t for q in range(KD) for t in terms("i1 g1", "12", q)]
         + [t for row in ("o0", "o1") for q in range(KD) for t in terms(row, "11 21 12", q)])
assert len(ORDER) == len(set(ORDER)) == 3 * KD * M6


def lstm_layer(nc, k, X, U, V, b):
    with Phase(nc, "ls") as ph:
        XT1 = ph.sb("XT1", [P, KD, N + HALF], F16)
        XT2 = ph.sb("XT2", [P, KD, N + HALF], F16)
        HT = ph.sb("HT", [P, NP, KD])
        U1, U2 = (ph.sb(n, [P, KD, M6, P], F16) for n in ("U1", "U2"))
        V1, V2 = (ph.sb(n, [P, KD, M6, P], F16) for n in ("V1", "V2"))
        b1, b2 = (ph.sb(n, [1, M6, P], F16) for n in ("b1", "b2"))
        ones = ph.sb("ones", [1, HALF], F16)
        sc = ph.sb("sc", [P, 2], I32)
        h = ph.sb("h", [P, BODY, KD])
        h1 = ph.sb("h1", [P, BODY, KD], F16)
        h2 = ph.sb("h2", [P, BODY, KD], F16)
        c = ph.sb("c", [P, 2, KD])
        S = ph.sb("S", [P, 2, M6])
        hc = ph.sb("hc", [P, KD])
        th = ph.sb("th", [P, 2, KD])

        with Phase(nc, "lp") as pp:
            Us, Vs = (pp.sb(n, [P, KD, M6, P]) for n in ("U", "V"))
            brow = pp.sb("brow", [1, M6, P])
            mx = pp.sb("mx", [P, 2, 2])
            big = pp.sb("big", [P, 2])
            top = pp.sb("top", [P, 1])
            ex = pp.sb("ex", [P, 2], I32)
            norm = RowNorm(nc, pp, X)
            xs = pp.sb("xs", [P, 2, 1, D])
            xT = pp.sb("xT", [P, 2, KD, P])
            psT = [pp.ps(f"T{j}") for j in range(2)]
            step, normed, trans, loaded = pp.sem("step"), pp.sem("normed"), pp.sem("trans"), pp.sem("loaded")
            copied, high, low, reduced = pp.sem("copied"), pp.sem("high"), pp.sem("low"), pp.sem("reduced")
            scale = sc[:, 0:1].bitcast(F32)
            with pp.block() as block:
                @block.sync
                def _(sp):
                    sp.dma_start(Us[:], U.rearrange("(k p) (m c) -> p k m c", k=KD, c=P)).then_inc(loaded, 16)
                    sp.dma_start(Vs[:], V.rearrange("(k p) (m c) -> p k m c", k=KD, c=P)).then_inc(loaded, 16)
                    sp.dma_start(brow[:], b.rearrange("(a m c) -> a m c", a=1, c=P)).then_inc(loaded, 16)

                @block.vector
                def _(dve):
                    ch = Chain(dve, step)
                    norm.stats(dve, ch)
                    norm.apply(xs[:, 0], 0).then_inc(normed, 1)
                    norm.apply(xs[:, 1], 1).then_inc(normed, 1)

                    def split_block(n, j, cols, count):
                        dve.wait_ge(high, n + 1)
                        nc.vector.tensor_tensor(XT2[:, :, cols], xT[:, j, :, 0:count], XT1[:, :, cols], ALU.subtract).then_inc(low, 1)

                    with dve.Fori(1, FULL // 2) as i:
                        for j in range(2):
                            n = 2 * i + j
                            dve.wait_ge(trans, n - 1)
                            norm.apply(xs[:, j], n).then_inc(normed, 1)
                            split_block(n - 2, j, bass.ds((n - 2) * P, P), P)
                    for j in range(2):
                        dve.wait_ge(trans, FULL + j - 1)
                        norm.apply(xs[:, j], FULL + j).then_inc(normed, 1)
                        split_block(FULL - 2 + j, j, slice((FULL - 2 + j) * P, (FULL - 1 + j) * P), P)
                    for j, (c0, count) in enumerate(TAILS):
                        split_block(FULL + j, j, slice(c0, c0 + count), count)
                    dve.wait_ge(loaded, 48)
                    ch(nc.vector.memset(mx[:], 0.0))
                    for j, w in enumerate((Us, Vs)):
                        v = w[:].rearrange("p k m c -> p (k m c)")
                        ch.mark(nc.vector.tensor_reduce(mx[:, 0, j:j + 1], v, AXX, ALU.max))
                        ch(nc.vector.tensor_reduce(mx[:, 1, j:j + 1], v, AXX, ALU.min))
                    ch(nc.vector.scalar_tensor_tensor(mx[:, 0], mx[:, 1], -1.0, mx[:, 0], ALU.mult, ALU.max))
                    ch(nc.vector.reduce_max(big[:, 0:1], mx[:, 0], AXX))
                    v = brow[:].rearrange("p m c -> p (m c)")
                    ch.mark(nc.vector.tensor_reduce(mx[0:1, 0, 0:1], v, AXX, ALU.max))
                    ch(nc.vector.tensor_reduce(mx[0:1, 1, 0:1], v, AXX, ALU.min))
                    ch(nc.vector.scalar_tensor_tensor(mx[0:1, 0, 0:1], mx[0:1, 1, 0:1], -1.0, mx[0:1, 0, 0:1], ALU.mult, ALU.max))
                    ch(nc.vector.tensor_tensor(big[0:1, 0:1], big[0:1, 0:1], mx[0:1, 0, 0:1], ALU.max))
                    nc.vector.tensor_scalar_max(big[:, 1:2], big[:, 0:1], 2.0 ** -60).then_inc(reduced, 1)
                    dve.wait_ge(reduced, 2)
                    ch(nc.vector.tensor_scalar(ex[:, 0:1], top[:].bitcast(I32), 23, None, ALU.logical_shift_right))
                    ch(nc.vector.tensor_scalar(ex[:, 1:2], ex[:, 0:1], -1.0, 254.0 + FP16_TOP, ALU.mult, ALU.add))
                    ch(nc.vector.tensor_scalar(ex[:, 0:1], ex[:, 1:2], -1.0, 254.0, ALU.mult, ALU.add))
                    ch.mark(nc.vector.tensor_scalar(sc[:, 0:1], ex[:, 1:2], 23, None, ALU.logical_shift_left))
                    ch(nc.vector.tensor_scalar(sc[:, 1:2], ex[:, 0:1], 23, None, ALU.logical_shift_left))
                    parts = ((Us, U1, U2, scale), (Vs, V1, V2, scale), (brow, b1, b2, sc[0:1, 0:1].bitcast(F32)))
                    for w, w1, w2, by in parts:
                        ch.mark(nc.vector.tensor_scalar_mul(w[:], w[:], by))
                    ch.wait()
                    for w, w1, w2, by in parts:
                        ch.mark(nc.vector.tensor_copy(w1[:], w[:]))
                    ch.wait()
                    for w, w1, w2, by in parts:
                        ch.mark(nc.vector.tensor_tensor(w2[:], w[:], w1[:], ALU.subtract))
                    ch.wait()

                @block.gpsimd
                def _(pool):
                    nc.gpsimd.memset(HT[:, N:NP, :], 0.0)
                    nc.gpsimd.memset(ones[:], 1.0)
                    pool.wait_ge(reduced, 1)
                    nc.gpsimd.partition_all_reduce(top[:], big[:, 1:2], P, bass.bass_isa.ReduceOp.max).then_inc(reduced, 1)

                @block.tensor
                def _(pe):
                    def turn(n, j, first=False):
                        pe.wait_ge(normed, n + 1)
                        if not first:
                            pe.wait_ge(high, n - 1)
                        for q in range(KD):
                            last = nc.tensor.transpose(psT[j][:, q * P:(q + 1) * P], xs[:, j, 0, q * P:(q + 1) * P], k.ident[:])
                        last.then_inc(trans, 1)
                    turn(0, 0, True)
                    turn(1, 1, True)
                    with pe.Fori(1, NB // 2) as i:
                        turn(2 * i, 0)
                        turn(2 * i + 1, 1)

                @block.scalar
                def _(act):
                    norm.root(act)

                    def take(n, j, cols, count, first=False):
                        act.wait_ge(trans, n + 1)
                        if not first:
                            act.wait_ge(low, n - 1)
                        src = psT[j][:, 0:D].rearrange("p (c n) -> p c n", c=KD)[:, :, 0:count]
                        nc.scalar.copy(xT[:, j, :, 0:count], src)
                        nc.scalar.copy(XT1[:, :, cols], src).then_inc(high, 1)

                    take(0, 0, slice(0, P), P, True)
                    take(1, 1, slice(P, 2 * P), P, True)
                    with act.Fori(1, FULL // 2) as i:
                        for j in range(2):
                            take(2 * i + j, j, bass.ds((2 * i + j) * P, P), P)
                    for j, (c0, count) in enumerate(TAILS):
                        take(FULL + j, j, slice(c0, c0 + count), count)

        with Phase(nc, "lr") as pr:
            Z = [[pr.ps(f"Z{i}{g}") for g in range(BANKS)] for i in range(2)]
            z = [pr.sem(f"z{g}") for g in range(BANKS)]
            gates, cell, tanh_made, h1_made = ([pr.sem(f"{n}{j}") for j in range(KD)] for n in ("gates", "cell", "tanh", "h1_"))
            h_made, h2_made, hc_made, kept = (pr.sem(n) for n in ("h", "h2", "hc", "kept"))
            with pr.block() as block:
                @block.gpsimd
                def _(pool):
                    pool.sem_inc(kept, 2)
                    with pool.Fori(0, N // BODY) as i:
                        for hf in range(2):
                            pool.wait_ge(h_made, i * BODY + HALF * (hf + 1))
                            nc.gpsimd.tensor_copy(HT[:, bass.ds(i * BODY + hf * HALF, HALF), :],
                                                  h[:, hf * HALF:(hf + 1) * HALF, :]).then_inc(kept, 1)

                @block.tensor
                def _(pe):
                    AHEAD = [(row, kk, part) for row in sorted(ROWS, key=lambda r: PLACE[r][1]) for kk in range(KD + 1)
                             for part in (("1", "2") if kk == 0 else ("11", "21", "12"))]
                    PER = -(-len(AHEAD) // HALF)

                    def ahead(a, t0, hf):
                        row, kk, part = AHEAD[a]
                        bank, col = PLACE[row]
                        m = ROWS.index(row)
                        o = Z[hf][bank][:, 0:KD * HALF].rearrange("p (t m) -> p t m", m=KD)[:, :, col]
                        opens = kk == 0 and part == "1" and col == 0
                        if kk == 0:
                            w, x = (b1 if part == "1" else b2)[:, m, :], ones[:]
                        else:
                            w = (U2 if part == "21" else U1)[:, kk - 1, m, :]
                            x = (XT2 if part == "12" else XT1)[:, kk - 1, bass.ds(t0, HALF)]
                        nc.tensor.matmul(o, w, x, start=opens, stop=False, skip_group_check=True)

                    for a in range(len(AHEAD)):
                        ahead(a, 0, 0)
                    with pe.Fori(0, N // BODY) as i:
                        for s in range(BODY):
                            hf, prev = s // HALF, (s - 1) % BODY
                            waited = []
                            for n, (row, part, q) in enumerate(ORDER):
                                bank, col = PLACE[row]
                                col += s % HALF * KD
                                hx, made = (h2, h2_made) if part == "12" else (h1, h1_made[q])
                                if (part == "12", q) not in waited:
                                    pe.wait_ge(made, i * BODY + s + 1)
                                    waited.append(made)
                                ends = all(PLACE[r][0] != bank for r, _, _ in ORDER[n + 1:])
                                mm = nc.tensor.matmul(Z[hf][bank][:, col:col + 1], (V2 if part == "21" else V1)[:, q, ROWS.index(row), :],
                                                      hx[:, prev, q:q + 1], start=False, stop=ends, skip_group_check=True)
                                if ends:
                                    mm.then_inc(z[bank], 1)
                            for a in range(s % HALF * PER, min(len(AHEAD), (s % HALF + 1) * PER)):
                                ahead(a, i * BODY + HALF * (hf + 1), 1 - hf)

                @block.scalar
                def _(act):
                    back = act.alloc_register("unscale")
                    act.reg_load(back, sc[0:1, 1:2])
                    with act.Fori(0, N // BODY) as i:
                        for s in range(BODY):
                            hf, col, t = s // HALF, s % HALF * KD, i * BODY + s
                            for m in range(KD):
                                act.wait_ge(z[m], t + 1)
                                nc.scalar.activation(S[:, s % 2, m:m + 1], Z[hf][m][:, col:col + 1], ACT.Sigmoid, scale=back)
                                nc.scalar.activation(S[:, s % 2, KD + m:KD + m + 1], Z[hf][m][:, col + 1:col + 2], ACT.Tanh,
                                                     scale=back).then_inc(gates[m], 1)
                            for m in range(KD):
                                act.wait_ge(z[2 + m], t + 1)
                                nc.scalar.activation(S[:, s % 2, 2 * KD + m:2 * KD + m + 1], Z[hf][2 + m][:, col:col + 1], ACT.Sigmoid, scale=back)
                            for m in range(KD):
                                act.wait_ge(cell[m], t + 1)
                                nc.scalar.activation(th[:, s % 2, m:m + 1], c[:, s % 2, m:m + 1], ACT.Tanh).then_inc(tanh_made[m], 1)

                @block.vector
                def _(dve):
                    for m in range(KD):
                        nc.vector.memset(h1[:, BODY - 1, m:m + 1], 0.0).then_inc(h1_made[m], 1)
                    nc.vector.memset(h2[:, BODY - 1, :], 0.0).then_inc(h2_made, 1)
                    nc.vector.memset(hc[:], 0.0).then_inc(hc_made, 1)
                    with dve.Fori(0, N // BODY) as i:
                        for s in range(BODY):
                            t, e = i * BODY + s, s % 2
                            for m in range(KD):
                                dve.wait_ge(gates[m], t + 1)
                                if m == 0:
                                    dve.wait_ge(hc_made, t + 1)
                                nc.vector.scalar_tensor_tensor(c[:, e, m:m + 1], S[:, e, KD + m:KD + m + 1], S[:, e, m:m + 1], hc[:, m:m + 1],
                                                               ALU.mult, ALU.add).then_inc(cell[m], 1)
                            if s % HALF == 0:
                                dve.wait_ge(kept, 2 * i + s // HALF + 1)
                            for m in range(KD):
                                dve.wait_ge(tanh_made[m], t + 1)
                                nc.vector.tensor_tensor(h1[:, s, m:m + 1], S[:, e, 2 * KD + m:2 * KD + m + 1], th[:, e, m:m + 1],
                                                        ALU.mult).then_inc(h1_made[m], 1)
                            nc.vector.tensor_tensor(h[:, s, :], S[:, e, 2 * KD:M6], th[:, e, :], ALU.mult).then_inc(h_made, 1)
                            dve.wait_ge(h_made, t + 1)
                            nc.vector.tensor_tensor(h2[:, s, :], h[:, s, :], h1[:, s, :], ALU.subtract).then_inc(h2_made, 1)
                            nc.vector.tensor_tensor(hc[:], h[:, s, :], c[:, e, :], ALU.mult).then_inc(hc_made, 1)

        with Phase(nc, "lf") as pf:
            hs = pf.sb("hs", [P, 2, KD, P])
            psT = [pf.ps(f"T{j}") for j in range(2)]
            ringed, trans, added = pf.sem("ringed"), pf.sem("trans"), pf.sem("added")
            with pf.block() as block:
                @block.scalar
                def _(act):
                    def ring(n, j, first=False):
                        if not first:
                            act.wait_ge(trans, n - 1)
                        nc.scalar.copy(hs[:, j], HT[:, bass.ds(n * P, P), :].rearrange("p t k -> p k t")).then_inc(ringed, 1)
                    ring(0, 0, True)
                    ring(1, 1, True)
                    with act.Fori(1, NB // 2) as i:
                        ring(2 * i, 0)
                        ring(2 * i + 1, 1)

                @block.tensor
                def _(pe):
                    def turn(n, j, first=False):
                        pe.wait_ge(ringed, n + 1)
                        if not first:
                            pe.wait_ge(added, n - 1)
                        for q in range(KD):
                            last = nc.tensor.transpose(psT[j][:, q * P:(q + 1) * P], hs[:, j, q], k.ident[:])
                        last.then_inc(trans, 1)
                    turn(0, 0, True)
                    turn(1, 1, True)
                    with pe.Fori(1, NB // 2) as i:
                        turn(2 * i, 0)
                        turn(2 * i + 1, 1)

                @block.vector
                def _(dve):
                    with dve.Fori(0, NB // 2) as i:
                        for j in range(2):
                            dve.wait_ge(trans, 2 * i + j + 1)
                            nc.vector.tensor_tensor(X[:, bass.ds(2 * i + j, 1)], X[:, bass.ds(2 * i + j, 1)],
                                                    psT[j][:, 0:D].unsqueeze(1), ALU.add).then_inc(added, 1)


class Constants:

    def __init__(self, nc, ph):
        self.cols = ph.sb("cols", [P, P])
        self.part = ph.sb("part", [P, 1])
        self.ident = ph.sb("ident", [P, P])
        self.ones = ph.sb("ones", [P, P], BF16)
        self.onesf = ph.sb("onesf", [P, P])
        self.before = ph.sb("before", [P, P], BF16)
        self.indirect = [ph.ctx.enter_context(nc.semaphore(f"indirect{j}")) for j in range(2)]
        self.indirect_before = 0
        self.scattered = [ph.ctx.enter_context(nc.semaphore(f"scattered{j}")) for j in range(2)]
        self.scattered_before = 0
        constants(nc, self)


def build(nc, x, src, dst, edge_weight, gat_W_src, gat_W_dst, gat_att_src, gat_att_dst, gat_bias, gat_gamma, gat_beta,
          gat_prelu, moe_Wr, moe_br, moe_g, moe_b, moe_W1, moe_b1, moe_W2, moe_b2, gnn_WnT, gnn_bn, gnn_WsT, gnn_bs,
          lstm_U, lstm_V, lstm_b, out):
    with Phase(nc, "all") as ph:
        k = Constants(nc, ph)
        X = ph.sb("X", [P, NB, D])
        load_rows(nc, x, X)
        order = EdgeOrder(nc, "ss", src, dst, edge_weight)
        at = gat_layer(nc, k, X, src, dst, gat_W_src, gat_W_dst, gat_att_src, gat_att_dst, gat_bias, gat_gamma, gat_beta, gat_prelu, order)
        moe_layer(nc, k, X, moe_Wr, moe_br, moe_g, moe_b, moe_W1, moe_b1, moe_W2, moe_b2, order, at)
        gnn_layer(nc, k, X, order, gnn_WnT, gnn_bn, gnn_WsT, gnn_bs)
        lstm_layer(nc, k, X, lstm_U, lstm_V, lstm_b)
        store_rows(nc, X, out)


def kernel(**inputs):
    import numpy as np
    import concourse.bacc as bacc
    from concourse.bass_utils import run_bass_kernel_spmd

    given = {name: np.ascontiguousarray(inputs[name]) for name in (
        "x", "src", "dst", "edge_weight", "L0_gnn_W_src", "L0_gnn_W_dst", "L0_gnn_att_src", "L0_gnn_att_dst", "L0_gnn_bias",
        "L0_gnn_ln_gamma", "L0_gnn_ln_beta", "L0_gnn_prelu_w", "L0_ffn_Wr", "L0_ffn_br", "L0_ffn_ln_g", "L0_ffn_ln_b",
        "L0_ffn_W1", "L0_ffn_b1", "L0_ffn_W2", "L0_ffn_b2")}
    given["gnn_WnT"] = np.ascontiguousarray(np.transpose(inputs["L1_gnn_Wn"], (0, 2, 1)))
    given["gnn_bn"] = np.ascontiguousarray(inputs["L1_gnn_bn"])
    given["gnn_WsT"] = np.ascontiguousarray(np.transpose(inputs["L1_gnn_Ws"], (0, 2, 1)))
    given["gnn_bs"] = np.ascontiguousarray(inputs["L1_gnn_bs"])
    for part in ("U", "V", "b"):
        given[f"lstm_{part}"] = np.concatenate([np.asarray(inputs[f"L1_ffn_{part}_{gate}"]) for gate in ("i", "c", "o")], axis=-1)

    nc = bacc.Bacc("TRN2", target_bir_lowering=False, num_devices=1)
    arrays = {f"in_{name}": a for name, a in given.items()}
    args = [nc.dram_tensor(name, a.shape, mybir.dt.from_np(a.dtype), kind="ExternalInput").ap() for name, a in arrays.items()]
    args.append(nc.dram_tensor("out_0", (N, D), F32, kind="ExternalOutput").ap())
    build(nc, *args)
    r = run_bass_kernel_spmd(nc, [arrays], core_ids=[0])
    return r.results[0]["out_0"]
```
